# Optimizing a Trainium2 kernel written in Bass

```python
import numpy as np
import jax
import jax.numpy as jnp

def _softmax(x, axis=-1):
    return jax.nn.softmax(x, axis=axis)

def _gelu(x):
    return jax.nn.gelu(x, approximate=True)

def _silu(x):
    return jax.nn.silu(x)

def _sigmoid(x):
    return jax.nn.sigmoid(x)

def _layernorm(x, axis=-1, eps=1e-05):
    m = jnp.mean(x, axis=axis, keepdims=True)
    v = jnp.var(x, axis=axis, keepdims=True)
    return (x - m) / jnp.sqrt(v + eps)

def _scatter_add(tgt, idx, src, axis=0):
    return tgt.at[idx].add(src)

def _segment_sum(src, seg, n):
    return jax.ops.segment_sum(src, seg, n)
kernel_name = 'mk_decoder_postln_d1_seqx_r4_727fcc'

def setup_inputs(seed: int=0):
    np.random.seed(seed)
    _w = jnp.asarray

    def _rec_inputs():
        import jax
        import jax.numpy as jnp
        _rk = jax.random.key(seed)
        x = -0.0002928 + 1 * jax.random.normal(jax.random.fold_in(_rk, 1), (8, 256, 256), jnp.float32)
        _lenS = 256 - jax.random.randint(jax.random.fold_in(_rk, 7), (8,), 0, max(1, 256 // 4) + 1, jnp.int32)
        _lenS2 = 256 - jax.random.randint(jax.random.fold_in(_rk, 8), (8,), 0, max(1, 256 // 4) + 1, jnp.int32)
        _ctx_1024P = jax.random.normal(jax.random.fold_in(_rk, 11), (8, 16, 256), jnp.float32)
        _ctx_1024c = jax.random.dirichlet(jax.random.fold_in(_rk, 511), 0.3 * jnp.ones((16,), jnp.float32), (8, 256))
        _ctx_1024t = jnp.einsum('bsk,bkd->bsd', _ctx_1024c, _ctx_1024P)
        _ctx_1024t = _ctx_1024t * jax.lax.rsqrt(jnp.mean(jnp.square(_ctx_1024t)) + 1e-12) * 0.953939
        ctx_1024 = -1.39393e-06 + 0.999914 * (_ctx_1024t + 0.3 * jax.random.normal(jax.random.fold_in(_rk, 611), (8, 256, 256), jnp.float32))
        return (x, ctx_1024)
    x, ctx_1024 = _rec_inputs()

    def _L0_attn_setup():
        import jax, jax.numpy as jnp
        import numpy as np
        B, T, D = (2, 512, 256)
        H, W = (16, 64)
        HD = D // H
        key = jax.random.key(seed)
        ks = jax.random.split(key, 5)
        s = 0.02
        return {'x': jax.random.normal(ks[0], (B, T, D), dtype=jnp.float32), 'Wqkv': jax.random.normal(ks[1], (3 * D, D), dtype=jnp.float32) * s, 'bqkv': jax.random.normal(ks[2], (3 * D,), dtype=jnp.float32) * s, 'Wo': jax.random.normal(ks[3], (D, D), dtype=jnp.float32) * s, 'bo': jax.random.normal(ks[4], (D,), dtype=jnp.float32) * s}
    _L0_attn_all = _L0_attn_setup()
    _L0_attn_in = {k: v for k, v in _L0_attn_all.items() if k in ('Wqkv', 'bqkv', 'Wo', 'bo')}
    del _L0_attn_all

    def _L0_xattn_setup():
        import jax, jax.numpy as jnp
        import numpy as np
        NUM_HEADS = 16
        EMBED = 256
        ATTN = 256
        HEAD_DIM = ATTN // NUM_HEADS
        NEG = -2.0 ** 32 + 1.0
        LN_EPS = 1e-05

        def _layer_norm(x, gamma, beta):
            mu = jnp.mean(x, axis=-1, keepdims=True)
            var = jnp.mean(jnp.square(x - mu), axis=-1, keepdims=True)
            return (x - mu) * jax.lax.rsqrt(var + LN_EPS) * gamma + beta
        key = jax.random.key(seed)
        ks = jax.random.split(key, 12)
        B, S = (2, 512)
        scale_in = 1.0 / np.sqrt(EMBED)
        return {'query': jax.random.normal(ks[0], (B, S, EMBED), jnp.float32), 'key': jax.random.normal(ks[1], (B, S, EMBED), jnp.float32), 'value': jax.random.normal(ks[2], (B, S, EMBED), jnp.float32), 'Wq': jax.random.normal(ks[3], (EMBED, ATTN), jnp.float32) * scale_in, 'bq': jnp.zeros((ATTN,), jnp.float32), 'Wk': jax.random.normal(ks[4], (EMBED, ATTN), jnp.float32) * scale_in, 'bk': jnp.zeros((ATTN,), jnp.float32), 'Wv': jax.random.normal(ks[5], (EMBED, ATTN), jnp.float32) * scale_in, 'bv': jnp.zeros((ATTN,), jnp.float32), 'gamma': jnp.ones((ATTN,), jnp.float32), 'beta': jnp.zeros((ATTN,), jnp.float32)}
    _L0_xattn_all = _L0_xattn_setup()
    _L0_xattn_in = {k: v for k, v in _L0_xattn_all.items() if k in ('Wq', 'bq', 'Wk', 'bk', 'Wv', 'bv', 'gamma', 'beta')}
    del _L0_xattn_all

    def _L0_ffn_setup():
        import jax, jax.numpy as jnp
        import numpy as np
        NUM_GROUPS = 2
        EXPERT_CAPACITY = 160
        NUM_SELECTED = 2
        key = jax.random.key(seed)
        k1, k2, k3, k4 = jax.random.split(key, 4)
        B, S, H, E, F = (4, 512, 256, 8, 1024)
        return {'input_emb': jax.random.normal(k1, (B, S, H), dtype=jnp.float32), 'w_router': jax.random.normal(k2, (H, E), dtype=jnp.float32) * 0.02, 'wi': jax.random.normal(k3, (E, H, F), dtype=jnp.float32) * 0.02, 'wo': jax.random.normal(k4, (E, F, H), dtype=jnp.float32) * 0.02}
    _L0_ffn_all = _L0_ffn_setup()
    _L0_ffn_in = {k: v for k, v in _L0_ffn_all.items() if k in ('w_router', 'wi', 'wo')}
    del _L0_ffn_all
    return {'x': x, 'ctx_1024': ctx_1024, 'L0_attn_Wqkv': _L0_attn_in['Wqkv'], 'L0_attn_bqkv': _L0_attn_in['bqkv'], 'L0_attn_Wo': _L0_attn_in['Wo'], 'L0_attn_bo': _L0_attn_in['bo'], 'L0_xattn_Wq': _L0_xattn_in['Wq'], 'L0_xattn_bq': _L0_xattn_in['bq'], 'L0_xattn_Wk': _L0_xattn_in['Wk'], 'L0_xattn_bk': _L0_xattn_in['bk'], 'L0_xattn_Wv': _L0_xattn_in['Wv'], 'L0_xattn_bv': _L0_xattn_in['bv'], 'L0_xattn_gamma': _L0_xattn_in['gamma'], 'L0_xattn_beta': _L0_xattn_in['beta'], 'L0_ffn_w_router': _L0_ffn_in['w_router'], 'L0_ffn_wi': _L0_ffn_in['wi'], 'L0_ffn_wo': _L0_ffn_in['wo']}

def reference(x, ctx_1024, L0_attn_Wqkv, L0_attn_bqkv, L0_attn_Wo, L0_attn_bo, L0_xattn_Wq, L0_xattn_bq, L0_xattn_Wk, L0_xattn_bk, L0_xattn_Wv, L0_xattn_bv, L0_xattn_gamma, L0_xattn_beta, L0_ffn_w_router, L0_ffn_wi, L0_ffn_wo):
    import jax
    import jax.numpy as jnp

    def _L0_attn_ref(x, Wqkv, bqkv, Wo, bo):
        import jax, jax.numpy as jnp
        import numpy as np
        B, T, D = (2, 512, 256)
        H, W = (16, 64)
        HD = D // H
        b, t, d = x.shape
        qkv = x @ Wqkv.T + bqkv
        qkv = qkv.reshape(b, t, 3, H, HD)
        q = jnp.transpose(qkv[:, :, 0], (0, 2, 1, 3))
        k = jnp.transpose(qkv[:, :, 1], (0, 2, 1, 3))
        v = jnp.transpose(qkv[:, :, 2], (0, 2, 1, 3))
        scores = jnp.einsum('bhid,bhjd->bhij', q, k) / jnp.sqrt(jnp.float32(HD))
        i = jnp.arange(t)[:, None]
        j = jnp.arange(t)[None, :]
        mask = (j <= i) & (j >= i - (W - 1))
        scores = jnp.where(mask, scores, -jnp.inf)
        probs = jax.nn.softmax(scores, axis=-1)
        y = jnp.einsum('bhij,bhjd->bhid', probs, v)
        y = jnp.transpose(y, (0, 2, 1, 3)).reshape(b, t, d)
        return y @ Wo.T + bo

    def _L0_xattn_ref(query, key, value, Wq, bq, Wk, bk, Wv, bv, gamma, beta):
        import jax, jax.numpy as jnp
        import numpy as np
        NUM_HEADS = 16
        EMBED = 256
        ATTN = 256
        HEAD_DIM = ATTN // NUM_HEADS
        NEG = -2.0 ** 32 + 1.0
        LN_EPS = 1e-05

        def _layer_norm(x, gamma, beta):
            mu = jnp.mean(x, axis=-1, keepdims=True)
            var = jnp.mean(jnp.square(x - mu), axis=-1, keepdims=True)
            return (x - mu) * jax.lax.rsqrt(var + LN_EPS) * gamma + beta
        B, S, _ = query.shape
        H, D = (NUM_HEADS, HEAD_DIM)
        q = jax.nn.relu(query @ Wq + bq)
        k = jax.nn.relu(key @ Wk + bk)
        v = jax.nn.relu(value @ Wv + bv)
        qh = q.reshape(B, S, H, D)
        kh = k.reshape(B, S, H, D)
        vh = v.reshape(B, S, H, D)
        scores = jnp.einsum('bqhd,bkhd->bhqk', qh, kh) / jnp.sqrt(jnp.float32(D))
        causal = jnp.tril(jnp.ones((S, S), jnp.bool_))
        scores = jnp.where(causal[None, None], scores, jnp.float32(NEG))
        probs = jax.nn.softmax(scores, axis=-1)
        out = jnp.einsum('bhqk,bkhd->bqhd', probs, vh).reshape(B, S, H * D)
        out = out + q
        return _layer_norm(out, gamma, beta)

    def _L0_ffn_ref(input_emb, w_router, wi, wo):
        import jax, jax.numpy as jnp
        import numpy as np
        NUM_GROUPS = 2
        EXPERT_CAPACITY = 160
        NUM_SELECTED = 2
        B, S, H = input_emb.shape
        E = w_router.shape[1]
        G = NUM_GROUPS
        T = B * S // G
        C = EXPERT_CAPACITY
        K = NUM_SELECTED
        x = input_emb.reshape(G, T, H)
        router_logits = jnp.einsum('gth,he->gte', x.astype(jnp.float32), w_router.astype(jnp.float32))
        router_probs = jax.nn.softmax(router_logits, axis=-1)
        gate, idx = jax.lax.top_k(router_probs, K)
        mask = jax.nn.one_hot(idx, E, dtype=jnp.float32)
        mask_kt = jnp.swapaxes(mask, 1, 2).reshape(G, K * T, E)
        pos = jnp.cumsum(mask_kt, axis=1) * mask_kt - 1.0
        pos = jnp.swapaxes(pos.reshape(G, K, T, E), 1, 2)
        disp_k = jax.nn.one_hot(pos, C, dtype=jnp.float32) * mask[..., None]
        dispatch = disp_k.sum(axis=2)
        combine = jnp.einsum('gtk,gtkec->gtec', gate, disp_k)
        expert_in = jnp.einsum('gtec,gth->egch', dispatch, x)
        h = jax.nn.relu(jnp.einsum('egch,ehf->egcf', expert_in, wi))
        expert_out = jnp.einsum('egcf,efh->egch', h, wo)
        y = jnp.einsum('gtec,egch->gth', combine, expert_out)
        return y.reshape(B, S, H)
    x = _layernorm(x + _L0_attn_ref(x, L0_attn_Wqkv, L0_attn_bqkv, L0_attn_Wo, L0_attn_bo), axis=-1)
    x = _layernorm(x + _L0_xattn_ref(x, ctx_1024, ctx_1024, L0_xattn_Wq, L0_xattn_bq, L0_xattn_Wk, L0_xattn_bk, L0_xattn_Wv, L0_xattn_bv, L0_xattn_gamma, L0_xattn_beta), axis=-1)
    x = _layernorm(x + _L0_ffn_ref(x, L0_ffn_w_router, L0_ffn_wi, L0_ffn_wo), axis=-1)
    return x

_drawn_inputs = setup_inputs


def setup_inputs(seed=0):
    import zlib

    import numpy as np

    out = dict(_drawn_inputs(seed))
    spreads = {'L0_xattn_bq': (0.0, 0.1),
     'L0_xattn_bk': (0.0, 2.0),
     'L0_xattn_bv': (0.0, 0.1),
     'L0_xattn_gamma': (1.0, 0.2),
     'L0_xattn_beta': (0.0, 0.1)}
    factors = {'L0_attn_bqkv': 5.039}
    for name, (base, spread) in spreads.items():
        noise = np.random.default_rng([zlib.crc32(name.encode()), seed]).standard_normal(out[name].shape)
        drawn = base * np.exp(spread * noise) if base else spread * noise
        out[name] = jnp.asarray(drawn.astype(out[name].dtype))
    for name, factor in factors.items():
        out[name] = (out[name] * factor).astype(out[name].dtype)
    return out
```

```python
from contextlib import ExitStack

import concourse.bass as bass
from concourse import mybir

F32 = mybir.dt.float32
BF16 = mybir.dt.bfloat16
U32 = mybir.dt.uint32
ALU = mybir.AluOpType
ACT = mybir.ActivationFunctionType
AX = mybir.AxisListType.X

P = 128
B, T, D = 8, 256, 256
H, HD, WIN = 16, 16, 64
C = D // P
STEP_B = 2
ST = STEP_B * T
STEPS = B // STEP_B
TT = ST // P
QT = T // P
NT = B * QT
G = H // 4
Q_SLOTS = (0, 1, 0, 1, 2, 0)
K_SLOTS = (0, 0, 1, 1, 0, 2)
KR = 6 * HD
MR = 3
KEYS0 = {"s": 192, "c": 256}
E, TOPK, CAP, F = 8, 2, 160, 1024
GROUPS = 2
GT = NT // GROUPS
SLOTS = GROUPS * CAP
FC = F // P
FULL = SLOTS // P
REST = SLOTS - FULL * P
BAD = 4096.0
NEG = -3.0e38
EPS = 1e-5

PROLOGUE = (
    [("SF",)] + [("N", "s", 0, g) for g in range(G)] + [("CK",), ("M", "s", 0)]
    + [("N", "s", 1, 0), ("N", "s", 1, 1), ("T", "s", 0, 0), ("N", "s", 1, 2), ("T", "s", 0, 1), ("N", "s", 1, 3)]
    + [("T", "s", 0, 2), ("M", "s", 1), ("T", "s", 0, 3), ("Y1", "s", 0), ("T", "s", 1, 0), ("Y2", "s", 0)]
    + [("T", "s", 1, 1), ("Y3", "s", 0), ("T", "s", 1, 2), ("T", "s", 1, 3), ("Y1", "s", 1), ("CV",), ("Y2", "s", 1)]
    + [("Y3", "s", 1), ("CQ",)]
)
LOOP = (
    [("SF",)] + [("N", "c", 0, g) for g in range(G)] + [("N", "c", 1, 0), ("M", "c", 0)]
    + [("N", "c", 1, g) for g in range(1, G)] + [("T", "c", 0, 0), ("M", "c", 1), ("T", "c", 0, 1)]
    + [("T", "c", 0, 2), ("T", "c", 0, 3), ("Y1", "c", 0)]
    + [("N", "s", 0, 0), ("N", "s", 0, 1), ("T", "c", 1, 0), ("N", "s", 0, 2), ("T", "c", 1, 1), ("N", "s", 0, 3)]
    + [("R", "c", 0), ("T", "c", 1, 2), ("M", "s", 0), ("T", "c", 1, 3), ("Y1", "c", 1)]
    + [("N", "s", 1, 0), ("N", "s", 1, 1), ("T", "s", 0, 0), ("N", "s", 1, 2), ("T", "s", 0, 1), ("N", "s", 1, 3)]
    + [("R", "c", 1), ("T", "s", 0, 2), ("M", "s", 1), ("T", "s", 0, 3), ("Y1", "s", 0), ("T", "s", 1, 0), ("Y2", "s", 0)]
    + [("T", "s", 1, 1), ("Y3", "s", 0), ("T", "s", 1, 2), ("T", "s", 1, 3), ("Y1", "s", 1), ("CK",), ("Y2", "s", 1)]
    + [("CV",), ("Y3", "s", 1), ("CQ",)]
)
EPILOGUE = (
    [("N", "c", 0, g) for g in range(G)] + [("N", "c", 1, 0), ("M", "c", 0)]
    + [("N", "c", 1, g) for g in range(1, G)] + [("T", "c", 0, 0), ("M", "c", 1), ("T", "c", 0, 1)]
    + [("T", "c", 0, 2), ("T", "c", 0, 3), ("Y1", "c", 0)]
    + [("T", "c", 1, 0), ("T", "c", 1, 1), ("R", "c", 0), ("T", "c", 1, 2), ("T", "c", 1, 3), ("Y1", "c", 1)]
    + [("R", "c", 1)]
)

WORK_JOBS = {"SF": 8, "CK": 4, "CV": 2, "CQ": 4, "M": 1, "Y1s": 2, "Y1c": 3, "Y2": 1, "Y3": 1, "R": 2, "W": 9}
WB = 2
W_LOADS = 10


def jobs_of(seg):
    return WORK_JOBS[seg[0] + seg[1] if seg[0] == "Y1" else seg[0]]


XB = 6
PAIR_JOBS = [(kind, i, n) for i in range(2) for kind, count in (("h", FC), ("y", FULL + 1)) for n in range(count)]
PER_BANK = [len(PAIR_JOBS[b::XB]) for b in range(XB)]


def expert_turn(job, it):
    kind, i, n = job
    if kind == "x":
        return XB + n, it * 2 + i
    n = PAIR_JOBS.index(job)
    return n % XB, it * PER_BANK[n % XB] + n // XB


class WorkTurns:

    def __init__(self):
        self.local = {}
        self.total = {}
        for name, plan in (("pro", [("W",)] + PROLOGUE), ("loop", LOOP), ("epi", EPILOGUE)):
            n, count = 0, [0] * WB
            for seg in plan:
                if seg[0] in ("N", "T"):
                    continue
                for j in range(jobs_of(seg)):
                    b = n % WB
                    self.local[(name, seg, j)] = (b, count[b])
                    count[b] += 1
                    n += 1
            self.total[name] = count

    def at(self, phase, seg, j):
        name, it = phase
        b, n = self.local[(name, seg, j)]
        if name == "loop":
            return b, it * self.total["loop"][b] + self.total["pro"][b] + n
        if name == "epi":
            return b, (STEPS - 1) * self.total["loop"][b] + self.total["pro"][b] + n
        return b, n


def wait(eng, sem, value):
    if not isinstance(value, int) or value > 0:
        eng.wait_ge(sem, value)


def attention_and_experts(nc: bass.Bass, a, out):
    turns = WorkTurns()
    with ExitStack() as ctx:
        def sb(name, shape, dt=F32):
            return ctx.enter_context(nc.sbuf_tensor(name, shape, dt))

        def sem(name):
            return ctx.enter_context(nc.semaphore(name))

        work = [ctx.enter_context(nc.psum_tensor(f"work{i}", [P, 512], F32)) for i in range(WB)]
        nat = [ctx.enter_context(nc.psum_tensor(f"nat{i}", [P, 512], F32)) for i in range(2)]
        byk = [ctx.enter_context(nc.psum_tensor(f"byk{i}", [P, 512], F32)) for i in range(2)]
        pv = ctx.enter_context(nc.psum_tensor("pv", [P, 512], F32))
        spare = ctx.enter_context(nc.psum_tensor("spare", [P, 512], F32))

        ident = sb("ident", [P, P])
        identb = sb("identb", [P, P], BF16)
        mq0 = {"s": sb("mq0s", [P, 4, P], BF16), "c": sb("mq0c", [P, 4, P], BF16)}
        mq1 = {"s": sb("mq1s", [P, 2, 192], BF16), "c": sb("mq1c", [P, 2, 256], BF16)}
        mk0 = {"s": sb("mk0s", [P, 2, 192], BF16), "c": sb("mk0c", [P, 2, 256], BF16)}
        mk1 = {"s": sb("mk1s", [P, 4, P], BF16), "c": sb("mk1c", [P, 4, P], BF16)}
        wqkvT = sb("wqkvT", [P, C, 3 * D])
        woT = sb("woT", [P, C, D])
        wc = {n: sb(f"w{n}_c", [P, C, D]) for n in "qkv"}
        bias_rows = sb("bias_rows", [4 * C, P])
        bias = sb("bias", [P, 2, 2 * C])
        bv = {"s": sb("bv_s", [P, D]), "c": sb("bv_c", [P, D])}
        bo = sb("bo", [P, D])
        gamma = sb("gamma", [P, D])
        beta = sb("beta", [P, D])
        wr = sb("wr", [P, C, 8])
        xres = sb("xres", [P, NT, D])
        xin = sb("xin", [P, TT, D])
        ctxin = sb("ctxin", [P, TT, D])
        xb = sb("xb", [P, TT, D])
        xT = sb("xT", [P, C, ST])
        fq = {"s": sb("fq_s", [P, C, ST]), "c": sb("fq_c", [P, C, ST])}
        fk = sb("fk", [P, C, ST])
        resq = sb("resq", [P, ST])
        resk = sb("resk", [P, ST])
        parts = {"q": sb("parts_q", [P, C, 3, ST], BF16), "k": sb("parts_k", [P, C, 3, ST], BF16)}
        arena = sb("arena", [P, 4 * H * ST // 2])
        ARENA_U = H * ST // 2
        stack = {}
        for i, key in enumerate(("sq", "sk", "cq", "ck")):
            stack[key] = arena[:, i * ARENA_U:(i + 1) * ARENA_U].bitcast(BF16).rearrange("p (h t) -> p h t", h=H)
        vone = {"s": sb("v_s", [P, TT, H, 32]), "c": sb("v_c", [P, TT, H, 32])}
        negm = sb("negm", [P, QT, H])
        rm = sb("rm", [P, QT, H])
        mp = sb("mp", [P, QT, P], BF16)
        mT = sb("mT", [MR * H, T], BF16)
        probs = sb("probs", [P, 2, 4, 384])
        yT = sb("yT", [P, G, T])
        rec = sb("rec", [P, QT, H])
        ynat = sb("ynat", [P, QT, D])
        ynT = sb("ynT", [P, C, T])
        r = sb("r", [P, QT, D])
        stats = sb("stats", [P, QT, 6])
        mv = sb("mv", [P, QT, 2])
        rstd = sb("rstd", [P, QT])
        lnv = sb("lnv", [P, QT])
        newton = sb("newton", [P, QT])
        eps = sb("eps", [P, 1])
        x1 = sb("x1", [P, TT, D])
        x2 = sb("x2", [P, QT, D])
        x2T = sb("x2T", [P, C, T])
        logits = sb("logits", [P, NT, E])
        iota_e = sb("iota_e", [P, E])
        tri = sb("tri", [P, P], BF16)
        onesb = sb("onesb", [P, P], BF16)
        NM = GROUPS * E * TOPK * GT
        goes_on = sb("goes_on", [P, NM])
        gbase = sb("gbase", [P, GROUPS, TOPK * GT])
        top = sb("top", [P, NT, 8])
        topi = sb("topi", [P, NT, 8], U32)
        diff = sb("diff", [P, NT, 8])
        expd = sb("expd", [P, NT, 8])
        esum = sb("esum", [P, NT])
        gates = sb("gates", [P, NT, TOPK])
        idxf = sb("idxf", [P, NT, TOPK])
        choice = sb("choice", [P, NM], BF16)
        before = sb("before", [P, NM])
        pos = sb("pos", [P, GROUPS, TOPK * GT])
        slot = sb("slot", [P, GROUPS, TOPK * GT])
        late = sb("late", [P, GROUPS, TOPK * GT])
        put = sb("put", [P, GROUPS * TOPK * GT], U32)
        get = sb("get", [P, GROUPS * TOPK * GT], U32)
        WI, WO, HT_, XE, XET = C * F, FC * D, FC * SLOTS, (FULL + 1) * D, C * SLOTS
        at = 0
        wi, wo, hT, xe, xeT = [], [], [], [], []
        for group, size, lead in ((wi, WI, C), (wo, WO, FC), (hT, HT_, FC), (xe, XE, FULL + 1), (xeT, XET, C)):
            for i in range(2):
                group.append(arena[:, at:at + size].rearrange("p (c n) -> p c n", c=lead))
                at += size
        assert at <= 4 * ARENA_U
        YE = FULL * D + P
        ye = [xb[:, :, :].rearrange("p a b -> p (a b)")[:, 0:YE], ctxin[:, :, :].rearrange("p a b -> p (a b)")[:, 0:YE]]
        got = arena[:, 0:NT * TOPK * D].rearrange("p (n d) -> p n d", d=D)
        zeros = sb("zeros", [P, D])

        part_dram = {k: nc.dram_tensor(f"part_{k}", [D, 3, ST], BF16).ap() for k in ("sq", "sk", "cq", "ck")}
        m_dram = nc.dram_tensor("m_rows", [MR, H, T], BF16).ap()

        x_dram = nc.dram_tensor("expert_x", [E * SLOTS, D], F32).ap()
        y_dram = nc.dram_tensor("expert_y", [E * SLOTS + 1, D], F32).ap()

        cleared = sem("cleared"); zeros_ready = sem("zeros_ready"); routed = sem("routed")
        diff_ready = sem("diff_ready"); expd_ready = sem("expd_ready"); choice_ready = sem("choice_ready")
        counted = sem("counted"); put_done = sem("put_done"); got_sem = [sem(f"got{i}") for i in range(NT // QT)]
        wi_in = [sem(f"wi_in{i}") for i in range(2)]; wo_in = [sem(f"wo_in{i}") for i in range(2)]
        xe_in = [sem(f"xe_in{i}") for i in range(2)]
        ex_full = [sem(f"ex_full{i}") for i in range(XB + C)]
        ex_free = [sem(f"ex_free{i}") for i in range(XB + C)]
        y_stored = [sem(f"y_stored{i}") for i in range(2)]
        out_ready = sem("out_ready"); out_stored = [sem(f"out_stored{i}") for i in range(2)]
        w_in = sem("w_in"); w_in2 = sem("w_in2"); x_in = sem("x_in"); ctx_in = sem("ctx_in")
        consts = sem("consts"); ones_ready = sem("ones_ready");
        work_full = [sem(f"work_full{i}") for i in range(WB)]
        work_free = [sem(f"work_free{i}") for i in range(WB)]
        nat_full = [sem(f"nat_full{i}") for i in range(2)]
        nat_free = [sem(f"nat_free{i}") for i in range(2)]
        byk_full = [sem(f"byk_full{i}") for i in range(2)]
        pv_full = sem("pv_full")
        yT_ready = sem("yT_ready")
        xin_ready = sem("xin_ready"); xb_ready = sem("xb_ready")
        split = {"q": sem("split_q"), "k": sem("split_k")}
        stored = {"q": sem("stored_q"), "k": sem("stored_k")}
        stacked = {k: sem(f"stacked_{k}") for k in ("sq", "sk", "cq", "ck")}
        v_ready = sem("v_ready")
        mp_ready = sem("mp_ready")
        m_stored = sem("m_stored"); m_rows = sem("m_rows")
        exp_ready = sem("exp_ready")
        x1_ready = sem("x1_ready"); x2_ready = sem("x2_ready")
        x2_free = sem("x2_free")
        var_ready = sem("var_ready"); rstd_ready = sem("rstd_ready"); lnv_ready = sem("lnv_ready")
        dve_seq = sem("dve_seq"); pool_seq = sem("pool_seq")
        done = sem("done")

        def unit(step, layer, b):
            return step * 4 + (b if layer == "s" else 2 + b)

        def norms_before(step, layer, b):
            return step * 6 + (b if layer == "s" else 2 + 2 * b)

        def walk(handlers, fori):
            def run(plan, phase, s_step, c_step):
                for seg in plan:
                    f = handlers.get(seg[0])
                    if f is not None:
                        step = c_step if len(seg) > 1 and seg[1] == "c" else s_step
                        f(phase, seg, step, *seg[1:])
            run(PROLOGUE, ("pro", 0), 0, 0)
            with fori(0, STEPS - 1) as it:
                if "begin" in handlers:
                    handlers["begin"]()
                run(LOOP, ("loop", it), it + 1, it)
            if "begin" in handlers:
                handlers["begin"]()
            run(EPILOGUE, ("epi", 0), STEPS, STEPS - 1)

        def emptied(eng, phase, seg, *jobs):
            for j in jobs:
                b, n = turns.at(phase, seg, j)
                eng.wait_ge(work_free[b], n + 1)

        banks8 = [*work, *nat, *byk, pv, spare]

        def experts(eng, pair):
            pair(0, False)
            with eng.Fori(1, E // 2 - 1) as it:
                pair(it, False)
            pair(E // 2 - 1, True)

        def ex_result(eng, job, it):
            b, n = expert_turn(job, it)
            eng.wait_ge(ex_free[b], n + 1)

        block = ctx.enter_context(nc.Block())

        @block.sync
        def _(sp):
            x_v = a["x"].rearrange("b (t p) d -> p (b t) d", p=P)
            sp.dma_start(xin[:, :, :], x_v[:, 0:TT, :]).then_inc(x_in, 16)
            wload = arena[:, 0:6 * D].rearrange("p (m d) -> p m d", m=6)
            sp.dma_start(wload, a["L0_attn_Wqkv"].rearrange("(m p) d -> p m d", p=P)).then_inc(w_in, 16)
            sp.dma_start(arena[:, 6 * D:8 * D].rearrange("p (m d) -> p m d", m=2),
                         a["L0_attn_Wo"].rearrange("(m p) d -> p m d", p=P)).then_inc(w_in, 16)
            sp.dma_start(bias_rows[0:2 * C, :], a["L0_attn_bqkv"][0:2 * D].rearrange("(m p) -> m p", p=P)).then_inc(w_in, 16)
            for n, b_in in enumerate("qk"):
                sp.dma_start(bias_rows[(2 + n) * C:(3 + n) * C, :], a[f"L0_xattn_b{b_in}"].rearrange("(m p) -> m p", p=P))\
                    .then_inc(w_in, 16)
            for dst, src in ((bv["s"], a["L0_attn_bqkv"][2 * D:3 * D]), (bv["c"], a["L0_xattn_bv"]), (bo, a["L0_attn_bo"]),
                             (gamma, a["L0_xattn_gamma"]), (beta, a["L0_xattn_beta"])):
                sp.dma_start(dst[:, :], src.partition_broadcast(P)).then_inc(w_in, 16)
            for i in range(1, STEPS):
                sp.dma_start(xres[:, i * TT:(i + 1) * TT, :], x_v[:, i * TT:(i + 1) * TT, :]).then_inc(x_in, 16)
            for n in "qkv":
                sp.dma_start(wc[n][:, :, :], a[f"L0_xattn_W{n}"].rearrange("(c p) n -> p c n", p=P)).then_inc(w_in2, 16)
            sp.dma_start(wr[:, :, :], a["L0_ffn_w_router"].rearrange("(c p) e -> p c e", p=P)).then_inc(w_in2, 16)
            sp.wait_ge(zeros_ready, 1)
            sp.dma_start(x_dram.rearrange("(n p) d -> p n d", p=P),
                         zeros[:, :].unsqueeze(1).broadcast_to([P, E * SLOTS // P, D])).then_inc(cleared, 16)
            sp.dma_start(y_dram[E * SLOTS:E * SLOTS + 1, :], zeros[0:1, :]).then_inc(cleared, 16)
            ctx_v = a["ctx_1024"].rearrange("b (t p) d -> p (b t) d", p=P)
            part_v = {k: v.rearrange("(h r) s t -> r s h t", r=HD) for k, v in part_dram.items()}

            def held(*values):
                for v in values:
                    if not isinstance(v, int):
                        sp.compute_val(v)
                return values

            def stack_side(layer, side, step, waits):
                key = layer + side
                n_before = step * 2 + (0 if layer == "s" else 1)
                was_loaded, is_split, is_stored = held(step * (6 * 16), (n_before + 1) * C, (n_before + 1) * 16)
                waits = [(s, held(v)[0]) for s, v in waits]
                sp.wait_ge(split[side], is_split)
                wait(sp, stacked[key], was_loaded)
                sp.dma_start(part_dram[key].rearrange("(c p) s t -> p c s t", p=P), parts[side][:, :, :, :])\
                    .then_inc(stored[side], 16)
                for s, v in waits:
                    wait(sp, s, v)
                sp.wait_ge(stored[side], is_stored)
                slots = Q_SLOTS if side == "q" else K_SLOTS
                for i, part in enumerate(slots):
                    sp.dma_start(stack[key][i * HD:(i + 1) * HD, :, :], part_v[key][:, part, :, :])\
                        .then_inc(stacked[key], 16)

            def unit_used(layer, step):
                return [(pv_full, (unit(step, layer, 1) - 4 + 1) * G)]

            def SF(ph, seg, step):
                sp.dma_start(ctxin[:, :, :], ctx_v[:, bass.ds(step * TT, TT), :]).then_inc(ctx_in, 16)
                stack_side("s", "q", step, unit_used("s", step))
                if isinstance(step, int):
                    emptied(sp, ph, ("W",), 6, 7)
                stack_side("s", "k", step, [])

            def CQ(ph, seg, step):
                stack_side("c", "k", step, unit_used("c", step))
                stack_side("c", "q", step, [])

            def M(ph, seg, step, layer, b):
                were_loaded, are_stored = held(unit(step, layer, b) * 16, unit(step, layer, b) * 16 + 16)
                emptied(sp, ph, seg, 0)
                wait(sp, m_rows, were_loaded)
                sp.dma_start(m_dram.rearrange("m h t -> (m h) t"), mT[:, :]).then_inc(m_stored, 16)
                sp.wait_ge(m_stored, are_stored)
                sp.dma_start(stack[layer + "q"][KR:KR + MR, :, b * T:(b + 1) * T], m_dram).then_inc(m_rows, 16)

            walk({"SF": SF, "CQ": CQ, "M": M}, sp.Fori)

            sp.wait_ge(pv_full, 2 * B * G)
            wi_v = a["L0_ffn_wi"].rearrange("e (c p) f -> p e c f", p=P)
            wo_v = a["L0_ffn_wo"].rearrange("e (c p) d -> p e c d", p=P)

            def load_weights(e, i):
                sp.dma_start(wi[i], wi_v[:, bass.ds(e, 1), :, :].rearrange("p e c f -> p (e c) f")).then_inc(wi_in[i], 16)
                sp.dma_start(wo[i], wo_v[:, bass.ds(e, 1), :, :].rearrange("p e c f -> p (e c) f")).then_inc(wo_in[i], 16)

            def load_tokens(e, i):
                sp.dma_start(xe[i][:, 0:FULL, :], x_dram[bass.ds(e * SLOTS, FULL * P), :].rearrange("(t p) d -> p t d", p=P))\
                    .then_inc(xe_in[i], 16)
                sp.dma_start(xe[i][0:REST, FULL, :], x_dram[bass.ds(e * SLOTS + FULL * P, REST), :]).then_inc(xe_in[i], 16)

            for i in range(2):
                load_weights(i, i)
            sp.wait_ge(put_done, NT * TOPK * 16)
            for i in range(2):
                load_tokens(i, i)

            def pair(it, last):
                for i in range(2):
                    e = it * 2 + i
                    for n in range(FULL + 1):
                        ex_result(sp, ("y", i, n), it)
                    sp.dma_start(y_dram[bass.ds(e * SLOTS, FULL * P), :].rearrange("(t p) d -> p t d", p=P),
                                 ye[i][:, 0:FULL * D].rearrange("p (t d) -> p t d", t=FULL)).then_inc(y_stored[i], 16)
                    for n in range(2):
                        sp.dma_start(y_dram[bass.ds(e * SLOTS + FULL * P, REST), n * P:(n + 1) * P],
                                     ye[i][n * REST:(n + 1) * REST, FULL * D:YE]).then_inc(y_stored[i], 16)
                    if not last:
                        load_weights(e + 2, i)
                        load_tokens(e + 2, i)

            experts(sp, pair)
            out_v = out.rearrange("b (t p) d -> p (b t) d", p=P)
            for n in range(NT // QT):
                sp.wait_ge(out_ready, n + 1)
                sp.dma_start(out_v[:, n * QT:(n + 1) * QT, :], xin[:, (n % 2) * QT:(n % 2) * QT + QT, :]).then_inc(out_stored[n % 2], 16)
            for i in range(2):
                sp.wait_ge(out_stored[i], 16 * (NT // QT // 2))

        @block.tensor
        def _(pe):
            def work_job(phase, seg, j, emit):
                b, n = turns.at(phase, seg, j)
                wait(pe, work_free[b], n)
                emit(work[b]).then_inc(work_full[b], 1)

            def transposes(bank, srcs):
                for i, src in enumerate(srcs):
                    last = nc.tensor.transpose(bank[:, i * P:(i + 1) * P], src, ident[:, :])
                return last

            def by_feature(bank, w, m):
                for c in range(C):
                    last = nc.tensor.matmul(bank[:, :], w[:, c, m * P:(m + 1) * P], xT[:, c, :], start=(c == 0), stop=(c == C - 1))
                return last

            def by_token(bank, w, t0):
                for t in range(2):
                    for c in range(C):
                        last = nc.tensor.matmul(bank[:, t * D:(t + 1) * D], xT[:, c, (t0 + t) * P:(t0 + t + 1) * P], w[:, c, :],
                                                start=(c == 0), stop=(c == C - 1))
                return last

            def chunks_in(phase, seg, src):
                for c in range(C):
                    work_job(phase, seg, c, lambda bank: transposes(bank, [src[:, t, c * P:(c + 1) * P] for t in range(TT)]))

            pe.wait_ge(consts, 1)
            pe.wait_ge(w_in, 16 * W_LOADS)
            for m in range(8):
                work_job(("pro", 0), ("W",), m,
                         lambda bank: transposes(bank, [arena[:, m * D + c * P:m * D + (c + 1) * P] for c in range(C)]))

            work_job(("pro", 0), ("W",), 8, lambda bank: nc.tensor.transpose(bank[:, 0:4 * C], bias_rows[:, :], ident[0:4 * C, 0:4 * C]))

            def SF(ph, seg, step):
                if isinstance(step, int):
                    pe.wait_ge(x_in, 16)
                else:
                    pe.wait_ge(xin_ready, step)
                chunks_in(ph, seg, xin)
                if isinstance(step, int):
                    emptied(pe, ph, ("W",), 6, 7)
                emptied(pe, ph, seg, 0, 1)
                for m in range(C):
                    work_job(ph, seg, C + m, lambda bank: by_feature(bank, wqkvT, m))
                for m in range(C):
                    work_job(ph, seg, 2 * C + m, lambda bank: by_feature(bank, wqkvT, C + m))
                for n in range(2):
                    work_job(ph, seg, 3 * C + n, lambda bank: by_token(bank, wqkvT[:, :, 2 * D:3 * D], 2 * n))

            def CK(ph, seg, step):
                pe.wait_ge(ctx_in, (step + 1) * 16)
                if isinstance(step, int):
                    pe.wait_ge(w_in2, 16 * 4)
                chunks_in(ph, seg, ctxin)
                emptied(pe, ph, seg, 0, 1)
                for m in range(C):
                    work_job(ph, seg, C + m, lambda bank: by_feature(bank, wc["k"], m))

            def CV(ph, seg, step):
                for n in range(2):
                    work_job(ph, seg, n, lambda bank: by_token(bank, wc["v"], 2 * n))

            def CQ(ph, seg, step):
                pe.wait_ge(x1_ready, (step + 1) * STEP_B)
                chunks_in(ph, seg, x1)
                emptied(pe, ph, seg, 0, 1)
                for m in range(C):
                    work_job(ph, seg, C + m, lambda bank: by_feature(bank, wc["q"], m))

            def bank_scores(bank, full, mask, pairs):
                n = mask.shape[1] * mask.shape[2]
                nc.tensor.matmul(bank[:, 0:n], identb[:, :], mask[:, :, :].rearrange("p a b -> p (a b)"), start=True, stop=False)
                w = mask.shape[2]
                for i, (lhsT, rhs) in enumerate(pairs):
                    last = nc.tensor.matmul(bank[:, i * w:(i + 1) * w], lhsT, rhs, start=False, stop=(i == len(pairs) - 1))
                last.then_inc(full, 1)

            def N(ph, seg, step, layer, b, g):
                q, k = stack[layer + "q"], stack[layer + "k"]
                if b == 0 and g == 0:
                    pe.wait_ge(stacked[layer + "q"], (step + 1) * (6 * 16))
                    pe.wait_ge(stacked[layer + "k"], (step + 1) * (6 * 16))
                U = unit(step, layer, b)
                t0 = b * T
                k1 = t0 + T - mq1[layer].shape[2]
                banks = [(mq0[layer], range(4 * g, 4 * g + 4), t0, t0)]
                banks += [(mq1[layer], range(4 * g + 2 * n, 4 * g + 2 * n + 2), t0 + P, k1) for n in range(2)]
                for i, (mask, heads, q0, k0) in enumerate(banks):
                    job = 3 * g + i
                    wait(pe, nat_free[job % 2], U * 6 + job // 2)
                    bank_scores(nat[job % 2], nat_full[job % 2], mask,
                                [(q[0:KR, h, q0:q0 + P], k[0:KR, h, k0:k0 + mask.shape[2]]) for h in heads])

            def M(ph, seg, step, layer, b):
                pe.wait_ge(mp_ready, unit(step, layer, b) + 1)

                def rows(bank):
                    o = bank[:, :].bitcast(BF16)
                    for t in range(QT):
                        last = nc.tensor.transpose(o[:, t * P:(t + 1) * P], mp[:, t, :], identb[:, :])
                    return last
                work_job(ph, seg, 0, rows)

            def product_v(ph, step, U, layer, b, g):
                pe.wait_ge(exp_ready, U * (3 * G) + 3 * g + 3)
                if g == 0 and layer == "s":
                    emptied(pe, ph, ("SF",), 3 * C, 3 * C + 1)
                elif g == 0:
                    pe.wait_ge(v_ready, (step + 1) * 2)
                wait(pe, yT_ready, U * G + g)
                for kt in range(QT):
                    for j in range(4):
                        h = 4 * g + j
                        cols, src = ((0, KEYS0[layer]), (0, KEYS0[layer])) if kt == 0 else ((P, T), (256, 384))
                        last = nc.tensor.matmul(pv[32 * j:32 * j + 32, cols[0]:cols[1]], vone[layer][:, b * QT + kt, h, :],
                                                probs[:, g % 2, j, src[0]:src[1]], start=(kt == 0), stop=(kt == QT - 1),
                                                skip_group_check=True)
                last.then_inc(pv_full, 1)

            def T_(ph, seg, step, layer, b, g):
                q, k = stack[layer + "q"], stack[layer + "k"]
                U = unit(step, layer, b)
                if g == 0:
                    pe.wait_ge(m_rows, U * 16 + 16)
                    if ph[0] == "pro" and b == 0:
                        pe.wait_ge(ones_ready, 1)
                t0, n0 = b * T, KEYS0[layer]
                banks = [(mk0[layer], range(4 * g + 2 * n, 4 * g + 2 * n + 2), t0, t0, n0) for n in range(2)]
                banks.append((mk1[layer], range(4 * g, 4 * g + 4), t0 + P, t0 + P, P))
                for i, (mask, heads, k0, q0, w) in enumerate(banks):
                    job = 3 * g + i
                    wait(pe, exp_ready, U * (3 * G) + job - 1)
                    bank_scores(byk[job % 2], byk_full[job % 2], mask,
                                [(k[0:KR + MR, h, k0:k0 + P], q[0:KR + MR, h, q0:q0 + w]) for h in heads])
                if g > 0:
                    product_v(ph, step, U, layer, b, g - 1)
                if g == G - 1:
                    product_v(ph, step, U, layer, b, g)

            def Y1(ph, seg, step, layer, b):
                U = unit(step, layer, b)
                pe.wait_ge(yT_ready, (U + 1) * G)
                for t in range(QT):
                    work_job(ph, seg, t, lambda bank: transposes(bank, [yT[:, g, t * P:(t + 1) * P] for g in range(G)]))
                if layer == "c":
                    work_job(ph, seg, QT, lambda bank: transposes(
                        bank, [fq["c"][:, c, b * T + t * P:b * T + (t + 1) * P] for t in range(QT) for c in range(C)]))

            def Y2(ph, seg, step, layer, b):
                emptied(pe, ph, ("Y1", "s", b), 0, 1)
                work_job(ph, seg, 0, lambda bank: transposes(
                    bank, [ynat[:, t, c * P:(c + 1) * P] for c in range(C) for t in range(QT)]))

            def Y3(ph, seg, step, layer, b):
                emptied(pe, ph, ("Y2", "s", b), 0)

                def project(bank):
                    for t in range(QT):
                        for c in range(C):
                            last = nc.tensor.matmul(bank[:, t * D:(t + 1) * D], ynT[:, c, t * P:(t + 1) * P], woT[:, c, :],
                                                    start=(c == 0), stop=(c == C - 1))
                    return last
                work_job(ph, seg, 0, project)

            def R(ph, seg, step, layer, b):
                pe.wait_ge(x2_ready, step * STEP_B + b + 1)
                work_job(ph, seg, 0, lambda bank: transposes(
                    bank, [x2[:, t, c * P:(c + 1) * P] for c in range(C) for t in range(QT)]))
                emptied(pe, ph, seg, 0)

                def router(bank):
                    for t in range(QT):
                        for c in range(C):
                            last = nc.tensor.matmul(bank[:, t * 8:(t + 1) * 8], x2T[:, c, t * P:(t + 1) * P], wr[:, c, :],
                                                    start=(c == 0), stop=(c == C - 1))
                    return last
                work_job(ph, seg, 1, router)

            pe.wait_ge(consts, 2)
            walk({"SF": SF, "CK": CK, "CV": CV, "CQ": CQ, "N": N, "M": M, "T": T_, "Y1": Y1, "Y2": Y2, "Y3": Y3, "R": R}, pe.Fori)

            pe.wait_ge(choice_ready, 1)
            pe.wait_ge(consts, 2)
            nc.tensor.matmul(spare[:, 0:NM], tri[:, :], choice[:, :], start=True, stop=True)
            nc.tensor.matmul(spare[:, NM:2 * NM], onesb[:, :], choice[:, :], start=False, stop=True, skip_group_check=True)\
                .then_inc(counted, 1)

            emptied(pe, ("epi", 0), ("R", "c", 1), 0, 1)
            pe.wait_ge(exp_ready, 2 * B * 3 * G)
            pe.wait_ge(yT_ready, 2 * B * G)
            pe.wait_ge(routed, 1)

            def ex_job(job, it, emit):
                b, n = expert_turn(job, it)
                wait(pe, ex_free[b], n)
                emit(banks8[b]).then_inc(ex_full[b], 1)

            def tokens_T(i, it):
                pe.wait_ge(xe_in[i], it * 32 + 32)
                for c in range(C):
                    def emit(bank):
                        for t in range(FULL + 1):
                            n = P if t < FULL else REST
                            mm = nc.tensor.transpose(bank[:, t * P:t * P + n], xe[i][0:n, t, c * P:(c + 1) * P], ident[0:n, 0:n])
                        return mm
                    ex_job(("x", i, c), it, emit)

            def hidden(i, it):
                pe.wait_ge(wi_in[i], it * 16 + 16)
                for f in range(FC):
                    def emit(bank):
                        for c in range(C):
                            mm = nc.tensor.matmul(bank[:, 0:SLOTS], wi[i][:, c, f * P:(f + 1) * P], xeT[i][:, c, :],
                                                  start=(c == 0), stop=(c == C - 1))
                        return mm
                    ex_job(("h", i, f), it, emit)

            def output(i, it):
                pe.wait_ge(wo_in[i], it * 16 + 16)
                for f in range(FC):
                    ex_result(pe, ("h", i, f), it)
                for t in range(FULL):
                    def emit(bank):
                        for f in range(FC):
                            mm = nc.tensor.matmul(bank[:, 0:D], hT[i][:, f, t * P:(t + 1) * P], wo[i][:, f, :],
                                                  start=(f == 0), stop=(f == FC - 1))
                        return mm
                    ex_job(("y", i, t), it, emit)

                def rest(bank):
                    for f in range(FC):
                        for n in range(2):
                            mm = nc.tensor.matmul(bank[n * REST:(n + 1) * REST, 0:P], hT[i][:, f, FULL * P:SLOTS],
                                                  wo[i][:, f, n * P:(n + 1) * P], start=(f == 0), stop=(f == FC - 1),
                                                  skip_group_check=True)
                    return mm
                ex_job(("y", i, FULL), it, rest)

            def pair(it, last):
                for i in range(2):
                    for c in range(C):
                        ex_result(pe, ("x", i, c), it)
                    hidden(i, it)
                    if not (last and i == 1):
                        tokens_T(1 - i, it + i)
                    output(i, it)

            tokens_T(0, 0)
            experts(pe, pair)

        @block.scalar
        def _(act):
            nc.scalar.preload_act_table_set("natural_log_exp_and_others")
            def take(phase, seg, j, emit):
                b, n = turns.at(phase, seg, j)
                act.wait_ge(work_full[b], n + 1)
                return emit(work[b]).then_inc(work_free[b], 1)

            def copy_out(phase, seg, j, dst, cols=512):
                take(phase, seg, j, lambda bank: nc.scalar.activation(dst, bank[:, 0:cols] if dst.ndim == 2 else
                     bank[:, 0:cols].rearrange("p (a b) -> p a b", a=dst.shape[1]), ACT.Copy))

            def xT_out(ph, seg):
                for c in range(C):
                    copy_out(ph, seg, c, xT[:, c, :])

            def f_out(phase, seg, j, dst, part, func, bias, scale):
                def emit(bank):
                    nc.scalar.activation(dst, bank[:, :], func, bias=bias, scale=scale)
                    return nc.scalar.activation(part, bank[:, :], func, bias=bias, scale=scale)
                take(phase, seg, j, emit)

            for m in range(8):
                dst = wqkvT[:, :, m * P:(m + 1) * P] if m < 6 else woT[:, :, (m - 6) * P:(m - 5) * P]
                copy_out(("pro", 0), ("W",), m, dst, cols=2 * P)

            def q_step(step, layer):
                return step * 2 + (0 if layer == "s" else 1)

            def SF(ph, seg, step):
                xT_out(ph, seg)
                if isinstance(step, int):
                    emptied(act, ph, ("W",), 8)
                    act.wait_ge(consts, 2)
                wait(act, stored["q"], q_step(step, "s") * 16)
                for m in range(C):
                    f_out(ph, seg, C + m, fq["s"][:, m, :], parts["q"][:, m, 0, :], ACT.Identity, bias[:, 0, m:m + 1], 0.25)
                wait(act, stored["k"], q_step(step, "s") * 16)
                for m in range(C):
                    f_out(ph, seg, 2 * C + m, fk[:, m, :], parts["k"][:, m, 0, :], ACT.Identity, bias[:, 0, C + m:C + m + 1], 1.0)

            def CK(ph, seg, step):
                xT_out(ph, seg)
                act.wait_ge(stored["k"], q_step(step, "c") * 16)
                for m in range(C):
                    f_out(ph, seg, C + m, fk[:, m, :], parts["k"][:, m, 0, :], ACT.Relu, bias[:, 1, C + m:C + m + 1], 1.0)

            def CQ(ph, seg, step):
                xT_out(ph, seg)
                act.wait_ge(stored["q"], q_step(step, "c") * 16)
                for m in range(C):
                    f_out(ph, seg, C + m, fq["c"][:, m, :], parts["q"][:, m, 0, :], ACT.Relu, bias[:, 1, m:m + 1], 0.25)

            def M(ph, seg, step, layer, b):
                U = unit(step, layer, b)
                wait(act, m_stored, U * 16)
                take(ph, seg, 0, lambda bank: nc.scalar.activation(mT[:, :], bank[0:MR * H, :].bitcast(BF16)[:, 0:T], ACT.Copy))

            def yT_out(U, g):
                act.wait_ge(pv_full, U * G + g + 1)
                nc.scalar.activation(yT[:, g, :], pv[:, 0:T], ACT.Copy).then_inc(yT_ready, 1)

            def T_(ph, seg, step, layer, b, g):
                U = unit(step, layer, b)
                n0 = KEYS0[layer]
                wait(act, pv_full, U * G + g - 1)
                for i in range(3):
                    job = 3 * g + i
                    act.wait_ge(byk_full[job % 2], U * 6 + job // 2 + 1)
                    if i < 2:
                        dst, src = probs[:, g % 2, 2 * i:2 * i + 2, 0:n0], byk[job % 2][:, 0:2 * n0].rearrange("p (a b) -> p a b", a=2)
                    else:
                        dst, src = probs[:, g % 2, :, 256:384], byk[job % 2][:, :].rearrange("p (a b) -> p a b", a=4)
                    nc.scalar.activation(dst, src, ACT.Exp).then_inc(exp_ready, 1)
                if g > 0:
                    yT_out(U, g - 1)
                if g == G - 1:
                    yT_out(U, g)

            def rstd_of(number):
                act.wait_ge(var_ready, number + 1)
                nc.scalar.activation(lnv[:, :], mv[:, :, 1], ACT.Ln, bias=eps[:, :]).then_inc(lnv_ready, 1)
                act.wait_ge(lnv_ready, number + 1)
                nc.scalar.activation(rstd[:, :], lnv[:, :], ACT.Exp, scale=-0.5).then_inc(rstd_ready, 1)

            def Y1(ph, seg, step, layer, b):
                if layer == "c":
                    for i in range(2):
                        rstd_of(norms_before(step, layer, b) + i)

            def Y3(ph, seg, step, layer, b):
                rstd_of(norms_before(step, layer, b))

            def Y2(ph, seg, step, layer, b):
                copy_out(ph, seg, 0, ynT[:, :, :])

            def R(ph, seg, step, layer, b):
                copy_out(ph, seg, 0, x2T[:, :, :])

            walk({"SF": SF, "CK": CK, "CQ": CQ, "M": M, "T": T_, "Y1": Y1, "Y2": Y2, "Y3": Y3, "R": R}, act.Fori)

            act.wait_ge(diff_ready, 1)
            nc.scalar.activation(expd[:, :, :], diff[:, :, :], ACT.Exp).then_inc(expd_ready, 1)

            def ex_take(job, it, emit):
                b, n = expert_turn(job, it)
                act.wait_ge(ex_full[b], n + 1)
                emit(banks8[b]).then_inc(ex_free[b], 1)

            def tokens_T(i, it):
                if i == 0 and isinstance(it, int) and it == 0:
                    act.wait_ge(routed, 1)
                for c in range(C):
                    ex_take(("x", i, c), it, lambda bank: nc.scalar.activation(xeT[i][:, c, :], bank[:, 0:SLOTS], ACT.Copy))

            def pair(it, last):
                for i in range(2):
                    for f in range(0, FC, 2):
                        ex_take(("h", i, f), it, lambda bank: nc.scalar.activation(hT[i][:, f, :], bank[:, 0:SLOTS], ACT.Relu))
                    if not (last and i == 1):
                        tokens_T(1 - i, it + i)
                    wait(act, y_stored[i], it * 48)
                    ex_take(("y", i, 1), it, lambda bank: nc.scalar.activation(ye[i][:, D:2 * D], bank[:, 0:D], ACT.Copy))

            tokens_T(0, 0)
            experts(act, pair)

            for n in range(NT // QT):
                rstd_of(6 * STEPS + n)

        @block.vector
        def _(dve):
            V = nc.vector
            seq = [0]

            def link(ins):
                seq[0] += 1
                ins.then_inc(dve_seq, 1)
                dve.wait_ge(dve_seq, seq[0])

            def begin():
                seq[0] = 0
                dve.sem_clear(dve_seq)

            def split23(dst, f, rest, last_sem, before):
                wait(dve, last_sem, before)
                link(V.tensor_tensor(rest, f, dst[0], ALU.subtract))
                link(V.tensor_copy(dst[1], rest))
                V.tensor_tensor(dst[2], rest, dst[1], ALU.subtract).then_inc(last_sem, 1)

            bk, n = turns.at(("pro", 0), ("W",), 8)
            dve.wait_ge(work_full[bk], n + 1)
            by_col = work[bk][:, 0:4 * C].rearrange("p (l m) -> p l m", l=2)
            V.tensor_scalar(bias[:, :, 0:C], by_col[:, :, 0:C], 0.25, None, ALU.mult)
            V.tensor_copy(bias[:, :, C:2 * C], by_col[:, :, C:2 * C]).then_inc(work_free[bk], 1)
            dve.wait_ge(w_in, 16 * W_LOADS)

            def q_split(ph, seg, layer, n_before):
                for m in range(C):
                    emptied(dve, ph, seg, C + m)
                    split23([parts["q"][:, m, i, :] for i in range(3)], fq[layer][:, m, :], resq[:, :], split["q"],
                            n_before * C + m)

            def v_out(ph, seg, j0, layer, step):
                wait(dve, pv_full, (unit(step, layer, 1) - 4 + 1) * G)
                for n in range(2):
                    b, cnt = turns.at(ph, seg, j0 + n)
                    dve.wait_ge(work_full[b], cnt + 1)
                    v = vone[layer][:, 2 * n:2 * n + 2, :, 0:HD]
                    bvb = bv[layer][:, :].unsqueeze(1).broadcast_to([P, 2, D]).rearrange("p t (h d) -> p t h d", h=H)
                    src = work[b][:, :].rearrange("p (t h d) -> p t h d", t=2, h=H)
                    if layer == "s":
                        V.tensor_tensor(v, src, bvb, ALU.add).then_inc(work_free[b], 1)
                    else:
                        V.tensor_tensor(v, src, bvb, ALU.add).then_inc(work_free[b], 1)
                        emptied(dve, ph, seg, j0 + n)
                        V.tensor_scalar(v, v, 0.0, None, ALU.max).then_inc(v_ready, 1)

            def SF(ph, seg, step):
                q_split(ph, seg, "s", step * 2)
                v_out(ph, seg, 3 * C, "s", step)

            def CV(ph, seg, step):
                v_out(ph, seg, 0, "c", step)

            def CQ(ph, seg, step):
                q_split(ph, seg, "c", step * 2 + 1)

            def N(ph, seg, step, layer, b, g):
                U = unit(step, layer, b)
                for i in range(3):
                    job = 3 * g + i
                    bank = nat[job % 2]
                    dve.wait_ge(nat_full[job % 2], U * 6 + job // 2 + 1)
                    if i == 0:
                        dst, src = negm[:, 0, 4 * g:4 * g + 4], bank[:, :].rearrange("p (h k) -> p h k", h=4)
                    else:
                        w = mq1[layer].shape[2]
                        dst = negm[:, 1, 4 * g + 2 * i - 2:4 * g + 2 * i]
                        src = bank[:, 0:2 * w].rearrange("p (h k) -> p h k", h=2)
                    V.tensor_reduce(dst, src, AX, ALU.max, negate=True).then_inc(nat_free[job % 2], 1)
                if g == G - 1:
                    for n in range(2):
                        dve.wait_ge(nat_free[n], (U + 1) * 6)
                    wait(dve, m_stored, U * 16)
                    link(V.tensor_copy(mp[:, :, 0:H], negm[:, :, :]))
                    split23([mp[:, :, i * H:(i + 1) * H] for i in range(3)], negm[:, :, :], rm[:, :, :], mp_ready, U)

            def norm(number, dst_of, last):
                for t in range(QT):
                    i = V.bn_stats(stats[:, t, :], r[:, t, :])
                link(i)
                for t in range(QT):
                    i = V.bn_aggr(mv[:, t, :], stats[:, t, :])
                i.then_inc(var_ready, 1)
                dve.wait_ge(rstd_ready, number + 1)
                link(V.tensor_tensor(newton[:, :], rstd[:, :], rstd[:, :], ALU.mult))
                link(V.scalar_tensor_tensor(out=newton[:, :], in0=mv[:, :, 1], scalar=EPS, in1=newton[:, :], op0=ALU.add, op1=ALU.mult))
                link(V.tensor_scalar(newton[:, :], newton[:, :], -0.5, 1.5, ALU.mult, ALU.add))
                link(V.tensor_tensor(rstd[:, :], rstd[:, :], newton[:, :], ALU.mult))
                for t in range(QT):
                    i = V.tensor_scalar(dst_of(t), r[:, t, :], mv[:, t, 0:1], rstd[:, t:t + 1], ALU.subtract, ALU.mult)
                last(i)

            def Y1(ph, seg, step, layer, b):
                for t in range(QT):
                    bk, n = turns.at(ph, seg, t)
                    dve.wait_ge(work_full[bk], n + 1)
                    y = work[bk][:, :].rearrange("p (h d) -> p h d", h=H)
                    link(V.reciprocal(rec[:, t, :], y[:, :, HD]))
                    V.tensor_tensor(ynat[:, t, :].rearrange("p (h d) -> p h d", h=H), y[:, :, 0:HD],
                                        rec[:, t, :].unsqueeze(2).broadcast_to([P, H, HD]), ALU.mult).then_inc(work_free[bk], 1)
                emptied(dve, ph, seg, 0, 1)
                if layer == "s":
                    return
                bk, n = turns.at(ph, seg, QT)
                dve.wait_ge(work_full[bk], n + 1)
                V.scalar_tensor_tensor(out=r[:, :, :], in0=work[bk][:, :].rearrange("p (t d) -> p t d", t=QT), scalar=4.0,
                                       in1=ynat[:, :, :], op0=ALU.mult, op1=ALU.add).then_inc(work_free[bk], 1)
                emptied(dve, ph, seg, QT)
                norm(norms_before(step, layer, b), lambda t: r[:, t, :], link)
                link(V.tensor_tensor(r[:, :, :], r[:, :, :], gamma[:, :].unsqueeze(1).broadcast_to([P, QT, D]), ALU.mult))
                link(V.tensor_tensor(r[:, :, :], r[:, :, :], beta[:, :].unsqueeze(1).broadcast_to([P, QT, D]), ALU.add))
                link(V.tensor_tensor(r[:, :, :], r[:, :, :], x1[:, b * QT:(b + 1) * QT, :], ALU.add))
                dve.wait_ge(x2_free, step * STEP_B + b + 1)
                norm(norms_before(step, layer, b) + 1, lambda t: x2[:, t, :], lambda i: i.then_inc(x2_ready, 1))

            def Y3(ph, seg, step, layer, b):
                bk, n = turns.at(ph, seg, 0)
                dve.wait_ge(work_full[bk], n + 1)
                dve.wait_ge(xb_ready, step + 1)
                V.tensor_tensor(r[:, :, :], work[bk][:, :].rearrange("p (t d) -> p t d", t=QT), xb[:, b * QT:(b + 1) * QT, :],
                                ALU.add).then_inc(work_free[bk], 1)
                emptied(dve, ph, seg, 0)
                norm(norms_before(step, layer, b), lambda t: x1[:, b * QT + t, :], lambda i: i.then_inc(x1_ready, 1))

            def R(ph, seg, step, layer, b):
                bk, n = turns.at(ph, seg, 1)
                dve.wait_ge(work_full[bk], n + 1)
                V.tensor_copy(logits[:, bass.ds((step * STEP_B + b) * QT, QT), :],
                              work[bk][:, 0:QT * 8].rearrange("p (t e) -> p t e", t=QT)).then_inc(work_free[bk], 1)

            walk({"begin": begin, "SF": SF, "CV": CV, "CQ": CQ, "N": N, "Y1": Y1, "Y3": Y3, "R": R}, dve.Fori)

            emptied(dve, ("epi", 0), ("R", "c", 1), 1)
            for t in range(NT):
                i = V.max(top[:, t, :], logits[:, t, :])
            link(i)
            V.tensor_tensor(diff[:, :, :], top[:, :, :], top[:, :, 0:1].broadcast_to([P, NT, 8]), ALU.subtract).then_inc(diff_ready, 1)
            for t in range(NT):
                i = V.max_index(topi[:, t, :], top[:, t, :], logits[:, t, :])
            link(i)
            link(V.tensor_copy(idxf[:, :, :], topi[:, :, 0:TOPK]))
            dve.wait_ge(consts, 2)
            by_choice = choice[:, :].rearrange("p (g e k t) -> p g t e k", g=GROUPS, e=E, k=TOPK)
            for g in range(GROUPS):
                for k in range(TOPK):
                    i = V.tensor_tensor(by_choice[:, g, :, :, k], iota_e[:, :].unsqueeze(1).broadcast_to([P, GT, E]),
                                        idxf[:, g * GT:(g + 1) * GT, k].unsqueeze(2).broadcast_to([P, GT, E]), ALU.is_equal)
            i.then_inc(choice_ready, 1)
            dve.wait_ge(expd_ready, 1)
            link(V.tensor_reduce(esum[:, :], expd[:, :, :], AX, ALU.add))
            link(V.reciprocal(esum[:, :], esum[:, :]))
            V.tensor_tensor(gates[:, :, :], expd[:, :, 0:TOPK], esum[:, :].unsqueeze(2).broadcast_to([P, NT, TOPK]), ALU.mult)
            dve.wait_ge(counted, 1)
            link(V.tensor_tensor_scan(before[:, :], goes_on[:, :], spare[:, NM:2 * NM], 0.0, ALU.mult, ALU.add))
            link(V.tensor_tensor(before[:, :], before[:, :], spare[:, NM:2 * NM], ALU.subtract))
            link(V.tensor_tensor(before[:, :], before[:, :], spare[:, 0:NM], ALU.add))
            link(V.tensor_tensor(before[:, :], before[:, :], choice[:, :], ALU.mult))
            for g in range(GROUPS):
                i = V.tensor_reduce(pos[:, g, :], before[:, g * (NM // GROUPS):(g + 1) * (NM // GROUPS)].rearrange(
                    "p (e kt) -> p kt e", e=E), AX, ALU.add)
            for g in range(GROUPS):
                for k in range(TOPK):
                    i = V.scalar_tensor_tensor(out=slot[:, g, k * GT:(k + 1) * GT], in0=idxf[:, g * GT:(g + 1) * GT, k],
                                               scalar=float(SLOTS), in1=gbase[:, g, k * GT:(k + 1) * GT], op0=ALU.mult, op1=ALU.add)
            link(i)
            V.tensor_scalar(late[:, :, :], pos[:, :, :], float(CAP), BAD, ALU.is_gt, ALU.mult)
            link(V.tensor_tensor(slot[:, :, :], slot[:, :, :], pos[:, :, :], ALU.add))
            link(V.tensor_tensor(slot[:, :, :], slot[:, :, :], late[:, :, :], ALU.add))
            flat = slot[:, :, :].rearrange("p g n -> p (g n)")
            V.tensor_copy(put[:, :], flat)
            link(V.tensor_scalar(flat, flat, float(E * SLOTS), None, ALU.min))
            V.tensor_copy(get[:, :], flat).then_inc(routed, 1)

            def ex_take(job, it, emit):
                b, n = expert_turn(job, it)
                dve.wait_ge(ex_full[b], n + 1)
                emit(banks8[b]).then_inc(ex_free[b], 1)

            def pair(it, last):
                for i in range(2):
                    for f in range(1, FC, 2):
                        ex_take(("h", i, f), it, lambda bank: V.tensor_scalar(hT[i][:, f, :], bank[:, 0:SLOTS], 0.0, None, ALU.max))
                    wait(dve, y_stored[i], it * 48)
                    ex_take(("y", i, 0), it, lambda bank: V.tensor_copy(ye[i][:, 0:D], bank[:, 0:D]))
                    ex_take(("y", i, FULL), it, lambda bank: V.tensor_copy(ye[i][:, FULL * D:YE], bank[:, 0:P]))

            experts(dve, pair)

            for n in range(NT // QT):
                dve.wait_ge(got_sem[n], QT * TOPK * 16)
                wait(dve, out_ready, n)
                for k in range(TOPK):
                    for t in range(QT):
                        tile = n * QT + t
                        i = V.scalar_tensor_tensor(out=r[:, t, :], in0=got[:, tile * TOPK + k, :], scalar=gates[:, tile, k:k + 1],
                                                   in1=xres[:, tile, :] if k == 0 else r[:, t, :], op0=ALU.mult, op1=ALU.add)
                    link(i)
                wait(dve, out_stored[n % 2], n // 2 * 16)
                norm(6 * STEPS + n, lambda t: xin[:, (n % 2) * QT + t, :], lambda i: i.then_inc(out_ready, 1))

        @block.gpsimd
        def _(pool):
            g_ = nc.gpsimd
            seq = [0]

            def link(ins):
                seq[0] += 1
                ins.then_inc(pool_seq, 1)
                pool.wait_ge(pool_seq, seq[0])

            def begin():
                seq[0] = 0
                pool.sem_clear(pool_seq)

            g_.memset(ident[:, :], 0.0)
            link(g_.memset(identb[:, :], 0.0))
            g_.affine_select(out=identb[:, :], in_=identb[:, :], compare_op=ALU.not_equal, fill=1.0, base=0,
                             pattern=[[-1, P]], channel_multiplier=1)
            g_.affine_select(out=ident[:, :], in_=ident[:, :], compare_op=ALU.not_equal, fill=1.0, base=0,
                             pattern=[[-1, P]], channel_multiplier=1).then_inc(consts, 1)
            g_.memset(eps[:, :], EPS).then_inc(x2_free, 1)
            g_.memset(mp[:, :, :], 0.0)
            for layer in "sc":
                g_.memset(vone[layer][:, :, :, :], 1.0)
            masks = [mq0["s"], mq0["c"], mq1["s"], mq1["c"], mk0["s"], mk0["c"], mk1["s"], mk1["c"]]
            for m in masks:
                last = g_.memset(m[:, :, :], 0.0)
            link(last)

            def keep(m, base, cm, step):
                return g_.affine_select(out=m[:, :, :], in_=m[:, :, :], compare_op=ALU.is_ge, fill=NEG, base=base,
                                        pattern=[[0, m.shape[1]], [step, m.shape[2]]], channel_multiplier=cm)
            keep(mq0["s"], 0, 1, -1)
            keep(mq0["c"], 0, 1, -1)
            keep(mq1["s"], P - WIN, 1, -1)
            keep(mq1["c"], P, 1, -1)
            keep(mk0["s"], 0, -1, 1)
            keep(mk0["c"], 0, -1, 1)
            keep(mk1["s"], 0, -1, 1)
            link(keep(mk1["c"], 0, -1, 1))
            keep(mq0["s"], WIN - 1, -1, 1)
            keep(mq1["s"], -1, -1, 1)
            keep(mk0["s"], WIN - 1, 1, -1)
            link(keep(mk1["s"], WIN - 1, 1, -1))
            g_.memset(zeros[:, :], 0.0)
            g_.memset(onesb[:, :], 1.0)
            g_.memset(tri[:, :], 1.0)
            g_.memset(goes_on[:, :], 1.0)
            for g in range(GROUPS):
                g_.memset(gbase[:, g, :], float(g * CAP - 1))
            link(g_.iota(iota_e[:, :], [[1, E]], base=0, channel_multiplier=0, allow_small_or_imprecise_dtypes=True))
            g_.memset(goes_on[:, :].rearrange("p (a b) -> p a b", b=TOPK * GT)[:, :, 0:1], 0.0).then_inc(zeros_ready, 1)
            pool.wait_ge(zeros_ready, 1)
            g_.affine_select(out=tri[:, :], in_=tri[:, :], compare_op=ALU.is_ge, fill=0.0, base=0,
                             pattern=[[1, P]], channel_multiplier=-1).then_inc(consts, 1)
            pool.wait_ge(consts, 2)

            def k_split(ph, seg, j0, n_before):
                for m in range(C):
                    emptied(pool, ph, seg, j0 + m)
                    p = [parts["k"][:, m, i, :] for i in range(3)]
                    wait(pool, split["k"], n_before * C + m)
                    link(g_.tensor_tensor(resk[:, :], fk[:, m, :], p[0], ALU.subtract))
                    link(g_.tensor_copy(p[1], resk[:, :]))
                    g_.tensor_tensor(p[2], resk[:, :], p[1], ALU.subtract).then_inc(split["k"], 1)

            def SF(ph, seg, step):
                if isinstance(step, int):
                    pool.wait_ge(x_in, 16 * STEPS)
                else:
                    g_.tensor_copy(xin[:, :, :], xres[:, bass.ds(step * TT, TT), :]).then_inc(xin_ready, 1)
                    pool.wait_ge(xin_ready, step)
                    pool.wait_ge(x1_ready, step * STEP_B)
                if isinstance(step, int):
                    pool.wait_ge(w_in, 16 * W_LOADS)
                g_.tensor_tensor(xb[:, :, :], xin[:, :, :], bo[:, :].unsqueeze(1).broadcast_to([P, TT, D]), ALU.add)\
                    .then_inc(xb_ready, 1)
                k_split(ph, seg, 2 * C, step * 2)
                if isinstance(step, int):
                    emptied(pool, ph, ("W",), 6, 7)
                    pool.wait_ge(split["k"], C)
                    link(g_.memset(stack["sk"][KR:KR + MR, :, :], 1.0))
                    g_.memset(stack["ck"][KR:KR + MR, :, :], 1.0).then_inc(ones_ready, 1)
                    pool.wait_ge(ones_ready, 1)

            def CQ(ph, seg, step):
                k_split(ph, ("CK",), C, step * 2 + 1)

            def R(ph, seg, step, layer, b):
                n = step * STEP_B + b
                pool.wait_ge(x2_ready, n + 1)
                g_.tensor_copy(xres[:, bass.ds(n * QT, QT), :], x2[:, :, :]).then_inc(x2_free, 1)

            walk({"begin": begin, "SF": SF, "CQ": CQ, "R": R}, pool.Fori)

            pool.wait_ge(routed, 1)
            pool.wait_ge(cleared, 32)
            pool.wait_ge(x2_free, B + 1)
            for tile in range(NT):
                for k in range(TOPK):
                    col = (tile // GT) * (TOPK * GT) + k * GT + tile % GT
                    pool.indirect_dma_start(out=x_dram, out_offset=bass.IndirectOffsetOnAxis(ap=put[:, col:col + 1], axis=0),
                                            in_=xres[:, tile, :], in_offset=None, bounds_check=E * SLOTS - 1, oob_is_err=False)\
                        .then_inc(put_done, 16)
            for i in range(2):
                pool.wait_ge(y_stored[i], (E // 2) * 48)
            for tile in range(NT):
                for k in range(TOPK):
                    col = (tile // GT) * (TOPK * GT) + k * GT + tile % GT
                    pool.indirect_dma_start(out=got[:, tile * TOPK + k, :], out_offset=None, in_=y_dram,
                                            in_offset=bass.IndirectOffsetOnAxis(ap=get[:, col:col + 1], axis=0))\
                        .then_inc(got_sem[tile // QT], 16)


_INS = ["x", "ctx_1024", "L0_attn_Wqkv", "L0_attn_bqkv", "L0_attn_Wo", "L0_attn_bo", "L0_xattn_Wq", "L0_xattn_bq",
        "L0_xattn_Wk", "L0_xattn_bk", "L0_xattn_Wv", "L0_xattn_bv", "L0_xattn_gamma", "L0_xattn_beta",
        "L0_ffn_w_router", "L0_ffn_wi", "L0_ffn_wo"]


def kernel(**inputs):
    import numpy as np
    import concourse.bacc as bacc
    from concourse.bass_utils import run_bass_kernel_spmd

    nc = bacc.Bacc("TRN2", target_bir_lowering=False, num_devices=1)
    arrays, a = {}, {}
    for name in _INS:
        array = np.ascontiguousarray(inputs[name])
        arrays[f"in_{name}"] = array
        a[name] = nc.dram_tensor(f"in_{name}", array.shape, mybir.dt.from_np(array.dtype), kind="ExternalInput").ap()
    out = nc.dram_tensor("out", [B, T, D], F32, kind="ExternalOutput").ap()
    attention_and_experts(nc, a, out)
    r = run_bass_kernel_spmd(nc, [arrays], core_ids=[0])
    return r.results[0]["out"]
```

```python
from contextlib import ExitStack

import concourse.bass as bass
from concourse import mybir

F32 = mybir.dt.float32
BF16 = mybir.dt.bfloat16
U32 = mybir.dt.uint32
ALU = mybir.AluOpType
ACT = mybir.ActivationFunctionType
AX = mybir.AxisListType.X

P = 128
B, T, D = 8, 256, 256
H, HD, WIN = 16, 16, 64
C = D // P
STEP_B = 2
ST = STEP_B * T
STEPS = B // STEP_B
TT = ST // P
QT = T // P
NT = B * QT
G = H // 4
Q_SLOTS = (0, 1, 0, 1, 2, 0)
K_SLOTS = (0, 0, 1, 1, 0, 2)
KR = 6 * HD
MR = 3
KEYS0 = {"s": 192, "c": 256}
E, TOPK, CAP, F = 8, 2, 160, 1024
GROUPS = 2
GT = NT // GROUPS
SLOTS = GROUPS * CAP
FC = F // P
FULL = SLOTS // P
REST = SLOTS - FULL * P
BAD = 4096.0
NEG = -3.0e38
EPS = 1e-5

BODY = (
    [("XI",), ("T", "s", 0, 3), ("T", "s", 1, 0), ("Y1", "s", 0), ("T", "s", 1, 1), ("Y2", "s", 0), ("T", "s", 1, 2), ("Y3", "s", 0)]
    + [("SX",), ("T", "s", 1, 3), ("L3", "s", 0), ("SQ",), ("CX", "c", 0), ("Y1", "s", 1), ("CQ", "c", 0), ("SK",), ("CS", "c", 0)]
    + [("Y2", "s", 1), ("SV",), ("Y3", "s", 1), ("SS",), ("L3", "s", 1), ("CX", "c", 1), ("N", "c", 0, 0), ("CQ", "c", 1)]
    + [("N", "c", 0, 1), ("CS", "c", 1), ("XB",), ("N", "c", 0, 2), ("KX",), ("N", "c", 0, 3), ("CK",), ("N", "c", 1, 0)]
    + [("M", "c", 0), ("N", "c", 1, 1), ("N", "c", 1, 2), ("T", "c", 0, 0), ("N", "c", 1, 3), ("T", "c", 0, 1), ("N", "s", 0, 0)]
    + [("M", "c", 1), ("T", "c", 0, 2), ("N", "s", 0, 1), ("T", "c", 0, 3), ("T", "c", 1, 0), ("Y1", "c", 0), ("T", "c", 1, 1)]
    + [("N", "s", 0, 2), ("L1", "c", 0), ("T", "c", 1, 2), ("N", "s", 0, 3), ("T", "c", 1, 3), ("L2", "c", 0), ("M", "s", 0)]
    + [("KL",), ("CV",), ("N", "s", 1, 0), ("Y1", "c", 1), ("RX", "c", 0), ("N", "s", 1, 1), ("L1", "c", 1), ("R", "c", 0)]
    + [("T", "s", 0, 0), ("N", "s", 1, 2), ("L2", "c", 1), ("N", "s", 1, 3), ("T", "s", 0, 1), ("RX", "c", 1), ("M", "s", 1)]
    + [("T", "s", 0, 2), ("R", "c", 1)]
)


def for_next(seg):
    return seg[0] in ("XI", "SX", "SQ", "SK", "SV", "SS", "XB", "KX", "CK", "KL", "CV") or seg[0:2] in (("N", "s"), ("M", "s")) or \
        seg in (("T", "s", 0, 0), ("T", "s", 0, 1), ("T", "s", 0, 2))


PROLOGUE = (
    [("SX",), ("SQ",), ("SK",), ("SS",), ("SV",), ("XB",), ("KX",), ("CK",), ("KL",)] + [("N", "s", 0, g) for g in range(G)]
    + [("CV",), ("M", "s", 0), ("N", "s", 1, 0), ("N", "s", 1, 1), ("T", "s", 0, 0), ("N", "s", 1, 2), ("N", "s", 1, 3)]
    + [("T", "s", 0, 1), ("M", "s", 1), ("T", "s", 0, 2)]
)
LOOP = BODY
EPILOGUE = [seg for seg in BODY if not for_next(seg)]

WORK_JOBS = {"SX": 2, "SQ": 2, "SK": 2, "SV": 2, "KX": 2, "CK": 2, "CV": 2, "CX": 1, "CQ": 1, "M": 1, "Y1s": 2, "Y1c": 3, "Y2": 1, "Y3": 1, "RX": 1, "R": 1, "W": 9}
WB = 2
W_LOADS = 10


def jobs_of(seg):
    return WORK_JOBS[seg[0] + seg[1] if seg[0] == "Y1" else seg[0]]


XB = 6
PAIR_JOBS = [(kind, i, n) for i in range(2) for kind, count in (("h", FC), ("y", FULL + 1)) for n in range(count)]
PER_BANK = [len(PAIR_JOBS[b::XB]) for b in range(XB)]


def expert_turn(job, it):
    kind, i, n = job
    if kind == "x":
        return XB + n, it * 2 + i
    n = PAIR_JOBS.index(job)
    return n % XB, it * PER_BANK[n % XB] + n // XB


class WorkTurns:

    def __init__(self):
        self.local = {}
        self.total = {}
        for name, plan in (("pro", [("W",)] + PROLOGUE), ("loop", LOOP), ("epi", EPILOGUE)):
            n, count = 0, [0] * WB
            for seg in plan:
                if seg[0] not in WORK_JOBS and seg[0] != "Y1":
                    continue
                for j in range(jobs_of(seg)):
                    b = n % WB
                    self.local[(name, seg, j)] = (b, count[b])
                    count[b] += 1
                    n += 1
            self.total[name] = count

    def at(self, phase, seg, j):
        name, it = phase
        b, n = self.local[(name, seg, j)]
        if name == "loop":
            return b, it * self.total["loop"][b] + self.total["pro"][b] + n
        if name == "epi":
            return b, (STEPS - 1) * self.total["loop"][b] + self.total["pro"][b] + n
        return b, n


def wait(eng, sem, value):
    if not isinstance(value, int) or value > 0:
        eng.wait_ge(sem, value)


def attention_and_experts(nc: bass.Bass, a, out):
    turns = WorkTurns()
    with ExitStack() as ctx:
        def sb(name, shape, dt=F32):
            return ctx.enter_context(nc.sbuf_tensor(name, shape, dt))

        def sem(name):
            return ctx.enter_context(nc.semaphore(name))

        work = [ctx.enter_context(nc.psum_tensor(f"work{i}", [P, 512], F32)) for i in range(WB)]
        nat = [ctx.enter_context(nc.psum_tensor(f"nat{i}", [P, 512], F32)) for i in range(2)]
        byk = [ctx.enter_context(nc.psum_tensor(f"byk{i}", [P, 512], F32)) for i in range(3)]
        pv = ctx.enter_context(nc.psum_tensor("pv", [P, 512], F32))

        ident = sb("ident", [P, P])
        identb = sb("identb", [P, P], BF16)
        mq0 = {"s": sb("mq0s", [P, 4, P], BF16), "c": sb("mq0c", [P, 4, P], BF16)}
        mq1 = {"s": sb("mq1s", [P, 2, 192], BF16), "c": sb("mq1c", [P, 2, P], BF16)}
        mk0 = {"s": sb("mk0s", [P, 2, 192], BF16), "c": sb("mk0c", [P, 2, P], BF16)}
        mk1 = {"s": sb("mk1s", [P, 4, P], BF16), "c": sb("mk1c", [P, 4, P], BF16)}
        wqkvT = sb("wqkvT", [P, C, 3 * D])
        woT = sb("woT", [P, C, D])
        wc = {n: sb(f"w{n}_c", [P, C, D]) for n in "qkv"}
        bias_rows = sb("bias_rows", [4 * C, P])
        bias = sb("bias", [P, 2, 2 * C])
        bv = {"s": sb("bv_s", [P, D]), "c": sb("bv_c", [P, D])}
        bo = sb("bo", [P, D])
        gamma = sb("gamma", [P, D])
        beta = sb("beta", [P, D])
        wr = sb("wr", [P, C, 8])
        xres = sb("xres", [P, NT, D])
        xin = sb("xin", [P, TT, D])
        ctxin = sb("ctxin", [P, TT, D])
        xb = sb("xb", [P, TT, D])
        xT = sb("xT", [P, C, ST])
        fq = {"s": sb("fq_s", [P, C, ST]), "c": sb("fq_c", [P, C, ST])}
        fk = sb("fk", [P, C, ST])
        resq = sb("resq", [P, ST])
        resk = sb("resk", [P, ST])
        parts = {k: sb(f"parts_{k}", [P, C, 3, ST], BF16) for k in ("sq", "cq", "k")}
        parts["sk"] = parts["ck"] = parts["k"]
        arena = sb("arena", [P, 4 * H * ST // 2])
        ARENA_U = H * ST // 2
        stack = {}
        for i, key in enumerate(("sq", "sk", "cq", "ck")):
            stack[key] = arena[:, i * ARENA_U:(i + 1) * ARENA_U].bitcast(BF16).rearrange("p (h t) -> p h t", h=H)
        vone = {"s": sb("v_s", [P, TT, H, 32]), "c": sb("v_c", [P, TT, H, 32])}
        negm = sb("negm", [P, QT, H])
        rm = sb("rm", [P, QT, H])
        mp = sb("mp", [P, QT, P], BF16)
        mT = sb("mT", [MR * H, T], BF16)
        probs = sb("probs", [P, 2, 4, 384])
        yT = sb("yT", [P, G, T])
        rec = sb("rec", [P, QT, H])
        ynat = sb("ynat", [P, QT, D])
        turned = sb("turned", [P, C, T])
        r = sb("r", [P, QT, D])
        stats = sb("stats", [P, QT, 6])
        mv = sb("mv", [P, QT, 2])
        rstd = sb("rstd", [P, QT])
        lnv = sb("lnv", [P, QT])
        newton = sb("newton", [P, QT])
        eps = sb("eps", [P, 1])
        x1 = sb("x1", [P, TT, D])
        x2 = sb("x2", [P, QT, D])
        logits = sb("logits", [P, NT, E])
        iota_e = sb("iota_e", [P, E])
        tri = sb("tri", [P, P], BF16)
        onesb = sb("onesb", [P, P], BF16)
        NM = GROUPS * E * TOPK * GT
        goes_on = sb("goes_on", [P, NM])
        gbase = sb("gbase", [P, GROUPS, TOPK * GT])
        top, topi, diff, expd = (fk[:, 0, i * NT * 8:(i + 1) * NT * 8].rearrange("p (t e) -> p t e", e=8) for i in range(4))
        topi = topi.bitcast(U32)
        esum = sb("esum", [P, NT])
        gates = sb("gates", [P, NT, TOPK])
        idxf = sb("idxf", [P, NT, TOPK])
        choice = sb("choice", [P, NM], BF16)
        before = fk[:, 1, 0:NM]
        pos = sb("pos", [P, GROUPS, TOPK * GT])
        slot = sb("slot", [P, GROUPS, TOPK * GT])
        late = sb("late", [P, GROUPS, TOPK * GT])
        put = sb("put", [P, GROUPS * TOPK * GT], U32)
        get = sb("get", [P, GROUPS * TOPK * GT], U32)
        WI, WO, HT_, XE, XET = C * F, FC * D, FC * SLOTS, (FULL + 1) * D, C * SLOTS
        at = 0
        wi, wo, hT, xe, xeT = [], [], [], [], []
        for group, size, lead in ((wi, WI, C), (wo, WO, FC), (hT, HT_, FC), (xe, XE, FULL + 1), (xeT, XET, C)):
            for i in range(2):
                group.append(arena[:, at:at + size].rearrange("p (c n) -> p c n", c=lead))
                at += size
        assert at <= 4 * ARENA_U
        YE = FULL * D + P
        ye = [xb[:, :, :].rearrange("p a b -> p (a b)")[:, 0:YE], ctxin[:, :, :].rearrange("p a b -> p (a b)")[:, 0:YE]]
        got = arena[:, 0:NT * TOPK * D].rearrange("p (n d) -> p n d", d=D)
        zeros = sb("zeros", [P, D // 2])

        part_dram = {k: nc.dram_tensor(f"part_{k}", [D, 3, ST], BF16).ap() for k in ("sq", "sk", "cq", "ck")}
        m_dram = nc.dram_tensor("m_rows", [MR, H, T], BF16).ap()

        x_dram = nc.dram_tensor("expert_x", [E * SLOTS, D], F32).ap()
        y_dram = nc.dram_tensor("expert_y", [E * SLOTS + 1, D], F32).ap()

        cleared = sem("cleared"); zeros_ready = sem("zeros_ready"); routed = sem("routed")
        diff_ready = sem("diff_ready"); expd_ready = sem("expd_ready"); choice_ready = sem("choice_ready")
        counted = sem("counted"); put_done = sem("put_done"); got_sem = [sem(f"got{i}") for i in range(NT // QT)]
        wi_in = [sem(f"wi_in{i}") for i in range(2)]; wo_in = [sem(f"wo_in{i}") for i in range(2)]
        xe_in = [sem(f"xe_in{i}") for i in range(2)]
        ex_full = [sem(f"ex_full{i}") for i in range(XB + C)]
        ex_free = [sem(f"ex_free{i}") for i in range(XB + C)]
        y_stored = [sem(f"y_stored{i}") for i in range(2)]
        out_ready = sem("out_ready"); out_stored = [sem(f"out_stored{i}") for i in range(2)]
        w_in = sem("w_in"); w_in2 = sem("w_in2"); x_in = sem("x_in"); ctx_in = sem("ctx_in")
        consts = sem("consts"); ones_ready = sem("ones_ready");
        work_full = [sem(f"work_full{i}") for i in range(WB)]
        work_free = [sem(f"work_free{i}") for i in range(WB)]
        nat_full = [sem(f"nat_full{i}") for i in range(2)]
        nat_free = [sem(f"nat_free{i}") for i in range(2)]
        byk_full = [sem(f"byk_full{i}") for i in range(3)]
        pv_full = sem("pv_full")
        yT_ready = sem("yT_ready")
        xin_ready = sem("xin_ready"); xb_ready = sem("xb_ready")
        split = {"q": sem("split_q"), "k": sem("split_k")}
        stored = {k: sem(f"stored_{k}") for k in ("sq", "cq", "k")}
        stored["sk"] = stored["ck"] = stored["k"]
        stacked = {k: sem(f"stacked_{k}") for k in ("sq", "sk", "cq", "ck")}
        v_ready = sem("v_ready")
        mp_ready = sem("mp_ready")
        m_stored = sem("m_stored"); m_rows = sem("m_rows")
        exp_ready = sem("exp_ready")
        x1_ready = sem("x1_ready"); x1b_ready = sem("x1b_ready"); x2_ready = sem("x2_ready")
        x2_free = sem("x2_free")
        var_ready = sem("var_ready"); rstd_ready = sem("rstd_ready"); lnv_ready = sem("lnv_ready")
        dve_seq = sem("dve_seq"); pool_seq = sem("pool_seq")
        done = sem("done")

        def unit(step, layer, b):
            return step * 4 + (b if layer == "s" else 2 + b)

        EXP0, PV0, YT0 = 3, 2, 1

        def q_splits(step, layer, b=0):
            if layer == "s":
                return 0 if isinstance(step, int) else (step * 3 - 1) * C
            return (step * 3 + 1 + (b if isinstance(step, int) else 2 * b)) * C

        def k_splits(step, layer):
            return (step * 2 + (0 if layer == "s" else 1)) * C

        def norms_before(step, layer, b):
            return step * 6 + (b if layer == "s" else 2 + 2 * b)

        def walk(handlers, fori):
            def run(plan, phase, step, following):
                for seg in plan:
                    f = handlers.get(seg[0])
                    if f is not None:
                        f(phase, seg, following if for_next(seg) else step, *seg[1:])
            run(PROLOGUE, ("pro", 0), None, 0)
            with fori(0, STEPS - 1) as it:
                if "begin" in handlers:
                    handlers["begin"]()
                run(LOOP, ("loop", it), it, it + 1)
            if "begin" in handlers:
                handlers["begin"]()
            run(EPILOGUE, ("epi", 0), STEPS - 1, None)

        def emptied(eng, phase, seg, *jobs):
            for j in jobs:
                b, n = turns.at(phase, seg, j)
                eng.wait_ge(work_free[b], n + 1)

        banks8 = [*work, *nat, *byk, pv]

        def experts(eng, pair):
            pair(0, False)
            with eng.Fori(1, E // 2 - 1) as it:
                pair(it, False)
            pair(E // 2 - 1, True)

        def ex_result(eng, job, it):
            b, n = expert_turn(job, it)
            eng.wait_ge(ex_free[b], n + 1)

        block = ctx.enter_context(nc.Block())

        @block.sync
        def _(sp):
            x_v = a["x"].rearrange("b (t p) d -> p (b t) d", p=P)
            sp.dma_start(xin[:, :, :], x_v[:, 0:TT, :]).then_inc(x_in, 16)
            wload = arena[:, 0:6 * D].rearrange("p (m d) -> p m d", m=6)
            sp.dma_start(wload, a["L0_attn_Wqkv"].rearrange("(m p) d -> p m d", p=P)).then_inc(w_in, 16)
            sp.dma_start(arena[:, 6 * D:8 * D].rearrange("p (m d) -> p m d", m=2),
                         a["L0_attn_Wo"].rearrange("(m p) d -> p m d", p=P)).then_inc(w_in, 16)
            sp.dma_start(bias_rows[0:2 * C, :], a["L0_attn_bqkv"][0:2 * D].rearrange("(m p) -> m p", p=P)).then_inc(w_in, 16)
            for n, b_in in enumerate("qk"):
                sp.dma_start(bias_rows[(2 + n) * C:(3 + n) * C, :], a[f"L0_xattn_b{b_in}"].rearrange("(m p) -> m p", p=P))\
                    .then_inc(w_in, 16)
            for dst, src in ((bv["s"], a["L0_attn_bqkv"][2 * D:3 * D]), (bv["c"], a["L0_xattn_bv"]), (bo, a["L0_attn_bo"]),
                             (gamma, a["L0_xattn_gamma"]), (beta, a["L0_xattn_beta"])):
                sp.dma_start(dst[:, :], src.partition_broadcast(P)).then_inc(w_in, 16)
            for i in range(1, STEPS):
                sp.dma_start(xres[:, i * TT:(i + 1) * TT, :], x_v[:, i * TT:(i + 1) * TT, :]).then_inc(x_in, 16)
            for n in "qkv":
                sp.dma_start(wc[n][:, :, :], a[f"L0_xattn_W{n}"].rearrange("(c p) n -> p c n", p=P)).then_inc(w_in2, 16)
            sp.dma_start(wr[:, :, :], a["L0_ffn_w_router"].rearrange("(c p) e -> p c e", p=P)).then_inc(w_in2, 16)
            sp.wait_ge(zeros_ready, 1)
            sp.dma_start(x_dram.rearrange("(p n) (a d) -> p (n a) d", p=P, a=2),
                         zeros[:, :].unsqueeze(1).broadcast_to([P, E * SLOTS // P * 2, D // 2])).then_inc(cleared, 16)
            sp.dma_start(y_dram[E * SLOTS:E * SLOTS + 1, :].rearrange("o (a d) -> o a d", a=2),
                         zeros[0:1, :].unsqueeze(1).broadcast_to([1, 2, D // 2])).then_inc(cleared, 16)
            ctx_v = a["ctx_1024"].rearrange("b (t p) d -> p (b t) d", p=P)
            part_v = {k: v.rearrange("(h r) s t -> r s h t", r=HD) for k, v in part_dram.items()}

            def held(*values):
                for v in values:
                    if v is not None and not isinstance(v, int):
                        sp.compute_val(v)
                return values

            def stack_side(layer, side, step, n_split, n_loads, tokens, free):
                key = layer + side
                *is_split, is_stored, is_free = held(*(n_split + c + 1 for c in range(C)), (n_loads + 1) * (C * 16), free)
                t0, t1 = tokens
                if is_free is not None:
                    sp.wait_ge(pv_full, is_free)
                for c in range(C):
                    sp.wait_ge(split[side], is_split[c])
                    sp.dma_start(part_dram[key][c * P:(c + 1) * P, :, t0:t1], parts[key][:, c, :, t0:t1]).then_inc(stored[key], 16)
                sp.wait_ge(stored[key], is_stored)
                slots = Q_SLOTS if side == "q" else K_SLOTS
                for i, part in enumerate(slots):
                    sp.dma_start(stack[key][i * HD:(i + 1) * HD, :, t0:t1], part_v[key][:, part, :, t0:t1])\
                        .then_inc(stacked[key], 16)

            def last_use(layer, step):
                if isinstance(step, int) and step == 0:
                    return None
                return PV0 + (unit(step, layer, 1) - 4 + 1) * G

            def SX(ph, seg, step):
                sp.dma_start(ctxin[:, :, :], ctx_v[:, bass.ds(step * TT, TT), :]).then_inc(ctx_in, 16)

            def SS(ph, seg, step):
                stack_side("s", "q", step, q_splits(step, "s"), step, (0, ST), last_use("s", step))

            def SK(ph, seg, step):
                if isinstance(step, int):
                    emptied(sp, ph, ("W",), 6, 7)
                stack_side("s", "k", step, k_splits(step, "s"), step * 2, (0, ST), last_use("s", step))

            def KL(ph, seg, step):
                stack_side("c", "k", step, k_splits(step, "c"), step * 2 + 1, (0, ST), last_use("c", step))

            def CS(ph, seg, step, layer, b):
                stack_side("c", "q", step, q_splits(step, "c", b), step * STEP_B + b, (b * T, (b + 1) * T),
                           PV0 + (unit(step, "s", 0) + 1) * G)

            def M(ph, seg, step, layer, b):
                were_loaded, are_stored = held(unit(step, layer, b) * 16, unit(step, layer, b) * 16 + 16)
                emptied(sp, ph, seg, 0)
                wait(sp, m_rows, were_loaded)
                sp.dma_start(m_dram.rearrange("m h t -> (m h) t"), mT[:, :]).then_inc(m_stored, 16)
                sp.wait_ge(m_stored, are_stored)
                sp.dma_start(stack[layer + "q"][KR:KR + MR, :, b * T:(b + 1) * T], m_dram).then_inc(m_rows, 16)

            walk({"SX": SX, "SS": SS, "SK": SK, "KL": KL, "CS": CS, "M": M}, sp.Fori)

            sp.wait_ge(pv_full, PV0 + 2 * B * G)
            wi_v = a["L0_ffn_wi"].rearrange("e (c p) f -> p e c f", p=P)
            wo_v = a["L0_ffn_wo"].rearrange("e (c p) d -> p e c d", p=P)

            def load_weights(e, i):
                sp.dma_start(wi[i], wi_v[:, bass.ds(e, 1), :, :].rearrange("p e c f -> p (e c) f")).then_inc(wi_in[i], 16)
                sp.dma_start(wo[i], wo_v[:, bass.ds(e, 1), :, :].rearrange("p e c f -> p (e c) f")).then_inc(wo_in[i], 16)

            def load_tokens(e, i):
                sp.dma_start(xe[i][:, 0:FULL, :], x_dram[bass.ds(e * SLOTS, FULL * P), :].rearrange("(t p) d -> p t d", p=P))\
                    .then_inc(xe_in[i], 16)
                sp.dma_start(xe[i][0:REST, FULL, :], x_dram[bass.ds(e * SLOTS + FULL * P, REST), :]).then_inc(xe_in[i], 16)

            for i in range(2):
                load_weights(i, i)
            sp.wait_ge(put_done, NT * TOPK * 16)
            for i in range(2):
                load_tokens(i, i)

            def pair(it, last):
                for i in range(2):
                    e = it * 2 + i
                    for n in range(FULL + 1):
                        ex_result(sp, ("y", i, n), it)
                    sp.dma_start(y_dram[bass.ds(e * SLOTS, FULL * P), :].rearrange("(t p) d -> p t d", p=P),
                                 ye[i][:, 0:FULL * D].rearrange("p (t d) -> p t d", t=FULL)).then_inc(y_stored[i], 16)
                    for n in range(2):
                        sp.dma_start(y_dram[bass.ds(e * SLOTS + FULL * P, REST), n * P:(n + 1) * P],
                                     ye[i][n * REST:(n + 1) * REST, FULL * D:YE]).then_inc(y_stored[i], 16)
                    if not last:
                        load_weights(e + 2, i)
                        load_tokens(e + 2, i)

            experts(sp, pair)
            out_v = out.rearrange("b (t p) d -> p (b t) d", p=P)
            for n in range(NT // QT):
                sp.wait_ge(out_ready, n + 1)
                sp.dma_start(out_v[:, n * QT:(n + 1) * QT, :], xin[:, (n % 2) * QT:(n % 2) * QT + QT, :]).then_inc(out_stored[n % 2], 16)
            for i in range(2):
                sp.wait_ge(out_stored[i], 16 * (NT // QT // 2))

        @block.tensor
        def _(pe):
            def work_job(phase, seg, j, emit):
                b, n = turns.at(phase, seg, j)
                wait(pe, work_free[b], n)
                emit(work[b]).then_inc(work_full[b], 1)

            def transposes(bank, srcs):
                for i, src in enumerate(srcs):
                    last = nc.tensor.transpose(bank[:, i * P:(i + 1) * P], src, ident[:, :])
                return last

            def by_feature(bank, w, m):
                for c in range(C):
                    last = nc.tensor.matmul(bank[:, :], w[:, c, m * P:(m + 1) * P], xT[:, c, :], start=(c == 0), stop=(c == C - 1))
                return last

            def by_token(bank, w, t0):
                for t in range(2):
                    for c in range(C):
                        last = nc.tensor.matmul(bank[:, t * D:(t + 1) * D], xT[:, c, (t0 + t) * P:(t0 + t + 1) * P], w[:, c, :],
                                                start=(c == 0), stop=(c == C - 1))
                return last

            def chunks_in(phase, seg, src):
                for c in range(C):
                    work_job(phase, seg, c, lambda bank: transposes(bank, [src[:, t, c * P:(c + 1) * P] for t in range(TT)]))

            pe.wait_ge(consts, 1)
            pe.wait_ge(w_in, 16 * W_LOADS)
            for m in range(8):
                work_job(("pro", 0), ("W",), m,
                         lambda bank: transposes(bank, [arena[:, m * D + c * P:m * D + (c + 1) * P] for c in range(C)]))

            work_job(("pro", 0), ("W",), 8, lambda bank: nc.tensor.transpose(bank[:, 0:4 * C], bias_rows[:, :], ident[0:4 * C, 0:4 * C]))

            def SX(ph, seg, step):
                if isinstance(step, int):
                    pe.wait_ge(x_in, 16)
                else:
                    pe.wait_ge(xin_ready, step)
                chunks_in(ph, seg, xin)

            def SQ(ph, seg, step):
                if isinstance(step, int):
                    emptied(pe, ph, ("W",), 6, 7)
                emptied(pe, ph, ("SX",), 0, 1)
                for m in range(C):
                    work_job(ph, seg, m, lambda bank: by_feature(bank, wqkvT, m))

            def SK(ph, seg, step):
                for m in range(C):
                    work_job(ph, seg, m, lambda bank: by_feature(bank, wqkvT, C + m))

            def SV(ph, seg, step):
                for n in range(2):
                    work_job(ph, seg, n, lambda bank: by_token(bank, wqkvT[:, :, 2 * D:3 * D], 2 * n))

            def KX(ph, seg, step):
                pe.wait_ge(ctx_in, (step + 1) * 16)
                chunks_in(ph, seg, ctxin)

            def CK(ph, seg, step):
                if isinstance(step, int):
                    pe.wait_ge(w_in2, 16 * 4)
                emptied(pe, ph, ("KX",), 0, 1)
                for m in range(C):
                    work_job(ph, seg, m, lambda bank: by_feature(bank, wc["k"], m))

            def CV(ph, seg, step):
                for n in range(2):
                    work_job(ph, seg, n, lambda bank: by_token(bank, wc["v"], 2 * n))

            def CX(ph, seg, step, layer, b):
                pe.wait_ge(x1_ready, step * STEP_B + b + 1)
                work_job(ph, seg, 0, lambda bank: transposes(
                    bank, [x1[:, b * QT + t, c * P:(c + 1) * P] for c in range(C) for t in range(QT)]))

            def CQ(ph, seg, step, layer, b):
                emptied(pe, ph, ("CX", "c", b), 0)

                def project(bank):
                    for m in range(C):
                        for c in range(C):
                            last = nc.tensor.matmul(bank[:, m * T:(m + 1) * T], wc["q"][:, c, m * P:(m + 1) * P], turned[:, c, :],
                                                    start=(c == 0), stop=(c == C - 1))
                    return last
                work_job(ph, seg, 0, project)

            def bank_scores(bank, full, mask, at, w, pairs):
                mw = mask.shape[2]
                nc.tensor.matmul(bank[:, 0:len(pairs) * w].rearrange("p (h t) -> p h t", t=w)[:, :, at:at + mw], identb[:, :],
                                 mask[:, :, :], start=True, stop=False, skip_group_check=True)
                for i, (lhsT, rhs) in enumerate(pairs):
                    last = nc.tensor.matmul(bank[:, i * w:(i + 1) * w], lhsT, rhs, start=False, stop=(i == len(pairs) - 1),
                                            skip_group_check=True)
                last.then_inc(full, 1)

            def N(ph, seg, step, layer, b, g):
                q, k = stack[layer + "q"], stack[layer + "k"]
                if g == 0 and layer == "c":
                    pe.wait_ge(stacked["cq"], (step * STEP_B + b + 1) * (6 * 16))
                if b == 0 and g == 0:
                    if layer == "s":
                        pe.wait_ge(stacked["sq"], (step + 1) * (6 * 16))
                    pe.wait_ge(stacked[layer + "k"], (step + 1) * (6 * 16))
                U = unit(step, layer, b)
                t0 = b * T
                n1 = KEYS0[layer]
                k1 = t0 + T - n1
                banks = [(mq0[layer], 0, range(4 * g, 4 * g + 4), t0, t0, P)]
                banks += [(mq1[layer], n1 - mq1[layer].shape[2], range(4 * g + 2 * n, 4 * g + 2 * n + 2), t0 + P, k1, n1) for n in range(2)]
                for i, (mask, at, heads, q0, k0, w) in enumerate(banks):
                    job = 3 * g + i
                    wait(pe, nat_free[job % 2], U * 6 + job // 2)
                    bank_scores(nat[job % 2], nat_full[job % 2], mask, at, w,
                                [(q[0:KR, h, q0:q0 + P], k[0:KR, h, k0:k0 + w]) for h in heads])

            def M(ph, seg, step, layer, b):
                pe.wait_ge(mp_ready, unit(step, layer, b) + 1)

                def rows(bank):
                    o = bank[:, :].bitcast(BF16)
                    for t in range(QT):
                        last = nc.tensor.transpose(o[:, t * P:(t + 1) * P], mp[:, t, :], identb[:, :])
                    return last
                work_job(ph, seg, 0, rows)

            def product_v(ph, step, U, layer, b, g):
                pe.wait_ge(exp_ready, EXP0 + U * (3 * G) + 3 * g + 3)
                if g == 0 and layer == "c":
                    pe.wait_ge(v_ready, (step + 1) * 2)
                pe.wait_ge(yT_ready, YT0 - 1 + U * G + g + 1)
                for kt in range(QT):
                    for j in range(4):
                        h = 4 * g + j
                        cols, src = ((0, KEYS0[layer]), (0, KEYS0[layer])) if kt == 0 else ((P, T), (256, 384))
                        last = nc.tensor.matmul(pv[32 * j:32 * j + 32, cols[0]:cols[1]], vone[layer][:, b * QT + kt, h, :],
                                                probs[:, g % 2, j, src[0]:src[1]], start=(kt == 0), stop=(kt == QT - 1),
                                                skip_group_check=True)
                last.then_inc(pv_full, 1)

            def T_(ph, seg, step, layer, b, g):
                q, k = stack[layer + "q"], stack[layer + "k"]
                U = unit(step, layer, b)
                if g == 0:
                    pe.wait_ge(m_rows, U * 16 + 16)
                    pe.wait_ge(ones_ready, 1)
                t0, n0 = b * T, KEYS0[layer]
                banks = [(mk0[layer], range(4 * g + 2 * n, 4 * g + 2 * n + 2), t0, t0, n0) for n in range(2)]
                banks.append((mk1[layer], range(4 * g, 4 * g + 4), t0 + P, t0 + P, P))
                for i, (mask, heads, k0, q0, w) in enumerate(banks):
                    job = 3 * g + i
                    pe.wait_ge(exp_ready, EXP0 + U * (3 * G) + job - 2)
                    bank_scores(byk[i], byk_full[i], mask, 0, w,
                                [(k[0:KR + MR, h, k0:k0 + P], q[0:KR + MR, h, q0:q0 + w]) for h in heads])
                if g > 0:
                    product_v(ph, step, U, layer, b, g - 1)
                if g == G - 1:
                    product_v(ph, step, U, layer, b, g)

            def Y1(ph, seg, step, layer, b):
                U = unit(step, layer, b)
                pe.wait_ge(yT_ready, YT0 + (U + 1) * G)
                for t in range(QT):
                    work_job(ph, seg, t, lambda bank: transposes(bank, [yT[:, g, t * P:(t + 1) * P] for g in range(G)]))
                if layer == "c":
                    work_job(ph, seg, QT, lambda bank: transposes(
                        bank, [fq["c"][:, c, b * T + t * P:b * T + (t + 1) * P] for t in range(QT) for c in range(C)]))

            def Y2(ph, seg, step, layer, b):
                emptied(pe, ph, ("Y1", "s", b), 0, 1)
                work_job(ph, seg, 0, lambda bank: transposes(
                    bank, [ynat[:, t, c * P:(c + 1) * P] for c in range(C) for t in range(QT)]))

            def Y3(ph, seg, step, layer, b):
                emptied(pe, ph, ("Y2", "s", b), 0)

                def project(bank):
                    for t in range(QT):
                        for c in range(C):
                            last = nc.tensor.matmul(bank[:, t * D:(t + 1) * D], turned[:, c, t * P:(t + 1) * P], woT[:, c, :],
                                                    start=(c == 0), stop=(c == C - 1))
                    return last
                work_job(ph, seg, 0, project)

            def RX(ph, seg, step, layer, b):
                pe.wait_ge(x2_ready, step * STEP_B + b + 1)
                work_job(ph, seg, 0, lambda bank: transposes(
                    bank, [x2[:, t, c * P:(c + 1) * P] for c in range(C) for t in range(QT)]))

            def R(ph, seg, step, layer, b):
                emptied(pe, ph, ("RX", "c", b), 0)

                def router(bank):
                    for t in range(QT):
                        for c in range(C):
                            last = nc.tensor.matmul(bank[:, t * 8:(t + 1) * 8], turned[:, c, t * P:(t + 1) * P], wr[:, c, :],
                                                    start=(c == 0), stop=(c == C - 1))
                    return last
                work_job(ph, seg, 0, router)

            pe.wait_ge(consts, 2)
            pe.sem_inc(pv_full, PV0)
            walk({"SX": SX, "SQ": SQ, "SK": SK, "SV": SV, "KX": KX, "CK": CK, "CV": CV, "CX": CX, "CQ": CQ, "N": N, "M": M,
                  "T": T_, "Y1": Y1, "Y2": Y2, "Y3": Y3, "RX": RX, "R": R}, pe.Fori)

            pe.wait_ge(choice_ready, 1)
            pe.wait_ge(exp_ready, EXP0 + 2 * B * 3 * G)
            counts = byk[0]
            nc.tensor.matmul(counts[:, 0:NM], tri[:, :], choice[:, :], start=True, stop=True)
            nc.tensor.matmul(counts[:, NM:2 * NM], onesb[:, :], choice[:, :], start=False, stop=True, skip_group_check=True)\
                .then_inc(counted, 1)

            emptied(pe, ("epi", 0), ("RX", "c", 1), 0)
            emptied(pe, ("epi", 0), ("R", "c", 1), 0)
            pe.wait_ge(yT_ready, YT0 + 2 * B * G)
            pe.wait_ge(routed, 1)

            def ex_job(job, it, emit):
                b, n = expert_turn(job, it)
                wait(pe, ex_free[b], n)
                emit(banks8[b]).then_inc(ex_full[b], 1)

            def tokens_T(i, it):
                pe.wait_ge(xe_in[i], it * 32 + 32)
                for c in range(C):
                    def emit(bank):
                        for t in range(FULL + 1):
                            n = P if t < FULL else REST
                            mm = nc.tensor.transpose(bank[:, t * P:t * P + n], xe[i][0:n, t, c * P:(c + 1) * P], ident[0:n, 0:n])
                        return mm
                    ex_job(("x", i, c), it, emit)

            def hidden(i, it):
                pe.wait_ge(wi_in[i], it * 16 + 16)
                for f in range(FC):
                    def emit(bank):
                        for c in range(C):
                            mm = nc.tensor.matmul(bank[:, 0:SLOTS], wi[i][:, c, f * P:(f + 1) * P], xeT[i][:, c, :],
                                                  start=(c == 0), stop=(c == C - 1))
                        return mm
                    ex_job(("h", i, f), it, emit)

            def output(i, it):
                pe.wait_ge(wo_in[i], it * 16 + 16)
                for f in range(FC):
                    ex_result(pe, ("h", i, f), it)
                for t in range(FULL):
                    def emit(bank):
                        for f in range(FC):
                            mm = nc.tensor.matmul(bank[:, 0:D], hT[i][:, f, t * P:(t + 1) * P], wo[i][:, f, :],
                                                  start=(f == 0), stop=(f == FC - 1))
                        return mm
                    ex_job(("y", i, t), it, emit)

                def rest(bank):
                    for f in range(FC):
                        for n in range(2):
                            mm = nc.tensor.matmul(bank[n * REST:(n + 1) * REST, 0:P], hT[i][:, f, FULL * P:SLOTS],
                                                  wo[i][:, f, n * P:(n + 1) * P], start=(f == 0), stop=(f == FC - 1),
                                                  skip_group_check=True)
                    return mm
                ex_job(("y", i, FULL), it, rest)

            def pair(it, last):
                for i in range(2):
                    for c in range(C):
                        ex_result(pe, ("x", i, c), it)
                    hidden(i, it)
                    if not (last and i == 1):
                        tokens_T(1 - i, it + i)
                    output(i, it)

            tokens_T(0, 0)
            experts(pe, pair)

        @block.scalar
        def _(act):
            nc.scalar.preload_act_table_set("natural_log_exp_and_others")
            def take(phase, seg, j, emit):
                b, n = turns.at(phase, seg, j)
                act.wait_ge(work_full[b], n + 1)
                return emit(work[b]).then_inc(work_free[b], 1)

            def copy_out(phase, seg, j, dst, cols=512):
                take(phase, seg, j, lambda bank: nc.scalar.activation(dst, bank[:, 0:cols] if dst.ndim == 2 else
                     bank[:, 0:cols].rearrange("p (a b) -> p a b", a=dst.shape[1]), ACT.Copy))

            def xT_out(ph, seg):
                for c in range(C):
                    copy_out(ph, seg, c, xT[:, c, :])

            def f_out(phase, seg, j, dst, part, func, bias, scale):
                def emit(bank):
                    nc.scalar.activation(dst, bank[:, :], func, bias=bias, scale=scale)
                    return nc.scalar.activation(part, bank[:, :], func, bias=bias, scale=scale)
                take(phase, seg, j, emit)

            for m in range(8):
                dst = wqkvT[:, :, m * P:(m + 1) * P] if m < 6 else woT[:, :, (m - 6) * P:(m - 5) * P]
                copy_out(("pro", 0), ("W",), m, dst, cols=2 * P)

            def SX(ph, seg, step):
                xT_out(ph, seg)

            def SQ(ph, seg, step):
                if isinstance(step, int):
                    emptied(act, ph, ("W",), 8)
                    act.wait_ge(consts, 2)
                for m in range(C):
                    f_out(ph, seg, m, fq["s"][:, m, :], parts["sq"][:, m, 0, :], ACT.Identity, bias[:, 0, m:m + 1], 0.25)

            def SK(ph, seg, step):
                wait(act, stored["k"], step * 2 * (C * 16))
                for m in range(C):
                    f_out(ph, seg, m, fk[:, m, :], parts["sk"][:, m, 0, :], ACT.Identity, bias[:, 0, C + m:C + m + 1], 1.0)

            def KX(ph, seg, step):
                xT_out(ph, seg)

            def CK(ph, seg, step):
                act.wait_ge(stored["k"], (step * 2 + 1) * (C * 16))
                for m in range(C):
                    f_out(ph, seg, m, fk[:, m, :], parts["ck"][:, m, 0, :], ACT.Relu, bias[:, 1, C + m:C + m + 1], 1.0)

            def to_turned(ph, seg, step, layer, b):
                copy_out(ph, seg, 0, turned[:, :, :])

            def CQ(ph, seg, step, layer, b):
                def emit(bank):
                    t = slice(b * T, (b + 1) * T)
                    for m in range(C):
                        act_in = bank[:, m * T:(m + 1) * T]
                        nc.scalar.activation(fq["c"][:, m, t], act_in, ACT.Relu, bias=bias[:, 1, m:m + 1], scale=0.25)
                        last = nc.scalar.activation(parts["cq"][:, m, 0, t], act_in, ACT.Relu, bias=bias[:, 1, m:m + 1], scale=0.25)
                    return last
                take(ph, seg, 0, emit)

            def M(ph, seg, step, layer, b):
                U = unit(step, layer, b)
                wait(act, m_stored, U * 16)
                take(ph, seg, 0, lambda bank: nc.scalar.activation(mT[:, :], bank[0:MR * H, :].bitcast(BF16)[:, 0:T], ACT.Copy))

            def yT_out(U, g):
                act.wait_ge(pv_full, PV0 + U * G + g + 1)
                nc.scalar.activation(yT[:, g, :], pv[:, 0:T], ACT.Copy).then_inc(yT_ready, 1)

            def T_(ph, seg, step, layer, b, g):
                U = unit(step, layer, b)
                n0 = KEYS0[layer]
                act.wait_ge(pv_full, PV0 + U * G + g - 1)
                for i in range(3):
                    act.wait_ge(byk_full[i], U * G + g + 1)
                    if i < 2:
                        dst, src = probs[:, g % 2, 2 * i:2 * i + 2, 0:n0], byk[i][:, 0:2 * n0].rearrange("p (a b) -> p a b", a=2)
                    else:
                        dst, src = probs[:, g % 2, :, 256:384], byk[i][:, :].rearrange("p (a b) -> p a b", a=4)
                    nc.scalar.activation(dst, src, ACT.Exp).then_inc(exp_ready, 1)
                if g > 0:
                    yT_out(U, g - 1)
                if g == G - 1:
                    yT_out(U, g)

            def rstd_of(number):
                act.wait_ge(var_ready, number + 1)
                nc.scalar.activation(lnv[:, :], mv[:, :, 1], ACT.Ln, bias=eps[:, :]).then_inc(lnv_ready, 1)
                act.wait_ge(lnv_ready, number + 1)
                nc.scalar.activation(rstd[:, :], lnv[:, :], ACT.Exp, scale=-0.5).then_inc(rstd_ready, 1)

            def L3(ph, seg, step, layer, b):
                rstd_of(norms_before(step, layer, b))

            def L1(ph, seg, step, layer, b):
                rstd_of(norms_before(step, layer, b))

            def L2(ph, seg, step, layer, b):
                rstd_of(norms_before(step, layer, b) + 1)

            act.sem_inc(exp_ready, EXP0)
            act.sem_inc(yT_ready, YT0)
            walk({"SX": SX, "SQ": SQ, "SK": SK, "KX": KX, "CK": CK, "CX": to_turned, "CQ": CQ, "M": M, "T": T_, "L1": L1, "L2": L2, "L3": L3,
                  "Y2": to_turned, "RX": to_turned}, act.Fori)

            act.wait_ge(diff_ready, 1)
            nc.scalar.activation(expd[:, :, :], diff[:, :, :], ACT.Exp).then_inc(expd_ready, 1)

            def ex_take(job, it, emit):
                b, n = expert_turn(job, it)
                act.wait_ge(ex_full[b], n + 1)
                emit(banks8[b]).then_inc(ex_free[b], 1)

            def tokens_T(i, it):
                if i == 0 and isinstance(it, int) and it == 0:
                    act.wait_ge(routed, 1)
                for c in range(C):
                    ex_take(("x", i, c), it, lambda bank: nc.scalar.activation(xeT[i][:, c, :], bank[:, 0:SLOTS], ACT.Copy))

            def pair(it, last):
                for i in range(2):
                    for f in range(0, FC, 2):
                        ex_take(("h", i, f), it, lambda bank: nc.scalar.activation(hT[i][:, f, :], bank[:, 0:SLOTS], ACT.Relu))
                    if not (last and i == 1):
                        tokens_T(1 - i, it + i)
                    wait(act, y_stored[i], it * 48)
                    ex_take(("y", i, 1), it, lambda bank: nc.scalar.activation(ye[i][:, D:2 * D], bank[:, 0:D], ACT.Copy))

            tokens_T(0, 0)
            experts(act, pair)

            for n in range(NT // QT):
                rstd_of(6 * STEPS + n)

        @block.vector
        def _(dve):
            V = nc.vector
            seq = [0]

            def link(ins):
                seq[0] += 1
                ins.then_inc(dve_seq, 1)
                dve.wait_ge(dve_seq, seq[0])

            def begin():
                seq[0] = 0
                dve.sem_clear(dve_seq)

            def split23(dst, f, rest, last_sem, before):
                wait(dve, last_sem, before)
                link(V.tensor_tensor(rest, f, dst[0], ALU.subtract))
                link(V.tensor_copy(dst[1], rest))
                V.tensor_tensor(dst[2], rest, dst[1], ALU.subtract).then_inc(last_sem, 1)

            bk, n = turns.at(("pro", 0), ("W",), 8)
            dve.wait_ge(work_full[bk], n + 1)
            by_col = work[bk][:, 0:4 * C].rearrange("p (l m) -> p l m", l=2)
            V.tensor_scalar(bias[:, :, 0:C], by_col[:, :, 0:C], 0.25, None, ALU.mult)
            V.tensor_copy(bias[:, :, C:2 * C], by_col[:, :, C:2 * C]).then_inc(work_free[bk], 1)
            dve.wait_ge(w_in, 16 * W_LOADS)

            def v_out(ph, seg, j0, layer, step):
                if not isinstance(step, int):
                    dve.wait_ge(pv_full, PV0 + (unit(step, layer, 1) - 4 + 1) * G)
                for n in range(2):
                    b, cnt = turns.at(ph, seg, j0 + n)
                    dve.wait_ge(work_full[b], cnt + 1)
                    v = vone[layer][:, 2 * n:2 * n + 2, :, 0:HD]
                    bvb = bv[layer][:, :].unsqueeze(1).broadcast_to([P, 2, D]).rearrange("p t (h d) -> p t h d", h=H)
                    src = work[b][:, :].rearrange("p (t h d) -> p t h d", t=2, h=H)
                    if layer == "s":
                        V.tensor_tensor(v, src, bvb, ALU.add).then_inc(work_free[b], 1)
                    else:
                        V.tensor_tensor(v, src, bvb, ALU.add).then_inc(work_free[b], 1)
                        emptied(dve, ph, seg, j0 + n)
                        V.tensor_scalar(v, v, 0.0, None, ALU.max).then_inc(v_ready, 1)

            def SS(ph, seg, step):
                for m in range(C):
                    emptied(dve, ph, ("SQ",), m)
                    split23([parts["sq"][:, m, i, :] for i in range(3)], fq["s"][:, m, :], resq[:, :], split["q"],
                            q_splits(step, "s") + m)

            def SV(ph, seg, step):
                v_out(ph, seg, 0, "s", step)

            def CV(ph, seg, step):
                v_out(ph, seg, 0, "c", step)

            def CS(ph, seg, step, layer, b):
                emptied(dve, ph, ("CQ", "c", b), 0)
                t = slice(b * T, (b + 1) * T)
                for m in range(C):
                    split23([parts["cq"][:, m, i, t] for i in range(3)], fq["c"][:, m, t], resq[:, 0:T], split["q"],
                            q_splits(step, "c", b) + m)

            def N(ph, seg, step, layer, b, g):
                U = unit(step, layer, b)
                for i in range(3):
                    job = 3 * g + i
                    bank = nat[job % 2]
                    dve.wait_ge(nat_full[job % 2], U * 6 + job // 2 + 1)
                    if i == 0:
                        dst, src = negm[:, 0, 4 * g:4 * g + 4], bank[:, :].rearrange("p (h k) -> p h k", h=4)
                    else:
                        w = KEYS0[layer]
                        dst = negm[:, 1, 4 * g + 2 * i - 2:4 * g + 2 * i]
                        src = bank[:, 0:2 * w].rearrange("p (h k) -> p h k", h=2)
                    V.tensor_reduce(dst, src, AX, ALU.max, negate=True).then_inc(nat_free[job % 2], 1)
                if g == G - 1:
                    for n in range(2):
                        dve.wait_ge(nat_free[n], (U + 1) * 6)
                    wait(dve, m_stored, U * 16)
                    link(V.tensor_copy(mp[:, :, 0:H], negm[:, :, :]))
                    split23([mp[:, :, i * H:(i + 1) * H] for i in range(3)], negm[:, :, :], rm[:, :, :], mp_ready, U)

            def moments():
                for t in range(QT):
                    i = V.bn_stats(stats[:, t, :], r[:, t, :])
                link(i)
                for t in range(QT):
                    i = V.bn_aggr(mv[:, t, :], stats[:, t, :])
                i.then_inc(var_ready, 1)

            def refine(number):
                dve.wait_ge(rstd_ready, number + 1)
                link(V.tensor_tensor(newton[:, :], rstd[:, :], rstd[:, :], ALU.mult))
                link(V.scalar_tensor_tensor(out=newton[:, :], in0=mv[:, :, 1], scalar=EPS, in1=newton[:, :], op0=ALU.add, op1=ALU.mult))
                link(V.tensor_scalar(newton[:, :], newton[:, :], -0.5, 1.5, ALU.mult, ALU.add))
                link(V.tensor_tensor(rstd[:, :], rstd[:, :], newton[:, :], ALU.mult))

            def scaled(number, dst_of, last):
                refine(number)
                for t in range(QT):
                    i = V.tensor_scalar(dst_of(t), r[:, t, :], mv[:, t, 0:1], rstd[:, t:t + 1], ALU.subtract, ALU.mult)
                last(i)

            def Y1(ph, seg, step, layer, b):
                for t in range(QT):
                    bk, n = turns.at(ph, seg, t)
                    dve.wait_ge(work_full[bk], n + 1)
                    y = work[bk][:, :].rearrange("p (h d) -> p h d", h=H)
                    link(V.reciprocal(rec[:, t, :], y[:, :, HD]))
                    V.tensor_tensor(ynat[:, t, :].rearrange("p (h d) -> p h d", h=H), y[:, :, 0:HD],
                                        rec[:, t, :].unsqueeze(2).broadcast_to([P, H, HD]), ALU.mult).then_inc(work_free[bk], 1)
                emptied(dve, ph, seg, 0, 1)
                if layer == "s":
                    return
                bk, n = turns.at(ph, seg, QT)
                dve.wait_ge(work_full[bk], n + 1)
                V.scalar_tensor_tensor(out=r[:, :, :], in0=work[bk][:, :].rearrange("p (t d) -> p t d", t=QT), scalar=4.0,
                                       in1=ynat[:, :, :], op0=ALU.mult, op1=ALU.add).then_inc(work_free[bk], 1)
                emptied(dve, ph, seg, QT)
                moments()
                dve.wait_ge(var_ready, norms_before(step, layer, b) + 1)
                for t in range(QT):
                    i = V.scalar_tensor_tensor(out=r[:, t, :], in0=r[:, t, :], scalar=mv[:, t, 0:1], in1=gamma[:, :],
                                               op0=ALU.subtract, op1=ALU.mult)
                link(i)

            def L1(ph, seg, step, layer, b):
                refine(norms_before(step, layer, b))
                dve.wait_ge(x1b_ready, step * STEP_B + b + 1)
                for t in range(QT):
                    i = V.scalar_tensor_tensor(out=r[:, t, :], in0=r[:, t, :], scalar=rstd[:, t:t + 1], in1=x1[:, b * QT + t, :],
                                               op0=ALU.mult, op1=ALU.add)
                link(i)
                moments()

            def L2(ph, seg, step, layer, b):
                dve.wait_ge(x2_free, step * STEP_B + b + 1)
                scaled(norms_before(step, layer, b) + 1, lambda t: x2[:, t, :], lambda i: i.then_inc(x2_ready, 1))

            def Y3(ph, seg, step, layer, b):
                bk, n = turns.at(ph, seg, 0)
                dve.wait_ge(work_full[bk], n + 1)
                dve.wait_ge(xb_ready, step + 1)
                V.tensor_tensor(r[:, :, :], work[bk][:, :].rearrange("p (t d) -> p t d", t=QT), xb[:, b * QT:(b + 1) * QT, :],
                                ALU.add).then_inc(work_free[bk], 1)
                emptied(dve, ph, seg, 0)
                moments()

            def L3(ph, seg, step, layer, b):
                scaled(norms_before(step, layer, b), lambda t: x1[:, b * QT + t, :], lambda i: i.then_inc(x1_ready, 1))

            def R(ph, seg, step, layer, b):
                bk, n = turns.at(ph, seg, 0)
                dve.wait_ge(work_full[bk], n + 1)
                V.tensor_copy(logits[:, bass.ds((step * STEP_B + b) * QT, QT), :],
                              work[bk][:, 0:QT * 8].rearrange("p (t e) -> p t e", t=QT)).then_inc(work_free[bk], 1)

            walk({"begin": begin, "SS": SS, "SV": SV, "CV": CV, "CS": CS, "N": N, "Y1": Y1, "L1": L1, "L2": L2, "Y3": Y3, "L3": L3,
                  "R": R}, dve.Fori)

            emptied(dve, ("epi", 0), ("R", "c", 1), 0)
            for t in range(NT):
                i = V.max(top[:, t, :], logits[:, t, :])
            link(i)
            V.tensor_tensor(diff[:, :, :], top[:, :, :], top[:, :, 0:1].broadcast_to([P, NT, 8]), ALU.subtract).then_inc(diff_ready, 1)
            for t in range(NT):
                i = V.max_index(topi[:, t, :], top[:, t, :], logits[:, t, :])
            link(i)
            link(V.tensor_copy(idxf[:, :, :], topi[:, :, 0:TOPK]))
            dve.wait_ge(consts, 2)
            by_choice = choice[:, :].rearrange("p (g e k t) -> p g t e k", g=GROUPS, e=E, k=TOPK)
            for g in range(GROUPS):
                for k in range(TOPK):
                    i = V.tensor_tensor(by_choice[:, g, :, :, k], iota_e[:, :].unsqueeze(1).broadcast_to([P, GT, E]),
                                        idxf[:, g * GT:(g + 1) * GT, k].unsqueeze(2).broadcast_to([P, GT, E]), ALU.is_equal)
            i.then_inc(choice_ready, 1)
            dve.wait_ge(expd_ready, 1)
            link(V.tensor_reduce(esum[:, :], expd[:, :, :], AX, ALU.add))
            link(V.reciprocal(esum[:, :], esum[:, :]))
            V.tensor_tensor(gates[:, :, :], expd[:, :, 0:TOPK], esum[:, :].unsqueeze(2).broadcast_to([P, NT, TOPK]), ALU.mult)
            dve.wait_ge(counted, 1)
            counts = byk[0]
            link(V.tensor_tensor_scan(before[:, :], goes_on[:, :], counts[:, NM:2 * NM], 0.0, ALU.mult, ALU.add))
            link(V.tensor_tensor(before[:, :], before[:, :], counts[:, NM:2 * NM], ALU.subtract))
            link(V.tensor_tensor(before[:, :], before[:, :], counts[:, 0:NM], ALU.add))
            link(V.tensor_tensor(before[:, :], before[:, :], choice[:, :], ALU.mult))
            for g in range(GROUPS):
                i = V.tensor_reduce(pos[:, g, :], before[:, g * (NM // GROUPS):(g + 1) * (NM // GROUPS)].rearrange(
                    "p (e kt) -> p kt e", e=E), AX, ALU.add)
            for g in range(GROUPS):
                for k in range(TOPK):
                    i = V.scalar_tensor_tensor(out=slot[:, g, k * GT:(k + 1) * GT], in0=idxf[:, g * GT:(g + 1) * GT, k],
                                               scalar=float(SLOTS), in1=gbase[:, g, k * GT:(k + 1) * GT], op0=ALU.mult, op1=ALU.add)
            link(i)
            V.tensor_scalar(late[:, :, :], pos[:, :, :], float(CAP), BAD, ALU.is_gt, ALU.mult)
            link(V.tensor_tensor(slot[:, :, :], slot[:, :, :], pos[:, :, :], ALU.add))
            link(V.tensor_tensor(slot[:, :, :], slot[:, :, :], late[:, :, :], ALU.add))
            flat = slot[:, :, :].rearrange("p g n -> p (g n)")
            V.tensor_copy(put[:, :], flat)
            link(V.tensor_scalar(flat, flat, float(E * SLOTS), None, ALU.min))
            V.tensor_copy(get[:, :], flat).then_inc(routed, 1)

            def ex_take(job, it, emit):
                b, n = expert_turn(job, it)
                dve.wait_ge(ex_full[b], n + 1)
                emit(banks8[b]).then_inc(ex_free[b], 1)

            def pair(it, last):
                for i in range(2):
                    for f in range(1, FC, 2):
                        ex_take(("h", i, f), it, lambda bank: V.tensor_scalar(hT[i][:, f, :], bank[:, 0:SLOTS], 0.0, None, ALU.max))
                    wait(dve, y_stored[i], it * 48)
                    ex_take(("y", i, 0), it, lambda bank: V.tensor_copy(ye[i][:, 0:D], bank[:, 0:D]))
                    ex_take(("y", i, FULL), it, lambda bank: V.tensor_copy(ye[i][:, FULL * D:YE], bank[:, 0:P]))

            experts(dve, pair)

            for n in range(NT // QT):
                dve.wait_ge(got_sem[n], QT * TOPK * 16)
                wait(dve, out_ready, n)
                for k in range(TOPK):
                    for t in range(QT):
                        tile = n * QT + t
                        i = V.scalar_tensor_tensor(out=r[:, t, :], in0=got[:, tile * TOPK + k, :], scalar=gates[:, tile, k:k + 1],
                                                   in1=xres[:, tile, :] if k == 0 else r[:, t, :], op0=ALU.mult, op1=ALU.add)
                    link(i)
                wait(dve, out_stored[n % 2], n // 2 * 16)
                moments()
                scaled(6 * STEPS + n, lambda t: xin[:, (n % 2) * QT + t, :], lambda i: i.then_inc(out_ready, 1))

        @block.gpsimd
        def _(pool):
            g_ = nc.gpsimd
            seq = [0]

            def link(ins):
                seq[0] += 1
                ins.then_inc(pool_seq, 1)
                pool.wait_ge(pool_seq, seq[0])

            def begin():
                seq[0] = 0
                pool.sem_clear(pool_seq)

            g_.memset(ident[:, :], 0.0)
            link(g_.memset(identb[:, :], 0.0))
            g_.affine_select(out=identb[:, :], in_=identb[:, :], compare_op=ALU.not_equal, fill=1.0, base=0,
                             pattern=[[-1, P]], channel_multiplier=1)
            g_.affine_select(out=ident[:, :], in_=ident[:, :], compare_op=ALU.not_equal, fill=1.0, base=0,
                             pattern=[[-1, P]], channel_multiplier=1).then_inc(consts, 1)
            g_.memset(eps[:, :], EPS).then_inc(x2_free, 1)
            g_.memset(mp[:, :, :], 0.0)
            for layer in "sc":
                g_.memset(vone[layer][:, :, :, :], 1.0)
            masks = [mq0["s"], mq0["c"], mq1["s"], mq1["c"], mk0["s"], mk0["c"], mk1["s"], mk1["c"]]
            for m in masks:
                last = g_.memset(m[:, :, :], 0.0)
            link(last)

            def keep(m, base, cm, step):
                return g_.affine_select(out=m[:, :, :], in_=m[:, :, :], compare_op=ALU.is_ge, fill=NEG, base=base,
                                        pattern=[[0, m.shape[1]], [step, m.shape[2]]], channel_multiplier=cm)
            keep(mq0["s"], 0, 1, -1)
            keep(mq0["c"], 0, 1, -1)
            keep(mq1["s"], P - WIN, 1, -1)
            keep(mq1["c"], 0, 1, -1)
            keep(mk0["s"], 0, -1, 1)
            keep(mk0["c"], 0, -1, 1)
            keep(mk1["s"], 0, -1, 1)
            link(keep(mk1["c"], 0, -1, 1))
            keep(mq0["s"], WIN - 1, -1, 1)
            keep(mq1["s"], -1, -1, 1)
            keep(mk0["s"], WIN - 1, 1, -1)
            link(keep(mk1["s"], WIN - 1, 1, -1))
            g_.memset(zeros[:, :], 0.0)
            g_.memset(onesb[:, :], 1.0)
            g_.memset(tri[:, :], 1.0)
            g_.memset(goes_on[:, :], 1.0)
            for g in range(GROUPS):
                g_.memset(gbase[:, g, :], float(g * CAP - 1))
            link(g_.iota(iota_e[:, :], [[1, E]], base=0, channel_multiplier=0, allow_small_or_imprecise_dtypes=True))
            g_.memset(goes_on[:, :].rearrange("p (a b) -> p a b", b=TOPK * GT)[:, :, 0:1], 0.0).then_inc(zeros_ready, 1)
            pool.wait_ge(zeros_ready, 1)
            g_.affine_select(out=tri[:, :], in_=tri[:, :], compare_op=ALU.is_ge, fill=0.0, base=0,
                             pattern=[[1, P]], channel_multiplier=-1).then_inc(consts, 1)
            pool.wait_ge(consts, 2)

            def k_split(ph, seg, key, j0, n_before):
                for m in range(C):
                    emptied(pool, ph, seg, j0 + m)
                    p = [parts[key][:, m, i, :] for i in range(3)]
                    wait(pool, split["k"], n_before + m)
                    link(g_.tensor_tensor(resk[:, :], fk[:, m, :], p[0], ALU.subtract))
                    link(g_.tensor_copy(p[1], resk[:, :]))
                    g_.tensor_tensor(p[2], resk[:, :], p[1], ALU.subtract).then_inc(split["k"], 1)

            def XI(ph, seg, step):
                g_.tensor_copy(xin[:, :, :], xres[:, bass.ds(step * TT, TT), :]).then_inc(xin_ready, 1)

            def XB(ph, seg, step):
                if isinstance(step, int):
                    pool.wait_ge(x_in, 16 * STEPS)
                    pool.wait_ge(w_in, 16 * W_LOADS)
                else:
                    pool.wait_ge(xin_ready, step)
                    pool.wait_ge(x1_ready, step * STEP_B)
                g_.tensor_tensor(xb[:, :, :], xin[:, :, :], bo[:, :].unsqueeze(1).broadcast_to([P, TT, D]), ALU.add)\
                    .then_inc(xb_ready, 1)

            def SK(ph, seg, step):
                k_split(ph, seg, "sk", 0, k_splits(step, "s"))
                if isinstance(step, int):
                    emptied(pool, ph, ("W",), 6, 7)
                    pool.wait_ge(split["k"], C)
                    link(g_.memset(stack["sk"][KR:KR + MR, :, :], 1.0))
                    g_.memset(stack["ck"][KR:KR + MR, :, :], 1.0).then_inc(ones_ready, 1)
                    pool.wait_ge(ones_ready, 1)

            def CK(ph, seg, step):
                k_split(ph, seg, "ck", 0, k_splits(step, "c"))

            def CX(ph, seg, step, layer, b):
                pool.wait_ge(x1_ready, step * STEP_B + b + 1)
                emptied(pool, ph, seg, 0)
                x1_b = x1[:, b * QT:(b + 1) * QT, :]
                g_.tensor_tensor(x1_b, x1_b, beta[:, :].unsqueeze(1).broadcast_to([P, QT, D]), ALU.add).then_inc(x1b_ready, 1)

            def RX(ph, seg, step, layer, b):
                n = step * STEP_B + b
                pool.wait_ge(x2_ready, n + 1)
                g_.tensor_copy(xres[:, bass.ds(n * QT, QT), :], x2[:, :, :]).then_inc(x2_free, 1)

            walk({"begin": begin, "XI": XI, "XB": XB, "SK": SK, "CK": CK, "CX": CX, "RX": RX}, pool.Fori)

            pool.wait_ge(routed, 1)
            pool.wait_ge(cleared, 32)
            pool.wait_ge(x2_free, B + 1)
            for tile in range(NT):
                for k in range(TOPK):
                    col = (tile // GT) * (TOPK * GT) + k * GT + tile % GT
                    pool.indirect_dma_start(out=x_dram, out_offset=bass.IndirectOffsetOnAxis(ap=put[:, col:col + 1], axis=0),
                                            in_=xres[:, tile, :], in_offset=None, bounds_check=E * SLOTS - 1, oob_is_err=False)\
                        .then_inc(put_done, 16)
            for i in range(2):
                pool.wait_ge(y_stored[i], (E // 2) * 48)
            for tile in range(NT):
                for k in range(TOPK):
                    col = (tile // GT) * (TOPK * GT) + k * GT + tile % GT
                    pool.indirect_dma_start(out=got[:, tile * TOPK + k, :], out_offset=None, in_=y_dram,
                                            in_offset=bass.IndirectOffsetOnAxis(ap=get[:, col:col + 1], axis=0))\
                        .then_inc(got_sem[tile // QT], 16)


_INS = ["x", "ctx_1024", "L0_attn_Wqkv", "L0_attn_bqkv", "L0_attn_Wo", "L0_attn_bo", "L0_xattn_Wq", "L0_xattn_bq",
        "L0_xattn_Wk", "L0_xattn_bk", "L0_xattn_Wv", "L0_xattn_bv", "L0_xattn_gamma", "L0_xattn_beta",
        "L0_ffn_w_router", "L0_ffn_wi", "L0_ffn_wo"]


def kernel(**inputs):
    import numpy as np
    import concourse.bacc as bacc
    from concourse.bass_utils import run_bass_kernel_spmd

    nc = bacc.Bacc("TRN2", target_bir_lowering=False, num_devices=1)
    arrays, a = {}, {}
    for name in _INS:
        array = np.ascontiguousarray(inputs[name])
        arrays[f"in_{name}"] = array
        a[name] = nc.dram_tensor(f"in_{name}", array.shape, mybir.dt.from_np(array.dtype), kind="ExternalInput").ap()
    out = nc.dram_tensor("out", [B, T, D], F32, kind="ExternalOutput").ap()
    attention_and_experts(nc, a, out)
    r = run_bass_kernel_spmd(nc, [arrays], core_ids=[0])
    return r.results[0]["out"]
```

```python
from contextlib import ExitStack

import concourse.bass as bass
from concourse import mybir

F32 = mybir.dt.float32
BF16 = mybir.dt.bfloat16
U32 = mybir.dt.uint32
ALU = mybir.AluOpType
ACT = mybir.ActivationFunctionType
AX = mybir.AxisListType.X

P = 128
B, T, D = 8, 256, 256
H, HD, WIN = 16, 16, 64
C = D // P
STEP_B = 2
ST = STEP_B * T
STEPS = B // STEP_B
TT = ST // P
QT = T // P
NT = B * QT
G = H // 4
Q_SLOTS = (0, 1, 0, 1, 2, 0)
K_SLOTS = (0, 0, 1, 1, 0, 2)
KR = 6 * HD
MR = 3
KEYS0 = {"s": 192, "c": 256}
E, TOPK, CAP, F = 8, 2, 160, 1024
GROUPS = 2
GT = NT // GROUPS
SLOTS = GROUPS * CAP
FC = F // P
FULL = SLOTS // P
REST = SLOTS - FULL * P
BAD = 4096.0
NEG = -3.0e38
EPS = 1e-5

BODY = (
    [("XI",), ("T", "s", 0, 3), ("T", "s", 1, 0), ("Y1", "s", 0), ("T", "s", 1, 1), ("Y2", "s", 0), ("T", "s", 1, 2), ("Y3", "s", 0)]
    + [("SX",), ("T", "s", 1, 3), ("L3", "s", 0), ("SQ",), ("CX", "c", 0), ("Y1", "s", 1), ("CQ", "c", 0), ("SK",), ("CS", "c", 0)]
    + [("Y2", "s", 1), ("SV",), ("Y3", "s", 1), ("L3", "s", 1), ("KS",), ("N", "c", 0, 0), ("CX", "c", 1), ("N", "c", 0, 1)]
    + [("CQ", "c", 1), ("KX",), ("CS", "c", 1), ("SS",), ("SL",), ("CK",), ("N", "c", 0, 2), ("XB",), ("N", "c", 0, 3), ("N", "c", 1, 0)]
    + [("M", "c", 0), ("N", "c", 1, 1), ("N", "c", 1, 2), ("T", "c", 0, 0), ("N", "c", 1, 3), ("T", "c", 0, 1), ("N", "s", 0, 0)]
    + [("M", "c", 1), ("T", "c", 0, 2), ("N", "s", 0, 1), ("T", "c", 0, 3), ("T", "c", 1, 0), ("Y1", "c", 0), ("T", "c", 1, 1)]
    + [("N", "s", 0, 2), ("L1", "c", 0), ("T", "c", 1, 2), ("N", "s", 0, 3), ("T", "c", 1, 3), ("L2", "c", 0), ("M", "s", 0)]
    + [("KL",), ("CV",), ("N", "s", 1, 0), ("Y1", "c", 1), ("RX", "c", 0), ("N", "s", 1, 1), ("L1", "c", 1), ("R", "c", 0)]
    + [("T", "s", 0, 0), ("N", "s", 1, 2), ("L2", "c", 1), ("N", "s", 1, 3), ("T", "s", 0, 1), ("RX", "c", 1), ("M", "s", 1)]
    + [("T", "s", 0, 2), ("R", "c", 1)]
)


def for_next(seg):
    return seg[0] in ("XI", "SX", "SQ", "SK", "SV", "SS", "SL", "KS", "XB", "KX", "CK", "KL", "CV") or seg[0:2] in (("N", "s"), ("M", "s")) or \
        seg in (("T", "s", 0, 0), ("T", "s", 0, 1), ("T", "s", 0, 2))


PROLOGUE = (
    [("SX",), ("SQ",), ("SK",), ("SS",), ("SL",), ("KS",), ("SV",), ("XB",), ("KX",), ("CK",)] + [("N", "s", 0, g) for g in range(G)]
    + [("CV",), ("M", "s", 0), ("N", "s", 1, 0), ("N", "s", 1, 1), ("T", "s", 0, 0), ("N", "s", 1, 2), ("N", "s", 1, 3)]
    + [("T", "s", 0, 1), ("M", "s", 1), ("T", "s", 0, 2), ("KL",)]
)
LOOP = BODY
EPILOGUE = [seg for seg in BODY if not for_next(seg)]
EPILOGUE.insert(EPILOGUE.index(("T", "c", 0, 1)), ("G", 0))
EPILOGUE.append(("G", 1))

WORK_JOBS = {"SX": 2, "SQ": 2, "SK": 2, "SV": 2, "KX": 2, "CK": 2, "CV": 2, "CX": 1, "CQ": 1, "M": 1, "Y1s": 2, "Y1c": 3, "Y2": 1, "Y3": 1, "RX": 1, "R": 1, "W": 9}
WB = 2
W_LOADS = 10


def jobs_of(seg):
    return WORK_JOBS[seg[0] + seg[1] if seg[0] == "Y1" else seg[0]]


XB = 6
PAIR_JOBS = [(kind, i, n) for i in range(2) for kind, count in (("h", FC), ("y", FULL + 1)) for n in range(count)]
PER_BANK = [len(PAIR_JOBS[b::XB]) for b in range(XB)]


def expert_turn(job, it):
    kind, i, n = job
    if kind == "x":
        return XB + n, it * 2 + i
    n = PAIR_JOBS.index(job)
    return n % XB, it * PER_BANK[n % XB] + n // XB


class WorkTurns:

    def __init__(self):
        self.local = {}
        self.total = {}
        for name, plan in (("pro", [("W",)] + PROLOGUE), ("loop", LOOP), ("epi", EPILOGUE)):
            n, count = 0, [0] * WB
            for seg in plan:
                if seg[0] not in WORK_JOBS and seg[0] != "Y1":
                    continue
                for j in range(jobs_of(seg)):
                    b = n % WB
                    self.local[(name, seg, j)] = (b, count[b])
                    count[b] += 1
                    n += 1
            self.total[name] = count

    def at(self, phase, seg, j):
        name, it = phase
        b, n = self.local[(name, seg, j)]
        if name == "loop":
            return b, it * self.total["loop"][b] + self.total["pro"][b] + n
        if name == "epi":
            return b, (STEPS - 1) * self.total["loop"][b] + self.total["pro"][b] + n
        return b, n


def wait(eng, sem, value):
    if not isinstance(value, int) or value > 0:
        eng.wait_ge(sem, value)


def attention_and_experts(nc: bass.Bass, a, out):
    turns = WorkTurns()
    with ExitStack() as ctx:
        def sb(name, shape, dt=F32):
            return ctx.enter_context(nc.sbuf_tensor(name, shape, dt))

        def sem(name):
            return ctx.enter_context(nc.semaphore(name))

        work = [ctx.enter_context(nc.psum_tensor(f"work{i}", [P, 512], F32)) for i in range(WB)]
        nat = [ctx.enter_context(nc.psum_tensor(f"nat{i}", [P, 512], F32)) for i in range(2)]
        byk = [ctx.enter_context(nc.psum_tensor(f"byk{i}", [P, 512], F32)) for i in range(3)]
        pv = ctx.enter_context(nc.psum_tensor("pv", [P, 512], F32))

        ident = sb("ident", [P, P])
        identb = sb("identb", [P, P], BF16)
        mq0 = {"s": sb("mq0s", [P, 4, P], BF16), "c": sb("mq0c", [P, 4, P], BF16)}
        mq1 = {"s": sb("mq1s", [P, 2, 192], BF16), "c": sb("mq1c", [P, 2, P], BF16)}
        mk0 = {"s": sb("mk0s", [P, 2, 192], BF16), "c": sb("mk0c", [P, 2, P], BF16)}
        mk1 = {"s": sb("mk1s", [P, 4, P], BF16), "c": sb("mk1c", [P, 4, P], BF16)}
        wqkvT = sb("wqkvT", [P, C, 3 * D])
        woT = sb("woT", [P, C, D])
        wc = {n: sb(f"w{n}_c", [P, C, D]) for n in "qkv"}
        bias_rows = sb("bias_rows", [4 * C, P])
        bias = sb("bias", [P, 2, 2 * C])
        bv = {"s": sb("bv_s", [P, D]), "c": sb("bv_c", [P, D])}
        bo = sb("bo", [P, D])
        gamma = sb("gamma", [P, D])
        beta = sb("beta", [P, D])
        wr = sb("wr", [P, C, 8])
        xres = sb("xres", [P, NT, D])
        xin = sb("xin", [P, TT, D])
        ctxin = sb("ctxin", [P, TT, D])
        xb = sb("xb", [P, TT, D])
        xT = sb("xT", [P, C, ST])
        fq = {"s": sb("fq_s", [P, C, ST]), "c": sb("fq_c", [P, C, ST])}
        fk = sb("fk", [P, C, ST])
        resq = sb("resq", [P, ST])
        resk = sb("resk", [P, ST])
        parts = {k: sb(f"parts_{k}", [P, C, 3, ST], BF16) for k in ("sq", "cq", "k")}
        parts["sk"] = parts["ck"] = parts["k"]
        arena = sb("arena", [P, 4 * H * ST // 2])
        ARENA_U = H * ST // 2
        stack = {}
        for i, key in enumerate(("sq", "sk", "cq", "ck")):
            stack[key] = arena[:, i * ARENA_U:(i + 1) * ARENA_U].bitcast(BF16).rearrange("p (h t) -> p h t", h=H)
        vone = {"s": sb("v_s", [P, TT, H, 32]), "c": sb("v_c", [P, TT, H, 32])}
        negm = sb("negm", [P, QT, H])
        rm = sb("rm", [P, QT, H])
        mp = sb("mp", [P, QT, P], BF16)
        mT = sb("mT", [MR * H, T], BF16)
        probs = sb("probs", [P, 2, 4, 384])
        yT = sb("yT", [P, G, T])
        rec = sb("rec", [P, QT, H])
        ynat = sb("ynat", [P, QT, D])
        turned = sb("turned", [P, C, T])
        r = sb("r", [P, QT, D])
        stats = sb("stats", [P, QT, 6])
        mv = sb("mv", [P, QT, 2])
        rstd = sb("rstd", [P, QT])
        lnv = sb("lnv", [P, QT])
        newton = sb("newton", [P, QT])
        eps = sb("eps", [P, 1])
        x1 = sb("x1", [P, TT, D])
        x2 = sb("x2", [P, QT, D])
        logits = sb("logits", [P, NT, E])
        iota_e = sb("iota_e", [P, E])
        tri = sb("tri", [P, P], BF16)
        onesb = sb("onesb", [P, P], BF16)
        NG = E * TOPK * GT
        NM = GROUPS * NG
        goes_on = sb("goes_on", [P, NM])
        gbase = sb("gbase", [P, GROUPS, TOPK * GT])
        top, topi, diff, expd = (fk[:, 0, i * NT * 8:(i + 1) * NT * 8].rearrange("p (t e) -> p t e", e=8) for i in range(4))
        topi = topi.bitcast(U32)
        esum = sb("esum", [P, NT])
        gates = sb("gates", [P, NT, TOPK])
        idxf = sb("idxf", [P, NT, TOPK])
        choice = sb("choice", [P, NM], BF16)
        before = fk[:, 1, 0:NM]
        pos = sb("pos", [P, GROUPS, TOPK * GT])
        slot = sb("slot", [P, GROUPS, TOPK * GT])
        late = sb("late", [P, GROUPS, TOPK * GT])
        put = sb("put", [P, GROUPS * TOPK * GT], U32)
        get = sb("get", [P, GROUPS * TOPK * GT], U32)
        WI, WO, HT_, XE, XET = C * F, FC * D, FC * SLOTS, (FULL + 1) * D, C * SLOTS
        at = 0
        wi, wo, hT, xe, xeT = [], [], [], [], []
        for group, size, lead in ((wi, WI, C), (wo, WO, FC), (hT, HT_, FC), (xe, XE, FULL + 1), (xeT, XET, C)):
            for i in range(2):
                group.append(arena[:, at:at + size].rearrange("p (c n) -> p c n", c=lead))
                at += size
        assert at <= 4 * ARENA_U
        YE = FULL * D + P
        ye = [xb[:, :, :].rearrange("p a b -> p (a b)")[:, 0:YE], ctxin[:, :, :].rearrange("p a b -> p (a b)")[:, 0:YE]]
        got = arena[:, 0:NT * TOPK * D].rearrange("p (n d) -> p n d", d=D)
        last_stats = xT[:, 0, 0:NT * 6].rearrange("p (t s) -> p t s", s=6)
        last_mv = xT[:, 0, NT * 6:NT * 8].rearrange("p (t s) -> p t s", s=2)
        last_rstd, last_log, last_newton = (xT[:, 0, NT * i:NT * (i + 1)] for i in (8, 9, 10))
        zeros = sb("zeros", [P, D // 2])

        part_dram = {k: nc.dram_tensor(f"part_{k}", [D, 3, ST], BF16).ap() for k in ("sq", "sk", "cq", "ck")}
        m_dram = nc.dram_tensor("m_rows", [MR, H, T], BF16).ap()

        x_dram = nc.dram_tensor("expert_x", [E * SLOTS, D], F32).ap()
        y_dram = nc.dram_tensor("expert_y", [E * SLOTS + 1, D], F32).ap()

        cleared = sem("cleared"); zeros_ready = sem("zeros_ready"); routed = sem("routed"); get_ready = sem("get_ready")
        diff_ready = sem("diff_ready"); expd_ready = sem("expd_ready"); choice_ready = sem("choice_ready")
        counted = sem("counted"); put_done = sem("put_done"); got_sem = [sem(f"got{i}") for i in range(STEPS)]
        wi_in = [sem(f"wi_in{i}") for i in range(2)]; wo_in = [sem(f"wo_in{i}") for i in range(2)]
        xe_in = [sem(f"xe_in{i}") for i in range(2)]
        ex_full = [sem(f"ex_full{i}") for i in range(XB + C)]
        ex_free = [sem(f"ex_free{i}") for i in range(XB + C)]
        y_stored = [sem(f"y_stored{i}") for i in range(2)]
        out_ready = sem("out_ready"); out_stored = sem("out_stored")
        w_in = sem("w_in"); w_in2 = sem("w_in2"); x_in = sem("x_in"); ctx_in = sem("ctx_in")
        consts = sem("consts"); ones_ready = sem("ones_ready");
        work_full = [sem(f"work_full{i}") for i in range(WB)]
        work_free = [sem(f"work_free{i}") for i in range(WB)]
        nat_full = [sem(f"nat_full{i}") for i in range(2)]
        nat_free = [sem(f"nat_free{i}") for i in range(2)]
        byk_full = [sem(f"byk_full{i}") for i in range(3)]
        pv_full = sem("pv_full")
        yT_ready = sem("yT_ready")
        xin_ready = sem("xin_ready"); xb_ready = sem("xb_ready")
        split = {"q": sem("split_q"), "k": sem("split_k")}
        stored = {k: sem(f"stored_{k}") for k in ("sq", "cq", "k")}
        stored["sk"] = stored["ck"] = stored["k"]
        stacked = {k: sem(f"stacked_{k}") for k in ("sq", "sk", "cq", "ck")}
        v_ready = sem("v_ready")
        mp_ready = sem("mp_ready")
        m_stored = sem("m_stored"); m_rows = sem("m_rows")
        exp_ready = sem("exp_ready")
        x1_ready = sem("x1_ready"); x1b_ready = sem("x1b_ready"); x2_ready = sem("x2_ready")
        x2_free = sem("x2_free")
        var_ready = sem("var_ready"); rstd_ready = sem("rstd_ready"); lnv_ready = sem("lnv_ready")
        dve_seq = sem("dve_seq"); pool_seq = sem("pool_seq")

        def unit(step, layer, b):
            return step * 4 + (b if layer == "s" else 2 + b)

        EXP0, PV0, YT0 = 3, 2, 1

        def q_splits(step, layer, b=0):
            return (step * 3 + (0 if layer == "s" else 1 + b)) * C

        def k_splits(step, layer):
            return (step * 2 + (0 if layer == "s" else 1)) * C

        def norms_before(step, layer, b):
            return step * 6 + (b if layer == "s" else 2 + 2 * b)

        def walk(handlers, fori):
            def run(plan, phase, step, following):
                for seg in plan:
                    f = handlers.get(seg[0])
                    if f is not None:
                        f(phase, seg, following if for_next(seg) else step, *seg[1:])
            run(PROLOGUE, ("pro", 0), None, 0)
            with fori(0, STEPS - 1) as it:
                if "begin" in handlers:
                    handlers["begin"]()
                run(LOOP, ("loop", it), it, it + 1)
            if "begin" in handlers:
                handlers["begin"]()
            run(EPILOGUE, ("epi", 0), STEPS - 1, None)

        def emptied(eng, phase, seg, *jobs):
            for j in jobs:
                b, n = turns.at(phase, seg, j)
                eng.wait_ge(work_free[b], n + 1)

        banks8 = [*work, *nat, *byk, pv]

        def experts(eng, pair):
            pair(0, False)
            with eng.Fori(1, E // 2 - 1) as it:
                pair(it, False)
            pair(E // 2 - 1, True)

        def ex_result(eng, job, it):
            b, n = expert_turn(job, it)
            eng.wait_ge(ex_free[b], n + 1)

        block = ctx.enter_context(nc.Block())

        @block.sync
        def _(sp):
            x_v = a["x"].rearrange("b (t p) d -> p (b t) d", p=P)
            sp.dma_start(xin[:, :, :], x_v[:, 0:TT, :]).then_inc(x_in, 16)
            wload = arena[:, 0:6 * D].rearrange("p (m d) -> p m d", m=6)
            sp.dma_start(wload, a["L0_attn_Wqkv"].rearrange("(m p) d -> p m d", p=P)).then_inc(w_in, 16)
            sp.dma_start(arena[:, 6 * D:8 * D].rearrange("p (m d) -> p m d", m=2),
                         a["L0_attn_Wo"].rearrange("(m p) d -> p m d", p=P)).then_inc(w_in, 16)
            sp.dma_start(bias_rows[0:2 * C, :], a["L0_attn_bqkv"][0:2 * D].rearrange("(m p) -> m p", p=P)).then_inc(w_in, 16)
            for n, b_in in enumerate("qk"):
                sp.dma_start(bias_rows[(2 + n) * C:(3 + n) * C, :], a[f"L0_xattn_b{b_in}"].rearrange("(m p) -> m p", p=P))\
                    .then_inc(w_in, 16)
            for dst, src in ((bv["s"], a["L0_attn_bqkv"][2 * D:3 * D]), (bv["c"], a["L0_xattn_bv"]), (bo, a["L0_attn_bo"]),
                             (gamma, a["L0_xattn_gamma"]), (beta, a["L0_xattn_beta"])):
                sp.dma_start(dst[:, :], src.partition_broadcast(P)).then_inc(w_in, 16)
            for i in range(1, STEPS):
                sp.dma_start(xres[:, i * TT:(i + 1) * TT, :], x_v[:, i * TT:(i + 1) * TT, :]).then_inc(x_in, 16)
            for n in "qkv":
                sp.dma_start(wc[n][:, :, :], a[f"L0_xattn_W{n}"].rearrange("(c p) n -> p c n", p=P)).then_inc(w_in2, 16)
            sp.dma_start(wr[:, :, :], a["L0_ffn_w_router"].rearrange("(c p) e -> p c e", p=P)).then_inc(w_in2, 16)
            sp.wait_ge(zeros_ready, 1)
            sp.dma_start(x_dram.rearrange("(p n) (a d) -> p (n a) d", p=P, a=2),
                         zeros[:, :].unsqueeze(1).broadcast_to([P, E * SLOTS // P * 2, D // 2])).then_inc(cleared, 16)
            sp.dma_start(y_dram[E * SLOTS:E * SLOTS + 1, :].rearrange("o (a d) -> o a d", a=2),
                         zeros[0:1, :].unsqueeze(1).broadcast_to([1, 2, D // 2])).then_inc(cleared, 16)
            ctx_v = a["ctx_1024"].rearrange("b (t p) d -> p (b t) d", p=P)
            part_v = {k: v.rearrange("(h r) s t -> r s h t", r=HD) for k, v in part_dram.items()}

            def held(*values):
                for v in values:
                    if v is not None and not isinstance(v, int):
                        sp.compute_val(v)
                return values

            def stack_side(layer, side, step, n_split, n_loads, tokens, free):
                key = layer + side
                *is_split, is_stored, is_free = held(*(n_split + c + 1 for c in range(C)), (n_loads + 1) * (C * 16), free)
                t0, t1 = tokens
                if is_free is not None:
                    sp.wait_ge(pv_full, is_free)
                for c in range(C):
                    sp.wait_ge(split[side], is_split[c])
                    sp.dma_start(part_dram[key][c * P:(c + 1) * P, :, t0:t1], parts[key][:, c, :, t0:t1]).then_inc(stored[key], 16)
                sp.wait_ge(stored[key], is_stored)
                slots = Q_SLOTS if side == "q" else K_SLOTS
                for i, part in enumerate(slots):
                    sp.dma_start(stack[key][i * HD:(i + 1) * HD, :, t0:t1], part_v[key][:, part, :, t0:t1])\
                        .then_inc(stacked[key], 16)

            def last_use(layer, step):
                if isinstance(step, int) and step == 0:
                    return None
                return PV0 + (unit(step, layer, 1) - 4 + 1) * G

            def SX(ph, seg, step):
                sp.dma_start(ctxin[:, :, :], ctx_v[:, bass.ds(step * TT, TT), :]).then_inc(ctx_in, 16)

            def SL(ph, seg, step):
                stack_side("s", "q", step, q_splits(step, "s"), step, (0, ST), last_use("s", step))

            def KS(ph, seg, step):
                if isinstance(step, int):
                    emptied(sp, ph, ("W",), 6, 7)
                stack_side("s", "k", step, k_splits(step, "s"), step * 2, (0, ST), last_use("s", step))

            def KL(ph, seg, step):
                stack_side("c", "k", step, k_splits(step, "c"), step * 2 + 1, (0, ST), last_use("c", step))

            def CS(ph, seg, step, layer, b):
                stack_side("c", "q", step, q_splits(step, "c", b), step * STEP_B + b, (b * T, (b + 1) * T),
                           PV0 + (unit(step, "s", 0) + 1) * G)

            def M(ph, seg, step, layer, b):
                were_loaded, are_stored = held(unit(step, layer, b) * 16, unit(step, layer, b) * 16 + 16)
                emptied(sp, ph, seg, 0)
                wait(sp, m_rows, were_loaded)
                sp.dma_start(m_dram.rearrange("m h t -> (m h) t"), mT[:, :]).then_inc(m_stored, 16)
                sp.wait_ge(m_stored, are_stored)
                sp.dma_start(stack[layer + "q"][KR:KR + MR, :, b * T:(b + 1) * T], m_dram).then_inc(m_rows, 16)

            walk({"SX": SX, "SL": SL, "KS": KS, "KL": KL, "CS": CS, "M": M}, sp.Fori)

            sp.wait_ge(pv_full, PV0 + 2 * B * G)
            wi_v = a["L0_ffn_wi"].rearrange("e (c p) f -> p e c f", p=P)
            wo_v = a["L0_ffn_wo"].rearrange("e (c p) d -> p e c d", p=P)

            def load_weights(e, i):
                sp.dma_start(wi[i], wi_v[:, bass.ds(e, 1), :, :].rearrange("p e c f -> p (e c) f")).then_inc(wi_in[i], 16)
                sp.dma_start(wo[i], wo_v[:, bass.ds(e, 1), :, :].rearrange("p e c f -> p (e c) f")).then_inc(wo_in[i], 16)

            def load_tokens(e, i):
                sp.dma_start(xe[i][:, 0:FULL, :], x_dram[bass.ds(e * SLOTS, FULL * P), :].rearrange("(t p) d -> p t d", p=P))\
                    .then_inc(xe_in[i], 16)
                sp.dma_start(xe[i][0:REST, FULL, :], x_dram[bass.ds(e * SLOTS + FULL * P, REST), :]).then_inc(xe_in[i], 16)

            for i in range(2):
                load_weights(i, i)
            sp.wait_ge(put_done, NT * TOPK * 16)
            for i in range(2):
                load_tokens(i, i)

            def pair(it, last):
                for i in range(2):
                    e = it * 2 + i
                    for n in range(FULL + 1):
                        ex_result(sp, ("y", i, n), it)
                    sp.dma_start(y_dram[bass.ds(e * SLOTS, FULL * P), :].rearrange("(t p) d -> p t d", p=P),
                                 ye[i][:, 0:FULL * D].rearrange("p (t d) -> p t d", t=FULL)).then_inc(y_stored[i], 16)
                    for n in range(2):
                        sp.dma_start(y_dram[bass.ds(e * SLOTS + FULL * P, REST), n * P:(n + 1) * P],
                                     ye[i][n * REST:(n + 1) * REST, FULL * D:YE]).then_inc(y_stored[i], 16)
                    if not last:
                        load_tokens(e + 2, i)
                        load_weights(e + 2, i)

            experts(sp, pair)
            out_v = out.rearrange("b (t p) d -> p (b t) d", p=P)
            for n in range(STEPS):
                sp.wait_ge(out_ready, n + 1)
                sp.dma_start(out_v[:, n * TT:(n + 1) * TT, :], xres[:, n * TT:(n + 1) * TT, :]).then_inc(out_stored, 16)
            sp.wait_ge(out_stored, 16 * STEPS)

        @block.tensor
        def _(pe):
            def work_job(phase, seg, j, emit):
                b, n = turns.at(phase, seg, j)
                wait(pe, work_free[b], n)
                emit(work[b]).then_inc(work_full[b], 1)

            def transposes(bank, srcs):
                for i, src in enumerate(srcs):
                    last = nc.tensor.transpose(bank[:, i * P:(i + 1) * P], src, ident[:, :])
                return last

            def by_feature(bank, w, m):
                for c in range(C):
                    last = nc.tensor.matmul(bank[:, :], w[:, c, m * P:(m + 1) * P], xT[:, c, :], start=(c == 0), stop=(c == C - 1))
                return last

            def by_token(bank, w, t0):
                for t in range(2):
                    for c in range(C):
                        last = nc.tensor.matmul(bank[:, t * D:(t + 1) * D], xT[:, c, (t0 + t) * P:(t0 + t + 1) * P], w[:, c, :],
                                                start=(c == 0), stop=(c == C - 1))
                return last

            def chunks_in(phase, seg, src):
                for c in range(C):
                    work_job(phase, seg, c, lambda bank: transposes(bank, [src[:, t, c * P:(c + 1) * P] for t in range(TT)]))

            pe.wait_ge(consts, 1)
            pe.wait_ge(w_in, 16 * W_LOADS)
            for m in range(8):
                work_job(("pro", 0), ("W",), m,
                         lambda bank: transposes(bank, [arena[:, m * D + c * P:m * D + (c + 1) * P] for c in range(C)]))

            work_job(("pro", 0), ("W",), 8, lambda bank: nc.tensor.transpose(bank[:, 0:4 * C], bias_rows[:, :], ident[0:4 * C, 0:4 * C]))

            def SX(ph, seg, step):
                if isinstance(step, int):
                    pe.wait_ge(x_in, 16)
                else:
                    pe.wait_ge(xin_ready, step)
                chunks_in(ph, seg, xin)

            def SQ(ph, seg, step):
                if isinstance(step, int):
                    emptied(pe, ph, ("W",), 6, 7)
                emptied(pe, ph, ("SX",), 0, 1)
                for m in range(C):
                    work_job(ph, seg, m, lambda bank: by_feature(bank, wqkvT, m))

            def SK(ph, seg, step):
                for m in range(C):
                    work_job(ph, seg, m, lambda bank: by_feature(bank, wqkvT, C + m))

            def SV(ph, seg, step):
                for n in range(2):
                    work_job(ph, seg, n, lambda bank: by_token(bank, wqkvT[:, :, 2 * D:3 * D], 2 * n))

            def KX(ph, seg, step):
                pe.wait_ge(ctx_in, (step + 1) * 16)
                chunks_in(ph, seg, ctxin)

            def CK(ph, seg, step):
                if isinstance(step, int):
                    pe.wait_ge(w_in2, 16 * 4)
                emptied(pe, ph, ("KX",), 0, 1)
                for m in range(C):
                    work_job(ph, seg, m, lambda bank: by_feature(bank, wc["k"], m))

            def CV(ph, seg, step):
                for n in range(2):
                    work_job(ph, seg, n, lambda bank: by_token(bank, wc["v"], 2 * n))

            def CX(ph, seg, step, layer, b):
                pe.wait_ge(x1_ready, step * STEP_B + b + 1)
                work_job(ph, seg, 0, lambda bank: transposes(
                    bank, [x1[:, b * QT + t, c * P:(c + 1) * P] for c in range(C) for t in range(QT)]))

            def CQ(ph, seg, step, layer, b):
                emptied(pe, ph, ("CX", "c", b), 0)

                def project(bank):
                    for m in range(C):
                        for c in range(C):
                            last = nc.tensor.matmul(bank[:, m * T:(m + 1) * T], wc["q"][:, c, m * P:(m + 1) * P], turned[:, c, :],
                                                    start=(c == 0), stop=(c == C - 1))
                    return last
                work_job(ph, seg, 0, project)

            def bank_scores(bank, full, mask, at, w, pairs):
                mw = mask.shape[2]
                nc.tensor.matmul(bank[:, 0:len(pairs) * w].rearrange("p (h t) -> p h t", t=w)[:, :, at:at + mw], identb[:, :],
                                 mask[:, :, :], start=True, stop=False, skip_group_check=True)
                for i, (lhsT, rhs) in enumerate(pairs):
                    last = nc.tensor.matmul(bank[:, i * w:(i + 1) * w], lhsT, rhs, start=False, stop=(i == len(pairs) - 1),
                                            skip_group_check=True)
                last.then_inc(full, 1)

            def N(ph, seg, step, layer, b, g):
                q, k = stack[layer + "q"], stack[layer + "k"]
                if g == 0 and layer == "c":
                    pe.wait_ge(stacked["cq"], (step * STEP_B + b + 1) * (6 * 16))
                if b == 0 and g == 0:
                    if layer == "s":
                        pe.wait_ge(stacked["sq"], (step + 1) * (6 * 16))
                    pe.wait_ge(stacked[layer + "k"], (step + 1) * (6 * 16))
                U = unit(step, layer, b)
                t0 = b * T
                n1 = KEYS0[layer]
                k1 = t0 + T - n1
                banks = [(mq0[layer], 0, range(4 * g, 4 * g + 4), t0, t0, P)]
                banks += [(mq1[layer], n1 - mq1[layer].shape[2], range(4 * g + 2 * n, 4 * g + 2 * n + 2), t0 + P, k1, n1) for n in range(2)]
                for i, (mask, at, heads, q0, k0, w) in enumerate(banks):
                    job = 3 * g + i
                    wait(pe, nat_free[job % 2], U * 6 + job // 2)
                    bank_scores(nat[job % 2], nat_full[job % 2], mask, at, w,
                                [(q[0:KR, h, q0:q0 + P], k[0:KR, h, k0:k0 + w]) for h in heads])

            def M(ph, seg, step, layer, b):
                pe.wait_ge(mp_ready, unit(step, layer, b) + 1)

                def rows(bank):
                    o = bank[:, :].bitcast(BF16)
                    for t in range(QT):
                        last = nc.tensor.transpose(o[:, t * P:(t + 1) * P], mp[:, t, :], identb[:, :])
                    return last
                work_job(ph, seg, 0, rows)

            def product_v(ph, step, U, layer, b, g):
                pe.wait_ge(exp_ready, EXP0 + U * (3 * G) + 3 * g + 3)
                if g == 0 and layer == "c":
                    pe.wait_ge(v_ready, (step + 1) * 2)
                pe.wait_ge(yT_ready, YT0 - 1 + U * G + g + 1)
                for kt in range(QT):
                    for j in range(4):
                        h = 4 * g + j
                        cols, src = ((0, KEYS0[layer]), (0, KEYS0[layer])) if kt == 0 else ((P, T), (256, 384))
                        last = nc.tensor.matmul(pv[32 * j:32 * j + 32, cols[0]:cols[1]], vone[layer][:, b * QT + kt, h, :],
                                                probs[:, g % 2, j, src[0]:src[1]], start=(kt == 0), stop=(kt == QT - 1),
                                                skip_group_check=True)
                last.then_inc(pv_full, 1)

            def T_(ph, seg, step, layer, b, g):
                q, k = stack[layer + "q"], stack[layer + "k"]
                U = unit(step, layer, b)
                if g == 0:
                    pe.wait_ge(m_rows, U * 16 + 16)
                    pe.wait_ge(ones_ready, 1 if layer == "s" else 2)
                t0, n0 = b * T, KEYS0[layer]
                banks = [(mk0[layer], range(4 * g + 2 * n, 4 * g + 2 * n + 2), t0, t0, n0) for n in range(2)]
                banks.append((mk1[layer], range(4 * g, 4 * g + 4), t0 + P, t0 + P, P))
                for i, (mask, heads, k0, q0, w) in enumerate(banks):
                    job = 3 * g + i
                    if ph[0] == "epi" and (layer, b, g, i) == ("c", 0, 1, 0):
                        pe.wait_ge(routed, 1)
                    pe.wait_ge(exp_ready, EXP0 + U * (3 * G) + job - 2)
                    bank_scores(byk[i], byk_full[i], mask, 0, w,
                                [(k[0:KR + MR, h, k0:k0 + P], q[0:KR + MR, h, q0:q0 + w]) for h in heads])
                if g > 0:
                    product_v(ph, step, U, layer, b, g - 1)
                if g == G - 1:
                    product_v(ph, step, U, layer, b, g)

            def Y1(ph, seg, step, layer, b):
                U = unit(step, layer, b)
                pe.wait_ge(yT_ready, YT0 + (U + 1) * G)
                for t in range(QT):
                    work_job(ph, seg, t, lambda bank: transposes(bank, [yT[:, g, t * P:(t + 1) * P] for g in range(G)]))
                if layer == "c":
                    work_job(ph, seg, QT, lambda bank: transposes(
                        bank, [fq["c"][:, c, b * T + t * P:b * T + (t + 1) * P] for t in range(QT) for c in range(C)]))

            def Y2(ph, seg, step, layer, b):
                emptied(pe, ph, ("Y1", "s", b), 0, 1)
                work_job(ph, seg, 0, lambda bank: transposes(
                    bank, [ynat[:, t, c * P:(c + 1) * P] for c in range(C) for t in range(QT)]))

            def Y3(ph, seg, step, layer, b):
                emptied(pe, ph, ("Y2", "s", b), 0)

                def project(bank):
                    for t in range(QT):
                        for c in range(C):
                            last = nc.tensor.matmul(bank[:, t * D:(t + 1) * D], turned[:, c, t * P:(t + 1) * P], woT[:, c, :],
                                                    start=(c == 0), stop=(c == C - 1))
                    return last
                work_job(ph, seg, 0, project)

            def RX(ph, seg, step, layer, b):
                pe.wait_ge(x2_ready, step * STEP_B + b + 1)
                work_job(ph, seg, 0, lambda bank: transposes(
                    bank, [x2[:, t, c * P:(c + 1) * P] for c in range(C) for t in range(QT)]))

            def R(ph, seg, step, layer, b):
                emptied(pe, ph, ("RX", "c", b), 0)

                def router(bank):
                    for t in range(QT):
                        for c in range(C):
                            last = nc.tensor.matmul(bank[:, t * 8:(t + 1) * 8], turned[:, c, t * P:(t + 1) * P], wr[:, c, :],
                                                    start=(c == 0), stop=(c == C - 1))
                    return last
                work_job(ph, seg, 0, router)

            pe.wait_ge(consts, 2)
            def G_(ph, seg, step, n):
                pe.wait_ge(choice_ready, n + 1)
                if n == 0:
                    pe.wait_ge(exp_ready, EXP0 + (2 * B - 2) * (3 * G) + 1)
                else:
                    pe.wait_ge(exp_ready, EXP0 + 2 * B * 3 * G)
                picked = choice[:, n * NG:(n + 1) * NG]
                nc.tensor.matmul(byk[n][:, 0:NG], tri[:, :], picked, start=True, stop=True)
                nc.tensor.matmul(byk[n][:, NG:2 * NG], onesb[:, :], picked, start=False, stop=True, skip_group_check=True)\
                    .then_inc(counted, 1)

            pe.sem_inc(pv_full, PV0)
            walk({"SX": SX, "SQ": SQ, "SK": SK, "SV": SV, "KX": KX, "CK": CK, "CV": CV, "CX": CX, "CQ": CQ, "N": N, "M": M,
                  "T": T_, "Y1": Y1, "Y2": Y2, "Y3": Y3, "RX": RX, "R": R, "G": G_}, pe.Fori)

            emptied(pe, ("epi", 0), ("RX", "c", 1), 0)
            emptied(pe, ("epi", 0), ("R", "c", 1), 0)
            pe.wait_ge(yT_ready, YT0 + 2 * B * G)
            pe.wait_ge(routed, GROUPS)

            def ex_job(job, it, emit):
                b, n = expert_turn(job, it)
                wait(pe, ex_free[b], n)
                emit(banks8[b]).then_inc(ex_full[b], 1)

            def tokens_T(i, it):
                pe.wait_ge(xe_in[i], it * 32 + 32)
                for c in range(C):
                    def emit(bank):
                        for t in range(FULL + 1):
                            n = P if t < FULL else REST
                            mm = nc.tensor.transpose(bank[:, t * P:t * P + n], xe[i][0:n, t, c * P:(c + 1) * P], ident[0:n, 0:n])
                        return mm
                    ex_job(("x", i, c), it, emit)

            def hidden(i, it):
                pe.wait_ge(wi_in[i], it * 16 + 16)
                for f in range(FC):
                    def emit(bank):
                        for c in range(C):
                            mm = nc.tensor.matmul(bank[:, 0:SLOTS], wi[i][:, c, f * P:(f + 1) * P], xeT[i][:, c, :],
                                                  start=(c == 0), stop=(c == C - 1))
                        return mm
                    ex_job(("h", i, f), it, emit)

            def output(i, it):
                pe.wait_ge(wo_in[i], it * 16 + 16)
                for f in range(FC):
                    ex_result(pe, ("h", i, f), it)
                for t in range(FULL):
                    def emit(bank):
                        for f in range(FC):
                            mm = nc.tensor.matmul(bank[:, 0:D], hT[i][:, f, t * P:(t + 1) * P], wo[i][:, f, :],
                                                  start=(f == 0), stop=(f == FC - 1))
                        return mm
                    ex_job(("y", i, t), it, emit)

                def rest(bank):
                    for f in range(FC):
                        for n in range(2):
                            mm = nc.tensor.matmul(bank[n * REST:(n + 1) * REST, 0:P], hT[i][:, f, FULL * P:SLOTS],
                                                  wo[i][:, f, n * P:(n + 1) * P], start=(f == 0), stop=(f == FC - 1),
                                                  skip_group_check=True)
                    return mm
                ex_job(("y", i, FULL), it, rest)

            def pair(it, last):
                for i in range(2):
                    for c in range(C):
                        ex_result(pe, ("x", i, c), it)
                    hidden(i, it)
                    if not (last and i == 1):
                        tokens_T(1 - i, it + i)
                    output(i, it)

            tokens_T(0, 0)
            experts(pe, pair)

        @block.scalar
        def _(act):
            nc.scalar.preload_act_table_set("natural_log_exp_and_others")
            def take(phase, seg, j, emit):
                b, n = turns.at(phase, seg, j)
                act.wait_ge(work_full[b], n + 1)
                return emit(work[b]).then_inc(work_free[b], 1)

            def copy_out(phase, seg, j, dst, cols=512):
                take(phase, seg, j, lambda bank: nc.scalar.activation(dst, bank[:, 0:cols] if dst.ndim == 2 else
                     bank[:, 0:cols].rearrange("p (a b) -> p a b", a=dst.shape[1]), ACT.Copy))

            def xT_out(ph, seg):
                for c in range(C):
                    copy_out(ph, seg, c, xT[:, c, :])

            def f_out(phase, seg, j, dst, part, func, bias, scale):
                def emit(bank):
                    nc.scalar.activation(dst, bank[:, :], func, bias=bias, scale=scale)
                    return nc.scalar.activation(part, bank[:, :], func, bias=bias, scale=scale)
                take(phase, seg, j, emit)

            for m in range(8):
                dst = wqkvT[:, :, m * P:(m + 1) * P] if m < 6 else woT[:, :, (m - 6) * P:(m - 5) * P]
                copy_out(("pro", 0), ("W",), m, dst, cols=2 * P)

            def SX(ph, seg, step):
                xT_out(ph, seg)

            def SQ(ph, seg, step):
                if isinstance(step, int):
                    emptied(act, ph, ("W",), 8)
                    act.wait_ge(consts, 2)
                for m in range(C):
                    f_out(ph, seg, m, fq["s"][:, m, :], parts["sq"][:, m, 0, :], ACT.Identity, bias[:, 0, m:m + 1], 0.25)

            def SK(ph, seg, step):
                wait(act, stored["k"], step * 2 * (C * 16))
                for m in range(C):
                    f_out(ph, seg, m, fk[:, m, :], parts["sk"][:, m, 0, :], ACT.Identity, bias[:, 0, C + m:C + m + 1], 1.0)

            def KX(ph, seg, step):
                xT_out(ph, seg)

            def CK(ph, seg, step):
                act.wait_ge(stored["k"], (step * 2 + 1) * (C * 16))
                for m in range(C):
                    f_out(ph, seg, m, fk[:, m, :], parts["ck"][:, m, 0, :], ACT.Relu, bias[:, 1, C + m:C + m + 1], 1.0)

            def to_turned(ph, seg, step, layer, b):
                copy_out(ph, seg, 0, turned[:, :, :])

            def CQ(ph, seg, step, layer, b):
                def emit(bank):
                    t = slice(b * T, (b + 1) * T)
                    for m in range(C):
                        act_in = bank[:, m * T:(m + 1) * T]
                        nc.scalar.activation(fq["c"][:, m, t], act_in, ACT.Relu, bias=bias[:, 1, m:m + 1], scale=0.25)
                        last = nc.scalar.activation(parts["cq"][:, m, 0, t], act_in, ACT.Relu, bias=bias[:, 1, m:m + 1], scale=0.25)
                    return last
                take(ph, seg, 0, emit)

            def M(ph, seg, step, layer, b):
                U = unit(step, layer, b)
                wait(act, m_stored, U * 16)
                take(ph, seg, 0, lambda bank: nc.scalar.activation(mT[:, :], bank[0:MR * H, :].bitcast(BF16)[:, 0:T], ACT.Copy))

            def yT_out(U, g):
                act.wait_ge(pv_full, PV0 + U * G + g + 1)
                nc.scalar.activation(yT[:, g, :], pv[:, 0:T], ACT.Copy).then_inc(yT_ready, 1)

            def T_(ph, seg, step, layer, b, g):
                U = unit(step, layer, b)
                n0 = KEYS0[layer]
                act.wait_ge(pv_full, PV0 + U * G + g - 1)
                for i in range(3):
                    act.wait_ge(byk_full[i], U * G + g + 1)
                    if i < 2:
                        dst, src = probs[:, g % 2, 2 * i:2 * i + 2, 0:n0], byk[i][:, 0:2 * n0].rearrange("p (a b) -> p a b", a=2)
                    else:
                        dst, src = probs[:, g % 2, :, 256:384], byk[i][:, :].rearrange("p (a b) -> p a b", a=4)
                    nc.scalar.activation(dst, src, ACT.Exp).then_inc(exp_ready, 1)
                if g > 0:
                    yT_out(U, g - 1)
                if g == G - 1:
                    yT_out(U, g)

            def rstd_of(number, y=rstd[:, :], variance=mv[:, :, 1], log=lnv[:, :]):
                act.wait_ge(var_ready, number + 1)
                nc.scalar.activation(log, variance, ACT.Ln, bias=eps[:, :]).then_inc(lnv_ready, 1)
                act.wait_ge(lnv_ready, number + 1)
                nc.scalar.activation(y, log, ACT.Exp, scale=-0.5).then_inc(rstd_ready, 1)

            def L3(ph, seg, step, layer, b):
                rstd_of(norms_before(step, layer, b))

            def L1(ph, seg, step, layer, b):
                rstd_of(norms_before(step, layer, b))

            def L2(ph, seg, step, layer, b):
                rstd_of(norms_before(step, layer, b) + 1)

            def G_(ph, seg, step, n):
                act.wait_ge(diff_ready, n + 1)
                nc.scalar.activation(expd[:, n * GT:(n + 1) * GT, :], diff[:, n * GT:(n + 1) * GT, :], ACT.Exp).then_inc(expd_ready, 1)

            act.sem_inc(exp_ready, EXP0)
            act.sem_inc(yT_ready, YT0)
            walk({"SX": SX, "SQ": SQ, "SK": SK, "KX": KX, "CK": CK, "CX": to_turned, "CQ": CQ, "M": M, "T": T_, "L1": L1, "L2": L2, "L3": L3,
                  "Y2": to_turned, "RX": to_turned, "G": G_}, act.Fori)

            def ex_take(job, it, emit):
                b, n = expert_turn(job, it)
                act.wait_ge(ex_full[b], n + 1)
                emit(banks8[b]).then_inc(ex_free[b], 1)

            def tokens_T(i, it):
                if i == 0 and isinstance(it, int) and it == 0:
                    act.wait_ge(routed, GROUPS)
                for c in range(C):
                    ex_take(("x", i, c), it, lambda bank: nc.scalar.activation(xeT[i][:, c, :], bank[:, 0:SLOTS], ACT.Copy))

            def pair(it, last):
                for i in range(2):
                    for f in range(0, FC, 2):
                        ex_take(("h", i, f), it, lambda bank: nc.scalar.activation(hT[i][:, f, :], bank[:, 0:SLOTS], ACT.Relu))
                    if not (last and i == 1):
                        tokens_T(1 - i, it + i)
                    wait(act, y_stored[i], it * 48)
                    ex_take(("y", i, 1), it, lambda bank: nc.scalar.activation(ye[i][:, D:2 * D], bank[:, 0:D], ACT.Copy))

            tokens_T(0, 0)
            experts(act, pair)

            for n in range(STEPS):
                t = slice(n * TT, (n + 1) * TT)
                rstd_of(6 * STEPS + n, last_rstd[:, t], last_mv[:, t, 1], last_log[:, t])

        @block.vector
        def _(dve):
            V = nc.vector
            seq = [0]

            def link(ins):
                seq[0] += 1
                ins.then_inc(dve_seq, 1)
                dve.wait_ge(dve_seq, seq[0])

            def begin():
                seq[0] = 0
                dve.sem_clear(dve_seq)

            def split23(dst, f, rest, last_sem, before):
                wait(dve, last_sem, before)
                link(V.tensor_tensor(rest, f, dst[0], ALU.subtract))
                link(V.tensor_copy(dst[1], rest))
                V.tensor_tensor(dst[2], rest, dst[1], ALU.subtract).then_inc(last_sem, 1)

            bk, n = turns.at(("pro", 0), ("W",), 8)
            dve.wait_ge(work_full[bk], n + 1)
            by_col = work[bk][:, 0:4 * C].rearrange("p (l m) -> p l m", l=2)
            V.tensor_scalar(bias[:, :, 0:C], by_col[:, :, 0:C], 0.25, None, ALU.mult)
            V.tensor_copy(bias[:, :, C:2 * C], by_col[:, :, C:2 * C]).then_inc(work_free[bk], 1)
            dve.wait_ge(w_in, 16 * W_LOADS)

            def v_out(ph, seg, j0, layer, step):
                if not isinstance(step, int):
                    dve.wait_ge(pv_full, PV0 + (unit(step, layer, 1) - 4 + 1) * G)
                for n in range(2):
                    b, cnt = turns.at(ph, seg, j0 + n)
                    dve.wait_ge(work_full[b], cnt + 1)
                    v = vone[layer][:, 2 * n:2 * n + 2, :, 0:HD]
                    bvb = bv[layer][:, :].unsqueeze(1).broadcast_to([P, 2, D]).rearrange("p t (h d) -> p t h d", h=H)
                    src = work[b][:, :].rearrange("p (t h d) -> p t h d", t=2, h=H)
                    if layer == "s":
                        V.tensor_tensor(v, src, bvb, ALU.add).then_inc(work_free[b], 1)
                    else:
                        V.tensor_tensor(v, src, bvb, ALU.add).then_inc(work_free[b], 1)
                        emptied(dve, ph, seg, j0 + n)
                        V.tensor_scalar(v, v, 0.0, None, ALU.max).then_inc(v_ready, 1)

            def SS(ph, seg, step):
                for m in range(C):
                    emptied(dve, ph, ("SQ",), m)
                    split23([parts["sq"][:, m, i, :] for i in range(3)], fq["s"][:, m, :], resq[:, :], split["q"],
                            q_splits(step, "s") + m)

            def SV(ph, seg, step):
                v_out(ph, seg, 0, "s", step)

            def CV(ph, seg, step):
                v_out(ph, seg, 0, "c", step)

            def KS(ph, seg, step):
                if isinstance(step, int):
                    for m in range(C):
                        emptied(dve, ph, ("SK",), m)
                        if m == 0:
                            dve.wait_ge(split["q"], C)
                        split23([parts["sk"][:, m, i, :] for i in range(3)], fk[:, m, :], resq[:, :], split["k"], m)

            def CS(ph, seg, step, layer, b):
                emptied(dve, ph, ("CQ", "c", b), 0)
                t = slice(b * T, (b + 1) * T)
                for m in range(C):
                    split23([parts["cq"][:, m, i, t] for i in range(3)], fq["c"][:, m, t], resq[:, 0:T], split["q"],
                            q_splits(step, "c", b) + m)

            def N(ph, seg, step, layer, b, g):
                U = unit(step, layer, b)
                for i in range(3):
                    job = 3 * g + i
                    bank = nat[job % 2]
                    dve.wait_ge(nat_full[job % 2], U * 6 + job // 2 + 1)
                    if i == 0:
                        dst, src = negm[:, 0, 4 * g:4 * g + 4], bank[:, :].rearrange("p (h k) -> p h k", h=4)
                    else:
                        w = KEYS0[layer]
                        dst = negm[:, 1, 4 * g + 2 * i - 2:4 * g + 2 * i]
                        src = bank[:, 0:2 * w].rearrange("p (h k) -> p h k", h=2)
                    V.tensor_reduce(dst, src, AX, ALU.max, negate=True).then_inc(nat_free[job % 2], 1)
                if g == G - 1:
                    for n in range(2):
                        dve.wait_ge(nat_free[n], (U + 1) * 6)
                    wait(dve, m_stored, U * 16)
                    link(V.tensor_copy(mp[:, :, 0:H], negm[:, :, :]))
                    split23([mp[:, :, i * H:(i + 1) * H] for i in range(3)], negm[:, :, :], rm[:, :, :], mp_ready, U)

            def moments():
                for t in range(QT):
                    i = V.bn_stats(stats[:, t, :], r[:, t, :])
                link(i)
                for t in range(QT):
                    i = V.bn_aggr(mv[:, t, :], stats[:, t, :])
                i.then_inc(var_ready, 1)

            def newton_step(y, variance, tmp):
                link(V.tensor_tensor(tmp, y, y, ALU.mult))
                link(V.scalar_tensor_tensor(out=tmp, in0=variance, scalar=EPS, in1=tmp, op0=ALU.add, op1=ALU.mult))
                link(V.tensor_scalar(tmp, tmp, -0.5, 1.5, ALU.mult, ALU.add))
                link(V.tensor_tensor(y, y, tmp, ALU.mult))

            def refine(number):
                dve.wait_ge(rstd_ready, number + 1)
                newton_step(rstd[:, :], mv[:, :, 1], newton[:, :])

            def scaled(number, dst_of, last):
                refine(number)
                for t in range(QT):
                    i = V.tensor_scalar(dst_of(t), r[:, t, :], mv[:, t, 0:1], rstd[:, t:t + 1], ALU.subtract, ALU.mult)
                last(i)

            def Y1(ph, seg, step, layer, b):
                for t in range(QT):
                    bk, n = turns.at(ph, seg, t)
                    dve.wait_ge(work_full[bk], n + 1)
                    y = work[bk][:, :].rearrange("p (h d) -> p h d", h=H)
                    link(V.reciprocal(rec[:, t, :], y[:, :, HD]))
                    V.tensor_tensor(ynat[:, t, :].rearrange("p (h d) -> p h d", h=H), y[:, :, 0:HD],
                                        rec[:, t, :].unsqueeze(2).broadcast_to([P, H, HD]), ALU.mult).then_inc(work_free[bk], 1)
                emptied(dve, ph, seg, 0, 1)
                if layer == "s":
                    return
                bk, n = turns.at(ph, seg, QT)
                dve.wait_ge(work_full[bk], n + 1)
                V.scalar_tensor_tensor(out=r[:, :, :], in0=work[bk][:, :].rearrange("p (t d) -> p t d", t=QT), scalar=4.0,
                                       in1=ynat[:, :, :], op0=ALU.mult, op1=ALU.add).then_inc(work_free[bk], 1)
                emptied(dve, ph, seg, QT)
                moments()
                dve.wait_ge(var_ready, norms_before(step, layer, b) + 1)
                for t in range(QT):
                    i = V.scalar_tensor_tensor(out=r[:, t, :], in0=r[:, t, :], scalar=mv[:, t, 0:1], in1=gamma[:, :],
                                               op0=ALU.subtract, op1=ALU.mult)
                link(i)

            def L1(ph, seg, step, layer, b):
                refine(norms_before(step, layer, b))
                dve.wait_ge(x1b_ready, step * STEP_B + b + 1)
                for t in range(QT):
                    i = V.scalar_tensor_tensor(out=r[:, t, :], in0=r[:, t, :], scalar=rstd[:, t:t + 1], in1=x1[:, b * QT + t, :],
                                               op0=ALU.mult, op1=ALU.add)
                link(i)
                moments()

            def L2(ph, seg, step, layer, b):
                dve.wait_ge(x2_free, step * STEP_B + b + 1)
                scaled(norms_before(step, layer, b) + 1, lambda t: x2[:, t, :], lambda i: i.then_inc(x2_ready, 1))

            def Y3(ph, seg, step, layer, b):
                bk, n = turns.at(ph, seg, 0)
                dve.wait_ge(work_full[bk], n + 1)
                dve.wait_ge(xb_ready, step + 1)
                V.tensor_tensor(r[:, :, :], work[bk][:, :].rearrange("p (t d) -> p t d", t=QT), xb[:, b * QT:(b + 1) * QT, :],
                                ALU.add).then_inc(work_free[bk], 1)
                emptied(dve, ph, seg, 0)
                moments()

            def L3(ph, seg, step, layer, b):
                scaled(norms_before(step, layer, b), lambda t: x1[:, b * QT + t, :], lambda i: i.then_inc(x1_ready, 1))

            def R(ph, seg, step, layer, b):
                bk, n = turns.at(ph, seg, 0)
                dve.wait_ge(work_full[bk], n + 1)
                V.tensor_copy(logits[:, bass.ds((step * STEP_B + b) * QT, QT), :],
                              work[bk][:, 0:QT * 8].rearrange("p (t e) -> p t e", t=QT)).then_inc(work_free[bk], 1)

            def route(n):
                tiles = slice(n * GT, (n + 1) * GT)
                cols = slice(n * NG, (n + 1) * NG)
                count_cols = slice(0, NG), slice(NG, 2 * NG)
                for t in range(n * GT, (n + 1) * GT):
                    i = V.max(top[:, t, :], logits[:, t, :])
                link(i)
                V.tensor_tensor(diff[:, tiles, :], top[:, tiles, :], top[:, tiles, 0:1].broadcast_to([P, GT, 8]), ALU.subtract)\
                    .then_inc(diff_ready, 1)
                for t in range(n * GT, (n + 1) * GT):
                    i = V.max_index(topi[:, t, :], top[:, t, :], logits[:, t, :])
                link(i)
                link(V.tensor_copy(idxf[:, tiles, :], topi[:, tiles, 0:TOPK]))
                dve.wait_ge(consts, 2)
                by_choice = choice[:, cols].rearrange("p (e k t) -> p t e k", e=E, k=TOPK)
                for k in range(TOPK):
                    i = V.tensor_tensor(by_choice[:, :, :, k], iota_e[:, :].unsqueeze(1).broadcast_to([P, GT, E]),
                                        idxf[:, tiles, k].unsqueeze(2).broadcast_to([P, GT, E]), ALU.is_equal)
                i.then_inc(choice_ready, 1)
                for k in range(TOPK):
                    i = V.scalar_tensor_tensor(out=slot[:, n, k * GT:(k + 1) * GT], in0=idxf[:, tiles, k],
                                               scalar=float(SLOTS), in1=gbase[:, n, k * GT:(k + 1) * GT], op0=ALU.mult, op1=ALU.add)
                dve.wait_ge(counted, n + 1)
                upto, sums = (byk[n][:, c] for c in count_cols)
                link(V.tensor_tensor_scan(before[:, cols], goes_on[:, cols], sums, 0.0, ALU.mult, ALU.add))
                link(V.tensor_tensor(before[:, cols], before[:, cols], sums, ALU.subtract))
                link(V.tensor_tensor(before[:, cols], before[:, cols], upto, ALU.add))
                link(V.tensor_tensor(before[:, cols], before[:, cols], choice[:, cols], ALU.mult))
                link(V.tensor_reduce(pos[:, n, :], before[:, cols].rearrange("p (e kt) -> p kt e", e=E), AX, ALU.add))
                V.tensor_scalar(late[:, n, :], pos[:, n, :], float(CAP), BAD, ALU.is_gt, ALU.mult)
                link(V.tensor_tensor(slot[:, n, :], slot[:, n, :], pos[:, n, :], ALU.add))
                link(V.tensor_tensor(slot[:, n, :], slot[:, n, :], late[:, n, :], ALU.add))
                link(V.tensor_copy(put[:, n * TOPK * GT:(n + 1) * TOPK * GT], slot[:, n, :]))
                V.tensor_scalar(slot[:, n, :], slot[:, n, :], float(E * SLOTS), None, ALU.min).then_inc(routed, 1)
                dve.wait_ge(routed, n + 1)
                V.tensor_copy(get[:, n * TOPK * GT:(n + 1) * TOPK * GT], slot[:, n, :])
                dve.wait_ge(expd_ready, n + 1)
                link(V.tensor_reduce(esum[:, tiles], expd[:, tiles, :], AX, ALU.add))
                link(V.reciprocal(esum[:, tiles], esum[:, tiles]))
                V.tensor_tensor(gates[:, tiles, :], expd[:, tiles, 0:TOPK], esum[:, tiles].unsqueeze(2).broadcast_to([P, GT, TOPK]), ALU.mult)\
                    .then_inc(get_ready, 1)

            def G_(ph, seg, step, n):
                if n == 1:
                    emptied(dve, ph, ("R", "c", 1), 0)
                route(n)

            walk({"begin": begin, "SS": SS, "KS": KS, "SV": SV, "CV": CV, "CS": CS, "N": N, "Y1": Y1, "L1": L1, "L2": L2, "Y3": Y3, "L3": L3,
                  "R": R, "G": G_}, dve.Fori)

            def ex_take(job, it, emit):
                b, n = expert_turn(job, it)
                dve.wait_ge(ex_full[b], n + 1)
                emit(banks8[b]).then_inc(ex_free[b], 1)

            def pair(it, last):
                for i in range(2):
                    for f in range(1, FC, 2):
                        ex_take(("h", i, f), it, lambda bank: V.tensor_scalar(hT[i][:, f, :], bank[:, 0:SLOTS], 0.0, None, ALU.max))
                    wait(dve, y_stored[i], it * 48)
                    ex_take(("y", i, 0), it, lambda bank: V.tensor_copy(ye[i][:, 0:D], bank[:, 0:D]))
                    ex_take(("y", i, FULL), it, lambda bank: V.tensor_copy(ye[i][:, FULL * D:YE], bank[:, 0:P]))

            experts(dve, pair)

            def combine(n):
                dve.wait_ge(got_sem[n], TT * TOPK * 16)
                tiles = range(n * TT, (n + 1) * TT)
                for k in range(TOPK):
                    for t in tiles:
                        i = V.scalar_tensor_tensor(out=xres[:, t, :], in0=got[:, t * TOPK + k, :], scalar=gates[:, t, k:k + 1],
                                                   in1=xres[:, t, :], op0=ALU.mult, op1=ALU.add)
                    link(i)
                for t in tiles:
                    i = V.bn_stats(last_stats[:, t, :], xres[:, t, :])
                link(i)
                for t in tiles:
                    i = V.bn_aggr(last_mv[:, t, :], last_stats[:, t, :])
                i.then_inc(var_ready, 1)

            def finish(n):
                dve.wait_ge(rstd_ready, 6 * STEPS + n + 1)
                tiles = slice(n * TT, (n + 1) * TT)
                newton_step(last_rstd[:, tiles], last_mv[:, tiles, 1], last_newton[:, tiles])
                for t in range(n * TT, (n + 1) * TT):
                    i = V.tensor_scalar(xres[:, t, :], xres[:, t, :], last_mv[:, t, 0:1], last_rstd[:, t:t + 1], ALU.subtract, ALU.mult)
                i.then_inc(out_ready, 1)

            combine(0)
            for n in range(1, STEPS):
                combine(n)
                finish(n - 1)
            finish(STEPS - 1)

        @block.gpsimd
        def _(pool):
            g_ = nc.gpsimd
            seq = [0]

            def link(ins):
                seq[0] += 1
                ins.then_inc(pool_seq, 1)
                pool.wait_ge(pool_seq, seq[0])

            def begin():
                seq[0] = 0
                pool.sem_clear(pool_seq)

            g_.memset(ident[:, :], 0.0)
            link(g_.memset(identb[:, :], 0.0))
            g_.affine_select(out=identb[:, :], in_=identb[:, :], compare_op=ALU.not_equal, fill=1.0, base=0,
                             pattern=[[-1, P]], channel_multiplier=1)
            g_.affine_select(out=ident[:, :], in_=ident[:, :], compare_op=ALU.not_equal, fill=1.0, base=0,
                             pattern=[[-1, P]], channel_multiplier=1).then_inc(consts, 1)
            g_.memset(eps[:, :], EPS).then_inc(x2_free, 1)
            g_.memset(mp[:, :, :], 0.0)
            for layer in "sc":
                g_.memset(vone[layer][:, :, :, :], 1.0)
            masks = [mq0["s"], mq0["c"], mq1["s"], mq1["c"], mk0["s"], mk0["c"], mk1["s"], mk1["c"]]
            for m in masks:
                last = g_.memset(m[:, :, :], 0.0)
            link(last)

            def keep(m, base, cm, step):
                return g_.affine_select(out=m[:, :, :], in_=m[:, :, :], compare_op=ALU.is_ge, fill=NEG, base=base,
                                        pattern=[[0, m.shape[1]], [step, m.shape[2]]], channel_multiplier=cm)
            keep(mq0["s"], 0, 1, -1)
            keep(mq0["c"], 0, 1, -1)
            keep(mq1["s"], P - WIN, 1, -1)
            keep(mq1["c"], 0, 1, -1)
            keep(mk0["s"], 0, -1, 1)
            keep(mk0["c"], 0, -1, 1)
            keep(mk1["s"], 0, -1, 1)
            link(keep(mk1["c"], 0, -1, 1))
            keep(mq0["s"], WIN - 1, -1, 1)
            keep(mq1["s"], -1, -1, 1)
            keep(mk0["s"], WIN - 1, 1, -1)
            link(keep(mk1["s"], WIN - 1, 1, -1))
            g_.memset(zeros[:, :], 0.0)
            g_.memset(onesb[:, :], 1.0)
            g_.memset(tri[:, :], 1.0)
            g_.memset(goes_on[:, :], 1.0)
            for g in range(GROUPS):
                g_.memset(gbase[:, g, :], float(g * CAP - 1))
            link(g_.iota(iota_e[:, :], [[1, E]], base=0, channel_multiplier=0, allow_small_or_imprecise_dtypes=True))
            g_.memset(goes_on[:, :].rearrange("p (a b) -> p a b", b=TOPK * GT)[:, :, 0:1], 0.0).then_inc(zeros_ready, 1)
            pool.wait_ge(zeros_ready, 1)
            g_.affine_select(out=tri[:, :], in_=tri[:, :], compare_op=ALU.is_ge, fill=0.0, base=0,
                             pattern=[[1, P]], channel_multiplier=-1).then_inc(consts, 1)
            pool.wait_ge(consts, 2)

            def k_split(ph, seg, key, j0, n_before):
                for m in range(C):
                    emptied(pool, ph, seg, j0 + m)
                    p = [parts[key][:, m, i, :] for i in range(3)]
                    wait(pool, split["k"], n_before + m)
                    link(g_.tensor_tensor(resk[:, :], fk[:, m, :], p[0], ALU.subtract))
                    link(g_.tensor_copy(p[1], resk[:, :]))
                    g_.tensor_tensor(p[2], resk[:, :], p[1], ALU.subtract).then_inc(split["k"], 1)

            def XI(ph, seg, step):
                g_.tensor_copy(xin[:, :, :], xres[:, bass.ds(step * TT, TT), :]).then_inc(xin_ready, 1)

            def XB(ph, seg, step):
                if isinstance(step, int):
                    pool.wait_ge(x_in, 16 * STEPS)
                    pool.wait_ge(w_in, 16 * W_LOADS)
                else:
                    pool.wait_ge(xin_ready, step)
                    pool.wait_ge(x1_ready, step * STEP_B)
                g_.tensor_tensor(xb[:, :, :], xin[:, :, :], bo[:, :].unsqueeze(1).broadcast_to([P, TT, D]), ALU.add)\
                    .then_inc(xb_ready, 1)

            def SK(ph, seg, step):
                if isinstance(step, int):
                    emptied(pool, ph, ("W",), 6, 7)
                    g_.memset(stack["sk"][KR:KR + MR, :, :], 1.0).then_inc(ones_ready, 1)
                    pool.wait_ge(ones_ready, 1)
                else:
                    k_split(ph, seg, "sk", 0, k_splits(step, "s"))

            def CK(ph, seg, step):
                k_split(ph, seg, "ck", 0, k_splits(step, "c"))
                if isinstance(step, int):
                    pool.wait_ge(split["k"], 2 * C)
                    g_.memset(stack["ck"][KR:KR + MR, :, :], 1.0).then_inc(ones_ready, 1)
                    pool.wait_ge(ones_ready, 2)

            def CX(ph, seg, step, layer, b):
                pool.wait_ge(x1_ready, step * STEP_B + b + 1)
                emptied(pool, ph, seg, 0)
                x1_b = x1[:, b * QT:(b + 1) * QT, :]
                g_.tensor_tensor(x1_b, x1_b, beta[:, :].unsqueeze(1).broadcast_to([P, QT, D]), ALU.add).then_inc(x1b_ready, 1)

            def RX(ph, seg, step, layer, b):
                n = step * STEP_B + b
                pool.wait_ge(x2_ready, n + 1)
                g_.tensor_copy(xres[:, bass.ds(n * QT, QT), :], x2[:, :, :]).then_inc(x2_free, 1)

            def G_(ph, seg, step, n):
                pool.wait_ge(routed, n + 1)
                pool.wait_ge(cleared, 32)
                pool.wait_ge(x2_free, (n + 1) * (B // GROUPS) + 1)
                for tile in range(n * GT, (n + 1) * GT):
                    for k in range(TOPK):
                        col = n * (TOPK * GT) + k * GT + tile % GT
                        put_rows(tile, col)

            def put_rows(tile, col):
                pool.indirect_dma_start(out=x_dram, out_offset=bass.IndirectOffsetOnAxis(ap=put[:, col:col + 1], axis=0),
                                        in_=xres[:, tile, :], in_offset=None, bounds_check=E * SLOTS - 1, oob_is_err=False)\
                    .then_inc(put_done, 16)

            walk({"begin": begin, "XI": XI, "XB": XB, "SK": SK, "CK": CK, "CX": CX, "RX": RX, "G": G_}, pool.Fori)

            pool.wait_ge(get_ready, GROUPS)
            for i in range(2):
                pool.wait_ge(y_stored[i], (E // 2) * 48)
            for tile in range(NT):
                for k in range(TOPK):
                    col = (tile // GT) * (TOPK * GT) + k * GT + tile % GT
                    pool.indirect_dma_start(out=got[:, tile * TOPK + k, :], out_offset=None, in_=y_dram,
                                            in_offset=bass.IndirectOffsetOnAxis(ap=get[:, col:col + 1], axis=0))\
                        .then_inc(got_sem[tile // TT], 16)


_INS = ["x", "ctx_1024", "L0_attn_Wqkv", "L0_attn_bqkv", "L0_attn_Wo", "L0_attn_bo", "L0_xattn_Wq", "L0_xattn_bq",
        "L0_xattn_Wk", "L0_xattn_bk", "L0_xattn_Wv", "L0_xattn_bv", "L0_xattn_gamma", "L0_xattn_beta",
        "L0_ffn_w_router", "L0_ffn_wi", "L0_ffn_wo"]


def kernel(**inputs):
    import numpy as np
    import concourse.bacc as bacc
    from concourse.bass_utils import run_bass_kernel_spmd

    nc = bacc.Bacc("TRN2", target_bir_lowering=False, num_devices=1)
    arrays, a = {}, {}
    for name in _INS:
        array = np.ascontiguousarray(inputs[name])
        arrays[f"in_{name}"] = array
        a[name] = nc.dram_tensor(f"in_{name}", array.shape, mybir.dt.from_np(array.dtype), kind="ExternalInput").ap()
    out = nc.dram_tensor("out", [B, T, D], F32, kind="ExternalOutput").ap()
    attention_and_experts(nc, a, out)
    r = run_bass_kernel_spmd(nc, [arrays], core_ids=[0])
    return r.results[0]["out"]
```
